# Optimizing a Trainium2 kernel written in Bass

```python
import numpy as np
import jax
import jax.numpy as jnp

def _softmax(x, axis=-1):
    return jax.nn.softmax(x, axis=axis)

def _gelu(x):
    return jax.nn.gelu(x, approximate=True)

def _silu(x):
    return jax.nn.silu(x)

def _sigmoid(x):
    return jax.nn.sigmoid(x)

def _layernorm(x, axis=-1, eps=1e-05):
    m = jnp.mean(x, axis=axis, keepdims=True)
    v = jnp.var(x, axis=axis, keepdims=True)
    return (x - m) / jnp.sqrt(v + eps)

def _scatter_add(tgt, idx, src, axis=0):
    return tgt.at[idx].add(src)

def _segment_sum(src, seg, n):
    return jax.ops.segment_sum(src, seg, n)
kernel_name = 'mk_gnn_preln_d2_gnn_r8_29ce80'

def setup_inputs(seed: int=0):
    np.random.seed(seed)
    _w = jnp.asarray

    def _rec_inputs():
        import jax
        import jax.numpy as jnp
        _gk = jax.random.key(seed)
        x = -0.0009044 + 1 * jax.random.normal(jax.random.fold_in(_gk, 1), (12500, 32), jnp.float32)
        _s = jax.random.randint(jax.random.fold_in(_gk, 2), (200000,), 0, 12500, jnp.int32)
        _d = jax.random.randint(jax.random.fold_in(_gk, 3), (200000,), 0, 12500, jnp.int32)
        _loop = jnp.arange(12500, dtype=jnp.int32)
        src = jnp.concatenate([_s, _d, _loop])
        dst = jnp.concatenate([_d, _s, _loop])
        _o = jnp.argsort(dst, stable=True)
        src = src[_o]
        dst = dst[_o]
        edge_attr_2 = -5.09086e-05 + 0.577461 * jax.random.normal(jax.random.fold_in(_gk, 12), (412500, 2), jnp.float32)
        edge_type_16 = jax.random.randint(jax.random.fold_in(_gk, 14), (412500,), 0, 16, jnp.int32)
        edge_weight1 = jax.random.uniform(jax.random.fold_in(_gk, 15), (412500, 1), jnp.float32, 0.0, 1)
        return (x, src, dst, edge_attr_2, edge_type_16, edge_weight1)
    x, src, dst, edge_attr_2, edge_type_16, edge_weight1 = _rec_inputs()

    def _L0_gnn_setup():
        import jax, jax.numpy as jnp
        import numpy as np
        N_NODES = 6250
        N_EDGES = 200000
        F_IN = 32
        F_OUT = 32
        BASIS = (4, 4)

        def _tent_basis(u, n):
            centers = jnp.linspace(-1.0, 1.0, n, dtype=u.dtype)
            h = 2.0 / (n - 1)
            return jnp.maximum(0.0, 1.0 - jnp.abs(u[:, None] - centers[None, :]) / h)
        key = jax.random.key(seed)
        k1, k2, k3, k4, k5 = jax.random.split(key, 5)
        x = jax.random.normal(k1, (N_NODES, F_IN), dtype=jnp.float32)
        edge_attr = jax.random.uniform(k2, (N_EDGES, 2), dtype=jnp.float32, minval=-1.0, maxval=1.0)
        weight = jax.random.uniform(k3, (*BASIS, F_IN, F_OUT), dtype=jnp.float32, minval=-0.05, maxval=0.05)
        src = jax.random.randint(k4, (N_EDGES,), 0, N_NODES)
        tgt = jax.random.randint(k5, (N_EDGES,), 0, N_NODES)
        edge_index = jnp.stack([tgt, src], axis=0).astype(jnp.int64)
        return {'x': x, 'edge_attr': edge_attr, 'weight': weight, 'edge_index': edge_index}
    _L0_gnn_all = _L0_gnn_setup()
    _L0_gnn_in = {k: v for k, v in _L0_gnn_all.items() if k in ('weight',)}
    del _L0_gnn_all

    def _L1_gnn_setup():
        import jax, jax.numpy as jnp
        import numpy as np
        N = 12500
        E = 200000
        IN = 32
        OUT = 32
        R = 16
        B = 8
        key = jax.random.key(seed)
        k = jax.random.split(key, 7)
        inputs = jax.random.normal(k[0], (N, IN), jnp.float32)
        weight = jax.random.normal(k[1], (B, IN, OUT), jnp.float32) * (1.414 * (2.0 / (IN + OUT)) ** 0.5)
        w_comp = jax.random.normal(k[2], (R, B), jnp.float32) * (1.414 * (2.0 / (R + B)) ** 0.5)
        norm = jax.random.uniform(k[3], (E, 1), jnp.float32)
        src = jax.random.randint(k[4], (E,), 0, N)
        dst = jax.random.randint(k[5], (E,), 0, N)
        rel_type = jax.random.randint(k[6], (E,), 0, R)
        return {'inputs': inputs, 'weight': weight, 'w_comp': w_comp, 'norm': norm, 'src': src, 'dst': dst, 'rel_type': rel_type}
    _L1_gnn_all = _L1_gnn_setup()
    _L1_gnn_in = {k: v for k, v in _L1_gnn_all.items() if k in ('weight', 'w_comp')}
    del _L1_gnn_all
    return {'x': x, 'src': src, 'dst': dst, 'edge_attr_2': edge_attr_2, 'edge_type_16': edge_type_16, 'edge_weight1': edge_weight1, 'L0_gnn_weight': _L0_gnn_in['weight'], 'L1_gnn_weight': _L1_gnn_in['weight'], 'L1_gnn_w_comp': _L1_gnn_in['w_comp']}

def reference(x, src, dst, edge_attr_2, edge_type_16, edge_weight1, L0_gnn_weight, L1_gnn_weight, L1_gnn_w_comp):
    import jax
    import jax.numpy as jnp

    def _L0_gnn_ref(x, edge_attr, weight, edge_index):
        import jax, jax.numpy as jnp
        import numpy as np
        N_NODES = 6250
        N_EDGES = 200000
        F_IN = 32
        F_OUT = 32
        BASIS = (4, 4)

        def _tent_basis(u, n):
            centers = jnp.linspace(-1.0, 1.0, n, dtype=u.dtype)
            h = 2.0 / (n - 1)
            return jnp.maximum(0.0, 1.0 - jnp.abs(u[:, None] - centers[None, :]) / h)
        k1, k2, f_in, f_out = weight.shape
        n_nodes = x.shape[0]
        bu = _tent_basis(edge_attr[:, 0], k1)
        bv = _tent_basis(edge_attr[:, 1], k2)
        basis = (bu[:, :, None] * bv[:, None, :]).reshape(-1, k1 * k2)
        xj = x[edge_index[1]]
        w2 = weight.reshape(k1 * k2, f_in, f_out)
        msg = basis[:, 0:1] * (xj @ w2[0])
        for k in range(1, k1 * k2):
            msg = msg + basis[:, k:k + 1] * (xj @ w2[k])
        out = jax.ops.segment_sum(msg, edge_index[0], num_segments=n_nodes)
        return out

    def _L1_gnn_ref(inputs, weight, w_comp, norm, src, dst, rel_type):
        import jax, jax.numpy as jnp
        import numpy as np
        N = 12500
        E = 200000
        IN = 32
        OUT = 32
        R = 16
        B = 8
        n, in_feat = inputs.shape
        num_bases, _, out_feat = weight.shape
        w = jnp.matmul(w_comp, weight.reshape(in_feat, num_bases, out_feat))
        w = w.reshape(-1, in_feat, out_feat)
        h_rel = jnp.einsum('ni,rio->nro', inputs, w)
        msg = h_rel[src, rel_type] * norm
        h = jax.ops.segment_sum(msg, dst, num_segments=n)
        return h
    edge_index = jnp.stack([src, dst])
    h = jnp.maximum(_layernorm(x, axis=-1), 0.0)
    x = x + _L0_gnn_ref(h, edge_attr_2, L0_gnn_weight, edge_index)
    h = jnp.maximum(_layernorm(x, axis=-1), 0.0)
    x = x + _L1_gnn_ref(h, L1_gnn_weight, L1_gnn_w_comp, edge_weight1, src, dst, edge_type_16)
    return x

_drawn_inputs = setup_inputs


def setup_inputs(seed=0):
    import zlib

    import numpy as np

    out = dict(_drawn_inputs(seed))
    spreads = {}
    factors = {}
    for name, (base, spread) in spreads.items():
        noise = np.random.default_rng([zlib.crc32(name.encode()), seed]).standard_normal(out[name].shape)
        drawn = base * np.exp(spread * noise) if base else spread * noise
        out[name] = jnp.asarray(drawn.astype(out[name].dtype))
    for name, factor in factors.items():
        out[name] = (out[name] * factor).astype(out[name].dtype)
    return out
```

```python
from contextlib import ExitStack

import numpy as np

import concourse.bass as bass
from concourse import mybir

ALU = mybir.AluOpType
ACT = mybir.ActivationFunctionType
AX = mybir.AxisListType.X
F32 = mybir.dt.float32
I32 = mybir.dt.int32
BF16 = mybir.dt.bfloat16

P = 128
FEAT = 32
NODES = 12500
EDGES = 412500
RELS = 16
BASES = 8
GRID = 4
EPS = 1e-5

TILES = -(-NODES // P)
LAST_ROWS = NODES - (TILES - 1) * P
GROUP = 7
GROUPS = TILES // GROUP
GCOLS = GROUP * FEAT
assert GROUPS * GROUP == TILES and GROUPS % 2 == 0

QUARTERS = 4
PER_PART = 4
BLOCK = P * PER_PART
TILES_PER_BLOCK = QUARTERS * PER_PART
BLOCKS = 2 * -(-EDGES // (2 * QUARTERS * BLOCK))
QEDGES = BLOCKS * BLOCK
PADDED = QUARTERS * QEDGES
assert PADDED >= EDGES

REC = 8
R_DST, R_SRC, R_TYPE, R_ATTR, R_NORM = 0, 1, 2, 3, 5

STAGE_CHUNKS = 18
STAGE_COLS = EDGES // P // STAGE_CHUNKS
STAGED = P * STAGE_CHUNKS * STAGE_COLS
TAIL_COLS = (PADDED - STAGED) // P
TAIL_ROWS, TAIL_REST = divmod(EDGES - STAGED, TAIL_COLS)
assert TAIL_COLS * P + STAGED == PADDED and STAGE_CHUNKS % 2 == 0

SPAN = 625
SPANS = EDGES // SPAN
assert SPAN * SPANS == EDGES

NODE_ROWS = TILES * P
COPIES = 8
COPY_SET = 4
TAB2_NODE = RELS * FEAT
W_COLS = GRID * GRID * FEAT
W_BANKS = 4


def gnn_kernel(nc, x, src, dst, edge_attr, edge_type, edge_weight, w_basis, w_rel, w_comp, out):
    records = nc.dram_tensor("records", [PADDED + 1, REC], I32)
    h_table = nc.dram_tensor("h_table", [NODE_ROWS, FEAT], F32)
    accs = [nc.dram_tensor(f"acc{n}", [NODE_ROWS + P, FEAT], F32) for n in range(COPIES)]
    table2 = nc.dram_tensor("table2", [TILES * P * RELS, FEAT], F32)
    sums = nc.dram_tensor("sums", [PADDED + 1, FEAT], F32)

    with ExitStack() as ctx:
        def sb(name, shape, dt=F32):
            return ctx.enter_context(nc.sbuf_tensor(name, shape, dt))

        def sem(name):
            return ctx.enter_context(nc.semaphore(name))

        x_sb = sb("x_sb", [P, TILES * FEAT])
        ident = sb("ident", [P, P])
        w1_sb = sb("w1_sb", [P, GRID * FEAT])
        spare_row = sb("spare_row", [P, 1])
        lower = sb("lower", [P, P])
        w2_sb = sb("w2_sb", [P, W_COLS])
        node_id = sb("node_id", [P, TILES])
        last_edge = sb("last_edge", [P, TILES], I32)
        local_id = sb("local_id", [QUARTERS - 1, GROUP * P])
        group_base = sb("group_base", [QUARTERS - 1, GROUPS])
        carry_id = sb("carry_id", [QUARTERS - 1, GROUPS])
        eps_sb = sb("eps_sb", [P, 1])

        prepare(nc, x, src, dst, edge_attr, edge_type, edge_weight, w_basis, w_rel, w_comp,
                records, sums, accs, x_sb, ident, w1_sb, w2_sb, node_id, last_edge, local_id,
                group_base, eps_sb, spare_row, lower, h_table)
        scatter_loop(nc, records, h_table, accs, ident, w1_sb, spare_row, lower)
        update_nodes(nc, accs, table2, x_sb, ident, w2_sb, eps_sb)
        edge_loop(nc, records, table2, sums, ident)
        node_loop(nc, records, sums, x_sb, last_edge, local_id, group_base, carry_id, out)


def ln_buffers(sb):
    return dict(total=sb("ln_total", [P, GROUP]), cent=sb("ln_cent", [P, GROUP, FEAT]),
                square=sb("ln_square", [P, GROUP, FEAT]), var=sb("ln_var", [P, 2, GROUP]),
                std=sb("ln_std", [P, 2, GROUP]), rstd=sb("ln_rstd", [P, GROUP]),
                h=sb("ln_h", [P, 2, GCOLS]))


LN_STEPS = 5


def ln_group(nc, dve, ln, xg, j, h, ln_step, var_ready, std_ready, h_ready):
    b = j * LN_STEPS
    dve.sem_inc(ln_step, 1)
    xg3 = xg.rearrange("p (t f) -> p t f", f=FEAT)
    nc.vector.tensor_reduce(ln["total"][:], xg3, AX, ALU.add).then_inc(ln_step, 1)
    dve.wait_ge(ln_step, b + 2)
    nc.vector.scalar_tensor_tensor(
        out=ln["cent"][:], in0=ln["total"][:].unsqueeze(2).to_broadcast([P, GROUP, FEAT]),
        scalar=-1.0 / FEAT, in1=xg3, op0=ALU.mult, op1=ALU.add).then_inc(ln_step, 1)
    dve.wait_ge(ln_step, b + 3)
    nc.vector.tensor_tensor(ln["square"][:], ln["cent"][:], ln["cent"][:], ALU.mult).then_inc(ln_step, 1)
    dve.wait_ge(ln_step, b + 4)
    nc.vector.tensor_reduce(ln["var"][:, h, :], ln["square"][:], AX, ALU.add).then_inc(var_ready, 1)
    dve.wait_ge(std_ready, j + 1)
    nc.vector.reciprocal(ln["rstd"][:], ln["std"][:, h, :]).then_inc(ln_step, 1)
    dve.wait_ge(ln_step, b + 5)
    nc.vector.scalar_tensor_tensor(
        out=ln["h"][:, h, :].rearrange("p (t f) -> p t f", f=FEAT), in0=ln["cent"][:], scalar=0.0,
        in1=ln["rstd"][:].unsqueeze(2).to_broadcast([P, GROUP, FEAT]),
        op0=ALU.max, op1=ALU.mult).then_inc(h_ready, 1)
    dve.wait_ge(h_ready, j + 1)


def turn_and_multiply(nc, pe, ln, ps_t, ps_w, ht, w_sb, ident, j, h, first,
                      h_ready, turned, ht_ready, product, evacuated):
    pe.wait_ge(h_ready, j + 1)
    if not first:
        pe.wait_ge(ht_ready, j - 1)
    nc.tensor.transpose(ps_t[h][:, 0:P], ln["h"][:, h, 0:P], ident[:])
    nc.tensor.transpose(ps_t[h][0:GCOLS - P, P:2 * P], ln["h"][:, h, P:GCOLS], ident[:]).then_inc(turned, 1)
    pe.wait_ge(ht_ready, j + 1)
    for k in range(GROUP):
        if not first or j * GROUP + k >= W_BANKS:
            pe.wait_ge(evacuated, j * GROUP + k - (W_BANKS - 2))
        rows = slice(FEAT * (k % 4), FEAT * (k % 4) + FEAT)
        nc.tensor.matmul(ps_w[k % W_BANKS][:], ht[rows, h, k // 4, :], w_sb[rows, :],
                         start=True, stop=True).then_inc(product, 1)


def root(nc, act, ln, eps_sb, j, h, var_ready, std_ready):
    act.wait_ge(var_ready, j + 1)
    nc.scalar.activation(ln["std"][:, h, :], ln["var"][:, h, :], ACT.Sqrt, bias=eps_sb[:],
                         scale=1.0 / FEAT).then_inc(std_ready, 1)


def table_rows(nc, act, ln, ps_t, ps_w, ht, rows_sb, eps_sb, table, j, h, first, more,
               var_ready, std_ready, turned, ht_ready, product, evacuated, stored):
    act.wait_ge(turned, j + 1)
    if not first:
        act.wait_ge(product, (j - 1) * GROUP)
    nc.scalar.copy(ht[:, h, 0, :], ps_t[h][:, 0:P])
    nc.scalar.copy(ht[0:GCOLS - P, h, 1, :], ps_t[h][0:GCOLS - P, P:2 * P]).then_inc(ht_ready, 1)
    if more:
        root(nc, act, ln, eps_sb, j + 1, 1 - h, var_ready, std_ready)
    words = TAB2_NODE
    for k in range(GROUP):
        n = j * GROUP + k
        act.wait_ge(product, n + 1)
        if not first or j > 0:
            act.wait_ge(stored[k], 16 * j)
        last = nc.scalar.copy(rows_sb[:, k, :], ps_w[k % W_BANKS][:])
        last.then_inc(evacuated, 1)
        act.wait_ge(evacuated, n + 1)
        act.dma_start(
            bass.AP(table, n * P * words, [[words, P], [1, words]]),
            rows_sb[:, k, 0:words]).then_inc(stored[k], 16)


def prepare(nc, x, src, dst, edge_attr, edge_type, edge_weight, w_basis, w_rel, w_comp,
            records, sums, accs, x_sb, ident, w1_sb, w2_sb, node_id, last_edge, local_id,
            group_base, eps_sb, spare_row, lower, h_table):
    with ExitStack() as ctx:
        def sb(name, shape, dt=F32):
            return ctx.enter_context(nc.sbuf_tensor(name, shape, dt))

        def ps(name, shape=(P, 512)):
            return ctx.enter_context(nc.psum_tensor(name, list(shape), F32))

        def sem(name):
            return ctx.enter_context(nc.semaphore(name))

        ln = ln_buffers(sb)
        zero_rows = sb("zero_rows", [P, (NODE_ROWS + P) // P * FEAT])
        spare_int = sb("spare_int", [P, 1], I32)
        raw_dst = sb("raw_dst", [P, 2, STAGE_COLS], I32)
        raw_src = sb("raw_src", [P, 2, STAGE_COLS], I32)
        raw_type = sb("raw_type", [P, 2, STAGE_COLS], I32)
        raw_attr = sb("raw_attr", [P, 2, 2 * STAGE_COLS])
        raw_norm = sb("raw_norm", [P, 2, STAGE_COLS])
        rec = sb("rec", [P, 2, STAGE_COLS, REC], I32)
        t_dst = sb("t_dst", [P, TAIL_COLS], I32)
        t_src = sb("t_src", [P, TAIL_COLS], I32)
        t_type = sb("t_type", [P, TAIL_COLS], I32)
        t_attr = sb("t_attr", [P, 2 * TAIL_COLS])
        t_norm = sb("t_norm", [P, TAIL_COLS])
        t_rec = sb("t_rec", [P, TAIL_COLS, REC], I32)
        lead = sb("lead", [1, REC], I32)
        zeros = sb("zeros", [1, FEAT])
        span_first = sb("span_first", [1, SPANS])
        span_int = sb("span_int", [1, SPANS], I32)
        ones_row = sb("ones_row", [1, P])
        span_all = sb("span_all", [P, SPANS])
        id_int = sb("id_int", [P, TILES], I32)
        local_int = sb("local_int", [QUARTERS - 1, GROUP * P], I32)
        base_int = sb("base_int", [QUARTERS - 1, GROUPS], I32)
        ids = sb("ids", [P, 2, GROUP])
        hits = sb("hits", [P, SPANS])
        span_no = sb("span_no", [P, 2, GROUP])
        span_base = sb("span_base", [P, 2, GROUP])
        span_idx = sb("span_idx", [P, 2, GROUP], I32)
        span_dst = sb("span_dst", [P, 2, GROUP, SPAN], I32)
        inside = sb("inside", [P, 2, GROUP])
        upto = sb("upto", [P, 1 + TILES])
        shift = sb("shift", [P, P])
        wrap = sb("wrap", [P, P])
        has = sb("has", [P, TILES])
        row = sb("row", [P, TILES])
        wr_sb = sb("wr_sb", [BASES, 2 * RELS, FEAT])
        wct = sb("wct", [BASES, RELS])
        wct_pad = sb("wct_pad", [BASES, 2, P])

        ps_t = [ps(f"ps_t{i}") for i in range(2)]
        ps_a, ps_b = ps("ps_a"), ps("ps_b")

        x_pad, x_in, w_in, span_in = sem("x_pad"), sem("x_in"), sem("w_in"), sem("span_in")
        raw_in = [sem(f"raw_in{i}") for i in range(2)]
        rec_out = [sem(f"rec_out{i}") for i in range(2)]
        rec_zero, rec_made = sem("rec_zero"), sem("rec_made")
        tail_zero, tail_in, tail_made, tail_out = sem("tail_zero"), sem("tail_in"), sem("tail_made"), sem("tail_out")
        const_step, ident_ready = sem("const_step"), sem("ident_ready")
        ln_step, var_ready, std_ready, h_ready = sem("ln_step"), sem("var_ready"), sem("std_ready"), sem("h_ready")
        h_stored = [sem(f"h_stored{h}") for h in range(2)]
        zero_ready, acc_zeroed = sem("zero_ready"), sem("acc_zeroed")
        spans_bcast, wrel_ready, setup, search = sem("spans_bcast"), sem("wrel_ready"), sem("setup"), sem("search")
        idx_ready, span_used = sem("idx_ready"), sem("span_used")
        span_got = [sem(f"span_got{i}") for i in range(2)]
        before_ready = sem("before_ready")
        pool_waited = sem("pool_waited")
        inside_step = sem("inside_step")
        counted = sem("counted")

        raw = [(raw_dst, dst, 1), (raw_src, src, 1), (raw_type, edge_type, 1),
               (raw_attr, edge_attr, 2), (raw_norm, edge_weight, 1)]
        tail = [(t_dst, dst, 1), (t_src, src, 1), (t_type, edge_type, 1), (t_attr, edge_attr, 2),
                (t_norm, edge_weight, 1)]

        with nc.Block() as block:

            @block.sync
            def _(sp):
                whole = (TILES - 1) * P
                sp.wait_ge(x_pad, 1)
                sp.dma_start(x_sb[:, 0:(TILES - 1) * FEAT].rearrange("p (t f) -> p t f", f=FEAT),
                             x[0:whole, :].rearrange("(t p) f -> p t f", p=P)).then_inc(x_in, 16)
                sp.dma_start(x_sb[0:LAST_ROWS, (TILES - 1) * FEAT:], x[whole:NODES, :]).then_inc(x_in, 16)
                for v in range(GRID):
                    sp.dma_start(w1_sb[FEAT * v:FEAT * v + FEAT, :].rearrange("i (u o) -> i u o", o=FEAT),
                                 w_basis[:, v, :, :].rearrange("u i o -> i u o")).then_inc(w_in, 16)
                sp.dma_start(wr_sb[:], bass.AP(w_rel.tensor, 0, [[FEAT, BASES], [BASES * FEAT, 2 * RELS], [1, FEAT]])
                             ).then_inc(w_in, 16)
                with nc.allow_non_contiguous_dma("128 words"):
                    sp.dma_start(wct[:], w_comp.rearrange("r b -> b r")).then_inc(w_in, 16)
                with nc.allow_non_contiguous_dma("the first destination of each span"):
                    sp.dma_start(span_int[:], bass.AP(dst.tensor, 0, [[SPAN * SPANS, 1], [SPAN, SPANS]])
                                 ).then_inc(span_in, 16)

                def load(c, h):
                    for tile, array, width in raw:
                        n = width * STAGE_COLS
                        sp.dma_start(tile[:, h, :], bass.AP(array.tensor, c * n, [[n * STAGE_CHUNKS, P], [1, n]])
                                     ).then_inc(raw_in[h], 16)

                def store(c, h):
                    sp.wait_ge(rec_made, c + 1)
                    n = REC * STAGE_COLS
                    sp.dma_start(bass.AP(records, REC + c * n, [[n * STAGE_CHUNKS, P], [1, n]]),
                                 rec[:, h, :, :].rearrange("p e r -> p (e r)")).then_inc(rec_out[h], 16)

                load(0, 0)
                load(1, 1)
                with sp.Fori(0, STAGE_CHUNKS // 2 - 1) as i:
                    for h in range(2):
                        store(2 * i + h, h)
                        load(2 * i + h + 2, h)
                for h in range(2):
                    store(STAGE_CHUNKS - 2 + h, h)

                sp.wait_ge(tail_zero, 5)
                for tile, array, width in tail:
                    n = width * TAIL_COLS
                    sp.dma_start(tile[0:TAIL_ROWS, :], bass.AP(array.tensor, width * STAGED, [[n, TAIL_ROWS], [1, n]])
                                 ).then_inc(tail_in, 16)
                    sp.dma_start(tile[TAIL_ROWS:TAIL_ROWS + 1, 0:width * TAIL_REST],
                                 bass.AP(array.tensor, width * STAGED + TAIL_ROWS * n, [[n, 1], [1, width * TAIL_REST]])
                                 ).then_inc(tail_in, 16)
                sp.wait_ge(tail_made, 8)
                sp.dma_start(bass.AP(records, REC * (STAGED + 1), [[REC * TAIL_COLS, P], [1, REC * TAIL_COLS]]),
                             t_rec[:, :, :].rearrange("p e r -> p (e r)")).then_inc(tail_out, 16)
                sp.dma_start(bass.AP(records, 0, [[REC, 1], [1, REC]]), lead[:]).then_inc(tail_out, 16)
                sp.dma_start(bass.AP(sums, PADDED * FEAT, [[FEAT, 1], [1, FEAT]]), zeros[:]).then_inc(tail_out, 16)
                sp.wait_ge(tail_out, 48)
                for h in range(2):
                    sp.wait_ge(rec_out[h], 16 * (STAGE_CHUNKS // 2))

            @block.gpsimd
            def _(pool):
                nc.gpsimd.memset(ident[:], 0.0).then_inc(const_step, 1)
                nc.gpsimd.memset(shift[:], 0.0).then_inc(const_step, 1)
                nc.gpsimd.memset(wrap[:], 0.0).then_inc(const_step, 1)
                nc.gpsimd.memset(lower[:], 1.0).then_inc(const_step, 1)
                pool.wait_ge(const_step, 4)
                nc.gpsimd.affine_select(out=ident[:], in_=ident[:], compare_op=ALU.not_equal, fill=1.0,
                                        base=0, pattern=[[-1, P]], channel_multiplier=1)
                nc.gpsimd.affine_select(out=shift[:], in_=shift[:], compare_op=ALU.not_equal, fill=1.0,
                                        base=1, pattern=[[-1, P]], channel_multiplier=1)
                nc.gpsimd.affine_select(out=wrap[:], in_=wrap[:], compare_op=ALU.not_equal, fill=1.0,
                                        base=1 - P, pattern=[[-1, P]], channel_multiplier=1)
                nc.gpsimd.iota(id_int[:], pattern=[[P, TILES]], base=0, channel_multiplier=1)
                nc.gpsimd.iota(local_int[:], pattern=[[1, GROUP * P]], base=0, channel_multiplier=0)
                nc.gpsimd.iota(spare_int[:], pattern=[[0, 1]], base=NODE_ROWS, channel_multiplier=1)
                nc.gpsimd.affine_select(out=lower[:], in_=lower[:], compare_op=ALU.is_gt, fill=0.0,
                                        base=0, pattern=[[-1, P]], channel_multiplier=1)
                nc.gpsimd.iota(base_int[:], pattern=[[-GROUP * P, GROUPS]], base=0,
                               channel_multiplier=0).then_inc(ident_ready, 1)
                nc.gpsimd.memset(rec[:].rearrange("p a e r -> p (a e r)"), 0).then_inc(rec_zero, 1)
                pool.wait_ge(rec_zero, 1)

                def make(i, h, first):
                    c = 2 * i + h
                    pool.wait_ge(raw_in[h], 80 * i + 80)
                    if not first:
                        pool.wait_ge(rec_out[h], 16 * i)
                    pool.sem_inc(pool_waited, 1)
                    r = rec[:, h, :, :]
                    rf = r.bitcast(F32)
                    nc.gpsimd.tensor_copy(r[:, :, R_DST], raw_dst[:, h, :])
                    nc.gpsimd.tensor_copy(r[:, :, R_SRC], raw_src[:, h, :])
                    nc.gpsimd.tensor_copy(r[:, :, R_TYPE], raw_type[:, h, :])
                    nc.gpsimd.tensor_copy(rf[:, :, R_ATTR:R_ATTR + 2],
                                          raw_attr[:, h, :].rearrange("p (e a) -> p e a", a=2))
                    nc.gpsimd.tensor_copy(rf[:, :, R_NORM], raw_norm[:, h, :]).then_inc(rec_made, 1)

                make(0, 0, True)
                make(0, 1, True)
                with pool.Fori(1, STAGE_CHUNKS // 2) as i:
                    for h in range(2):
                        make(i, h, False)

                nc.gpsimd.memset(t_dst[:], NODES).then_inc(tail_zero, 1)
                for tile in (t_src, t_type, t_attr, t_norm):
                    nc.gpsimd.memset(tile[:], 0).then_inc(tail_zero, 1)
                nc.gpsimd.memset(t_rec[:].rearrange("p e r -> p (e r)"), 0).then_inc(tail_made, 1)
                nc.gpsimd.memset(lead[:], -1).then_inc(tail_made, 1)
                nc.gpsimd.memset(zeros[:], 0.0).then_inc(tail_made, 1)
                pool.wait_ge(tail_made, 3)
                pool.wait_ge(tail_in, 160)
                nc.gpsimd.tensor_copy(t_rec[:, :, R_DST], t_dst[:]).then_inc(tail_made, 1)
                nc.gpsimd.tensor_copy(t_rec[:, :, R_SRC], t_src[:]).then_inc(tail_made, 1)
                nc.gpsimd.tensor_copy(t_rec[:, :, R_TYPE], t_type[:]).then_inc(tail_made, 1)
                nc.gpsimd.tensor_copy(t_rec[:].bitcast(F32)[:, :, R_ATTR:R_ATTR + 2],
                                      t_attr[:].rearrange("p (e a) -> p e a", a=2)).then_inc(tail_made, 1)
                nc.gpsimd.tensor_copy(t_rec[:].bitcast(F32)[:, :, R_NORM], t_norm[:]).then_inc(tail_made, 1)

                spans = dst.rearrange("(s e) -> s e", e=SPAN)

                def fetch(i, h, first):
                    pool.wait_ge(idx_ready, 2 * i + h + 1)
                    if not first:
                        pool.wait_ge(span_used, 2 * i + h - 1)
                    pool.sem_inc(pool_waited, 1)
                    for k in range(GROUP):
                        pool.indirect_dma_start(
                            out=span_dst[:, h, k, :], out_offset=None, in_=spans,
                            in_offset=bass.IndirectOffsetOnAxis(ap=span_idx[:, h, k:k + 1], axis=0)
                        ).then_inc(span_got[h], 16)

                fetch(0, 0, True)
                fetch(0, 1, True)
                with pool.Fori(1, GROUPS // 2) as i:
                    for h in range(2):
                        fetch(i, h, False)

            @block.vector
            def _(dve):
                nc.vector.memset(x_sb[:, (TILES - 1) * FEAT:], 0.0).then_inc(x_pad, 1)
                nc.vector.memset(eps_sb[:], EPS).then_inc(setup, 1)
                nc.vector.memset(ones_row[:], 1.0).then_inc(setup, 1)
                nc.vector.memset(upto[:, 0:1], 0.0).then_inc(setup, 1)
                nc.vector.memset(wct_pad[:].rearrange("b a c -> b (a c)"), 0.0).then_inc(setup, 1)
                nc.vector.memset(zero_rows[:], 0.0).then_inc(zero_ready, 1)
                dve.wait_ge(setup, 4)
                dve.wait_ge(ident_ready, 1)
                nc.vector.tensor_copy(node_id[:], id_int[:]).then_inc(setup, 1)
                nc.vector.tensor_copy(local_id[:], local_int[:]).then_inc(setup, 1)
                nc.vector.tensor_copy(spare_row[:], spare_int[:])
                nc.vector.tensor_copy(group_base[:], base_int[:]).then_inc(setup, 1)
                dve.wait_ge(w_in, 96)
                for par in range(2):
                    last = nc.vector.tensor_copy(
                        wct_pad[:, par, :].rearrange("b (g q r) -> b g q r", g=4, q=2)[:, :, par, :],
                        wct[:].unsqueeze(1).to_broadcast([BASES, 4, RELS]))
                last.then_inc(setup, 1)
                dve.wait_ge(span_in, 16)
                nc.vector.tensor_copy(span_first[:], span_int[:]).then_inc(setup, 1)
                dve.wait_ge(x_in, 32)

                def normalise(j, h, first):
                    if not first:
                        dve.wait_ge(h_stored[h], 16 * (j - h) // 2)
                    ln_group(nc, dve, ln, x_sb[:, bass.ds(j * GCOLS, GCOLS)], j, h, ln_step,
                             var_ready, std_ready, h_ready)

                dve.wait_ge(wrel_ready, 1)
                nc.vector.tensor_copy(w2_sb[:], ps_a[:]).then_inc(setup, 1)
                dve.wait_ge(spans_bcast, 1)
                nc.vector.tensor_copy(span_all[:, 0:512], ps_b[:]).then_inc(setup, 1)
                nc.vector.tensor_copy(span_all[:, 512:SPANS], ps_t[1][:, 0:SPANS - 512]).then_inc(setup, 1)
                dve.wait_ge(setup, 12)
                normalise(0, 0, True)
                normalise(1, 1, True)

                steps = GROUP + 3

                def find_span(i, h, first):
                    j = 2 * i + h
                    nc.vector.tensor_copy(ids[:, h, :], node_id[:, bass.ds(j * GROUP, GROUP)]).then_inc(search, 1)
                    dve.wait_ge(search, j * steps + 1)
                    for k in range(GROUP):
                        nc.vector.tensor_scalar(hits[:], span_all[:], ids[:, h, k:k + 1], 0.0, ALU.is_le, ALU.add,
                                                accum_out=span_no[:, h, k:k + 1]).then_inc(search, 1)
                        dve.wait_ge(search, j * steps + k + 2)
                    nc.vector.tensor_scalar(span_no[:, h, :], span_no[:, h, :], -1.0, 0.0, ALU.add, ALU.max
                                            ).then_inc(search, 1)
                    dve.wait_ge(search, j * steps + GROUP + 2)
                    nc.vector.tensor_scalar(span_base[:, h, :], span_no[:, h, :], float(SPAN), None, ALU.mult
                                            ).then_inc(search, 1)
                    nc.vector.tensor_copy(span_idx[:, h, :], span_no[:, h, :]).then_inc(idx_ready, 1)

                def count_inside(i, h):
                    j = 2 * i + h
                    dve.wait_ge(span_got[h], 16 * GROUP * (i + 1))
                    for k in range(GROUP):
                        last = nc.vector.tensor_scalar(
                            hits[:, 0:SPAN], span_dst[:, h, k, :], ids[:, h, k:k + 1], 0.0, ALU.is_le, ALU.add,
                            accum_out=inside[:, h, k:k + 1])
                        if k < GROUP - 1:
                            last.then_inc(inside_step, 1)
                            dve.wait_ge(inside_step, j * (GROUP - 1) + k + 1)
                    last.then_inc(span_used, 1)
                    dve.wait_ge(span_used, j + 1)
                    nc.vector.tensor_tensor(upto[:, bass.ds(1 + j * GROUP, GROUP)], inside[:, h, :],
                                            span_base[:, h, :], ALU.add).then_inc(counted, 1)

                find_span(0, 0, True)
                find_span(0, 1, True)
                with dve.Fori(1, GROUPS // 2) as i:
                    for h in range(2):
                        normalise(2 * i + h, h, False)
                        count_inside(i - 1, h)
                        dve.wait_ge(counted, 2 * i + h - 1)
                        find_span(i, h, False)
                for h in range(2):
                    count_inside(GROUPS // 2 - 1, h)
                dve.wait_ge(counted, GROUPS)
                dve.wait_ge(before_ready, 1)
                nc.vector.tensor_tensor(has[:], upto[:, 1:], ps_b[:, 0:TILES], ALU.is_gt).then_inc(counted, 1)
                dve.wait_ge(counted, GROUPS + 1)
                nc.vector.scalar_tensor_tensor(out=row[:], in0=upto[:, 1:], scalar=-float(PADDED + 1), in1=has[:],
                                               op0=ALU.add, op1=ALU.mult).then_inc(counted, 1)
                dve.wait_ge(counted, GROUPS + 2)
                nc.vector.tensor_scalar(last_edge[:], row[:], float(PADDED), None, ALU.add).then_inc(counted, 1)

            @block.scalar
            def _(act):
                act.wait_ge(zero_ready, 1)
                for acc in accs:
                    act.dma_start(bass.AP(acc, 0, [[(NODE_ROWS + P) // P * FEAT, P], [1, (NODE_ROWS + P) // P * FEAT]]),
                                  zero_rows[:]).then_inc(acc_zeroed, 16)
                act.wait_ge(setup, 1)

                def store_h(j, h):
                    act.wait_ge(h_ready, j + 1)
                    act.dma_start(bass.AP(h_table, j * (GROUP * P * FEAT), [[FEAT, P], [P * FEAT, GROUP], [1, FEAT]]),
                                  ln["h"][:, h, :].rearrange("p (t f) -> p t f", f=FEAT)).then_inc(h_stored[h], 16)

                with act.Fori(0, GROUPS // 2) as i:
                    for h in range(2):
                        root(nc, act, ln, eps_sb, 2 * i + h, h, var_ready, std_ready)
                        store_h(2 * i + h, h)
                for h in range(2):
                    act.wait_ge(h_stored[h], 16 * (GROUPS // 2))
                act.wait_ge(acc_zeroed, 16 * COPIES)

            @block.tensor
            def _(pe):
                pe.wait_ge(ident_ready, 1)
                pe.wait_ge(setup, 9)
                pe.wait_ge(w_in, 96)
                wr = wr_sb[:].rearrange("b (r q) o -> b q r o", q=2)
                nc.tensor.matmul(ps_a[:], wct_pad[:, 0, :], wr[:, 0, :, :], start=True, stop=False)
                nc.tensor.matmul(ps_a[:], wct_pad[:, 1, :], wr[:, 1, :, :], start=False, stop=True
                                 ).then_inc(wrel_ready, 1)
                nc.tensor.matmul(ps_b[:], ones_row[:], span_first[:, 0:512], start=True, stop=True)
                nc.tensor.matmul(ps_t[1][:, 0:SPANS - 512], ones_row[:], span_first[:, 512:SPANS],
                                 start=True, stop=True).then_inc(spans_bcast, 1)
                pe.wait_ge(setup, 12)
                pe.wait_ge(counted, GROUPS)
                nc.tensor.matmul(ps_b[:, 0:TILES], shift[:], upto[:, 1:], start=True, stop=False)
                nc.tensor.matmul(ps_b[:, 0:TILES], wrap[:], upto[:, 0:TILES], start=False, stop=True
                                 ).then_inc(before_ready, 1)


def group_first(group):
    group(0, 0, True)
    group(1, 1, True)


def scatter_loop(nc, records, h_table, accs, ident, w1_sb, spare_row, lower):
    groups = TILES_PER_BLOCK // COPY_SET
    with ExitStack() as ctx:
        def sb(name, shape, dt=F32):
            return ctx.enter_context(nc.sbuf_tensor(f"{name}_s", shape, dt))

        def ps(name):
            return ctx.enter_context(nc.psum_tensor(f"{name}_s", [P, BLOCK], F32))

        def sem(name):
            return ctx.enter_context(nc.semaphore(f"{name}_s"))

        rec = sb("rec", [P, 2, QUARTERS, PER_PART, REC], I32)
        idx = sb("idx", [P, 2, TILES_PER_BLOCK], I32)
        source = sb("source", [P, 2, TILES_PER_BLOCK])
        scaled = sb("scaled", [P, TILES_PER_BLOCK, 2])
        centre_int = sb("centre_int", [P, GRID], I32)
        centre = sb("centre", [P, GRID])
        rising = sb("rising", [P, 2 * TILES_PER_BLOCK, GRID])
        falling = sb("falling", [P, 2 * TILES_PER_BLOCK, GRID])
        tent = sb("tent", [P, 2, 2 * TILES_PER_BLOCK, GRID])
        got = sb("got", [P, 2, TILES_PER_BLOCK, FEAT])
        spread = sb("spread", [P, 2, TILES_PER_BLOCK, GRID * FEAT])
        spread_t = sb("spread_t", [P, 2, COPY_SET, P])
        scaled_w = sb("scaled_w", [P, 2, COPY_SET, GRID * FEAT])
        same = sb("same", [P, 2, COPY_SET, P])
        earlier = sb("earlier", [P, COPY_SET, P])
        n_earlier = sb("n_earlier", [P, TILES_PER_BLOCK])
        to_spare = sb("to_spare", [P, TILES_PER_BLOCK])
        target = sb("target", [P, 2, TILES_PER_BLOCK], I32)
        summed = sb("summed", [P, 2, TILES_PER_BLOCK, FEAT])

        ps_src = [ps(f"ps_src{s}") for s in range(2)]
        ps_t = [ps(f"ps_t{s}") for s in range(2)]
        ps_z = [ps(f"ps_z{s}") for s in range(2)]
        ps_sum = [ps(f"ps_sum{h}") for h in range(2)]

        rec_in = [sem(f"rec_in{h}") for h in range(2)]
        gathered = [sem(f"gathered{h}") for h in range(2)]
        added = [sem(f"added{s}") for s in range(2)]
        setup, prep_step, prepared, spread_ready = sem("setup"), sem("prep_step"), sem("prepared"), sem("spread_ready")
        src_ready, same_ready, turned, turned_copied = sem("src_ready"), sem("same_ready"), sem("turned"), sem("turned_copied")
        product, scaled_ready, set_summed, summed_ready = sem("product"), sem("scaled_ready"), sem("set_summed"), sem("summed_ready")
        target_step, target_ready, pool_waited = sem("target_step"), sem("target_ready"), sem("pool_waited")
        PREP, TARGET = 5, 3

        with nc.Block() as block:

            @block.sync
            def _(sp):
                def load(t, h):
                    sp.dma_start(
                        rec[:, h, :, :, :].rearrange("p q e r -> p q (e r)"),
                        bass.AP(records, t * (BLOCK * REC) + REC,
                                [[PER_PART * REC, P], [QEDGES * REC, QUARTERS], [1, PER_PART * REC]])
                    ).then_inc(rec_in[h], 16)

                load(0, 0)
                load(1, 1)
                with sp.Fori(0, BLOCKS // 2 - 1) as i:
                    for h in range(2):
                        sp.wait_ge(prepared, 2 * i + h + 1)
                        load(2 * i + h + 2, h)

            @block.gpsimd
            def _(pool):
                nc.gpsimd.iota(centre_int[:], pattern=[[1, GRID]], base=0, channel_multiplier=0).then_inc(setup, 1)

                def fetch(i, h, first):
                    t = 2 * i + h
                    pool.wait_ge(prepared, t + 1)
                    if not first:
                        pool.wait_ge(spread_ready, t - 1)
                    pool.sem_inc(pool_waited, 1)
                    for k in range(TILES_PER_BLOCK):
                        pool.indirect_dma_start(
                            out=got[:, h, k, :], out_offset=None, in_=h_table.ap(),
                            in_offset=bass.IndirectOffsetOnAxis(ap=idx[:, h, k:k + 1], axis=0)
                        ).then_inc(gathered[h], 16)

                def scatter(i, h, first):
                    t = 2 * i + h
                    pool.wait_ge(target_ready, t + 1)
                    pool.wait_ge(summed_ready, t + 1)
                    for g in range(groups):
                        if not (first and h == 0 and g < 2):
                            pool.wait_ge(added[g % 2], 16 * COPY_SET * (t * (groups // 2) + g // 2))
                        pool.sem_inc(pool_waited, 1)
                        for n in range(COPY_SET):
                            k = g * COPY_SET + n
                            pool.indirect_dma_start(
                                out=accs[(g % 2) * COPY_SET + n].ap(),
                                out_offset=bass.IndirectOffsetOnAxis(ap=target[:, h, k:k + 1], axis=0),
                                in_=summed[:, h, k, :], in_offset=None, compute_op=ALU.add
                            ).then_inc(added[g % 2], 16)

                fetch(0, 0, True)
                fetch(0, 1, True)
                scatter(0, 0, True)
                fetch(1, 0, False)
                scatter(0, 1, True)
                fetch(1, 1, False)
                with pool.Fori(1, BLOCKS // 2 - 1) as i:
                    for h in range(2):
                        scatter(i, h, False)
                        fetch(i + 1, h, False)
                for h in range(2):
                    scatter(BLOCKS // 2 - 1, h, False)
                for s in range(2):
                    pool.wait_ge(added[s], 16 * COPY_SET * BLOCKS * (groups // 2))

            @block.vector
            def _(dve):
                dve.wait_ge(setup, 1)
                nc.vector.tensor_copy(centre[:], centre_int[:]).then_inc(setup, 1)
                dve.wait_ge(setup, 2)

                def prepare_block(i, h, first):
                    t = 2 * i + h
                    b = t * PREP
                    dve.wait_ge(rec_in[h], 16 * i + 16)
                    r = rec[:, h, :, :, :].rearrange("p q e r -> p e q r")
                    attr = r[:, :, :, R_ATTR:R_ATTR + 2].bitcast(F32)
                    wide = [P, 2 * TILES_PER_BLOCK, GRID]

                    def quad(ap):
                        return ap.rearrange("p (e q) -> p e q", q=QUARTERS)

                    nc.vector.tensor_scalar(scaled[:].rearrange("p (e q) a -> p e q a", q=QUARTERS), attr,
                                            (GRID - 1) / 2, (GRID - 1) / 2, ALU.mult, ALU.add).then_inc(prep_step, 1)
                    nc.vector.tensor_copy(quad(idx[:, h, :]), r[:, :, :, R_DST])
                    dve.wait_ge(prep_step, b + 1)
                    nc.vector.tensor_tensor(rising[:], scaled[:].rearrange("p k a -> p (k a)").unsqueeze(2).to_broadcast(wide),
                                            centre[:].unsqueeze(1).to_broadcast(wide), ALU.subtract).then_inc(prep_step, 1)
                    if not first:
                        dve.wait_ge(src_ready, groups * (t - 1))
                    nc.vector.tensor_copy(quad(source[:, h, :]), r[:, :, :, R_SRC])
                    dve.wait_ge(prep_step, b + 2)
                    nc.vector.tensor_scalar(falling[:], rising[:], -1.0, 1.0, ALU.mult, ALU.add).then_inc(prep_step, 1)
                    dve.wait_ge(prep_step, b + 3)
                    nc.vector.scalar_tensor_tensor(out=rising[:], in0=rising[:], scalar=1.0, in1=falling[:],
                                                   op0=ALU.add, op1=ALU.min).then_inc(prep_step, 1)
                    dve.wait_ge(prep_step, b + 4)
                    nc.vector.tensor_scalar(tent[:, h, :, :], rising[:], 0.0, None, ALU.max).then_inc(prep_step, 1)
                    dve.wait_ge(prep_step, b + 5)
                    dve.sem_inc(prepared, 1)

                def tent_of(h, a):
                    return tent[:, h, :, :].rearrange("p (k a) c -> p k a c", a=2)[:, :, a, :]

                def block_work(i, h, first):
                    t = 2 * i + h
                    dve.wait_ge(gathered[h], 16 * TILES_PER_BLOCK * (i + 1))
                    if not first:
                        dve.wait_ge(turned, groups * (t - 1))
                    wide = [P, TILES_PER_BLOCK, GRID, FEAT]
                    nc.vector.tensor_tensor(
                        spread[:, h, :, :].rearrange("p k (v f) -> p k v f", f=FEAT),
                        got[:, h, :, :].unsqueeze(2).to_broadcast(wide),
                        tent_of(h, 1).unsqueeze(3).to_broadcast(wide), ALU.mult).then_inc(spread_ready, 1)

                    def compare(g):
                        s, n = g % 2, groups * t + g
                        dve.wait_ge(src_ready, n + 1)
                        if not (first and h == 0 and g < 2):
                            dve.wait_ge(set_summed, n - 1)
                        mine = source[:, h, g * COPY_SET:(g + 1) * COPY_SET]
                        nc.vector.tensor_tensor(same[:, s, :, :], ps_src[s][:].rearrange("p (n e) -> p n e", n=COPY_SET),
                                                mine.unsqueeze(2).to_broadcast([P, COPY_SET, P]), ALU.is_equal)
                        if not (first and h == 0 and g < 1):
                            dve.wait_ge(same_ready, n)
                        for m in range(COPY_SET):
                            k = g * COPY_SET + m
                            last = nc.vector.scalar_tensor_tensor(
                                out=earlier[:, m, :], in0=ps_src[s][:, m * P:(m + 1) * P], scalar=source[:, h, k:k + 1],
                                in1=lower[:], op0=ALU.is_equal, op1=ALU.mult, accum_out=n_earlier[:, k:k + 1])
                        last.then_inc(same_ready, 1)

                    def scale(g):
                        s, n = g % 2, groups * t + g
                        dve.wait_ge(product, n + 1)
                        if not (first and h == 0 and g < 2):
                            dve.wait_ge(set_summed, n - 1)
                        wide = [P, COPY_SET, GRID, FEAT]
                        nc.vector.tensor_tensor(
                            scaled_w[:, s, :, :].rearrange("p n (u f) -> p n u f", f=FEAT),
                            ps_z[s][:].rearrange("p (n u f) -> p n u f", n=COPY_SET, f=FEAT),
                            tent_of(h, 0)[:, g * COPY_SET:(g + 1) * COPY_SET, :].unsqueeze(3).to_broadcast(wide),
                            ALU.mult).then_inc(scaled_ready, 1)

                    compare(0)
                    for g in range(1, groups):
                        compare(g)
                        scale(g - 1)
                    scale(groups - 1)

                    b = t * TARGET
                    if not first:
                        for s in range(2):
                            dve.wait_ge(added[s], 16 * COPY_SET * (groups // 2) * (t - 1))
                    dve.wait_ge(same_ready, groups * (t + 1))
                    nc.vector.tensor_scalar(to_spare[:], source[:, h, :], -1.0, spare_row[:, 0:1], ALU.mult, ALU.add
                                            ).then_inc(target_step, 1)
                    dve.wait_ge(target_step, b + 1)
                    nc.vector.scalar_tensor_tensor(out=to_spare[:], in0=n_earlier[:], scalar=0.0, in1=to_spare[:],
                                                   op0=ALU.is_gt, op1=ALU.mult).then_inc(target_step, 1)
                    dve.wait_ge(target_step, b + 2)
                    nc.vector.tensor_tensor(target[:, h, :], to_spare[:], source[:, h, :], ALU.add
                                            ).then_inc(target_ready, 1)
                    dve.wait_ge(target_ready, t + 1)
                    dve.sem_inc(target_step, 1)

                prepare_block(0, 0, True)
                prepare_block(0, 1, True)
                for h in range(2):
                    block_work(0, h, True)
                    prepare_block(1, h, False)
                with dve.Fori(1, BLOCKS // 2 - 1) as i:
                    for h in range(2):
                        block_work(i, h, False)
                        prepare_block(i + 1, h, False)
                for h in range(2):
                    block_work(BLOCKS // 2 - 1, h, False)

            @block.tensor
            def _(pe):
                def turn(i, h, g, first):
                    t = 2 * i + h
                    s, n = g % 2, groups * t + g
                    fresh = first and h == 0 and g < 2
                    pe.wait_ge(prepared, t + 1)
                    if not fresh:
                        pe.wait_ge(same_ready, n - 1)
                    for m in range(COPY_SET):
                        k = g * COPY_SET + m
                        mm = nc.tensor.matmul(ps_src[s][:, m * P:(m + 1) * P],
                                              source[:, h, k:k + 1].to_broadcast([P, P]), ident[:],
                                              start=True, stop=True)
                    mm.then_inc(src_ready, 1)
                    pe.wait_ge(spread_ready, t + 1)
                    if not fresh:
                        pe.wait_ge(turned_copied, n - 1)
                    for m in range(COPY_SET):
                        mm = nc.tensor.transpose(ps_t[s][:, m * P:(m + 1) * P],
                                                 spread[:, h, g * COPY_SET + m, :], ident[:])
                    mm.then_inc(turned, 1)

                def multiply(i, h, g, first):
                    t = 2 * i + h
                    s, n = g % 2, groups * t + g
                    pe.wait_ge(turned_copied, n + 1)
                    if not (first and h == 0 and g < 2):
                        pe.wait_ge(scaled_ready, n - 1)
                    for m in range(COPY_SET):
                        mm = nc.tensor.matmul(ps_z[s][:, m * P:(m + 1) * P], spread_t[:, s, m, :], w1_sb[:],
                                              start=True, stop=True)
                    mm.then_inc(product, 1)

                def add_up(i, h, g, first):
                    t = 2 * i + h
                    s, n = g % 2, groups * t + g
                    pe.wait_ge(scaled_ready, n + 1)
                    pe.wait_ge(same_ready, n + 1)
                    if not first and g == 0:
                        pe.wait_ge(summed_ready, t - 1)
                    for m in range(COPY_SET):
                        k = g * COPY_SET + m
                        for u in range(GRID):
                            mm = nc.tensor.matmul(ps_sum[h][:, k * FEAT:(k + 1) * FEAT], same[:, s, m, :],
                                                  scaled_w[:, s, m, u * FEAT:(u + 1) * FEAT],
                                                  start=(u == 0), stop=(u == GRID - 1))
                    mm.then_inc(set_summed, 1)

                def block_work(i, h, first):
                    for g in range(groups + 2):
                        if g < groups:
                            turn(i, h, g, first)
                        if 1 <= g <= groups:
                            multiply(i, h, g - 1, first)
                        if g >= 2:
                            add_up(i, h, g - 2, first)

                block_work(0, 0, True)
                block_work(0, 1, True)
                with pe.Fori(1, BLOCKS // 2) as i:
                    for h in range(2):
                        block_work(i, h, False)

            @block.scalar
            def _(act):
                def copies(i, h, first):
                    t = 2 * i + h
                    for g in range(groups):
                        s, n = g % 2, groups * t + g
                        act.wait_ge(turned, n + 1)
                        if not (first and h == 0 and g < 2):
                            act.wait_ge(product, n - 1)
                        nc.scalar.copy(spread_t[:, s, :, :].rearrange("p n e -> p (n e)"), ps_t[s][:]
                                       ).then_inc(turned_copied, 1)
                    act.wait_ge(set_summed, groups * (t + 1))
                    if not first:
                        for s in range(2):
                            act.wait_ge(added[s], 16 * COPY_SET * (groups // 2) * (t - 1))
                    nc.scalar.copy(summed[:, h, :, :].rearrange("p k f -> p (k f)"), ps_sum[h][:]
                                   ).then_inc(summed_ready, 1)

                copies(0, 0, True)
                copies(0, 1, True)
                with act.Fori(1, BLOCKS // 2) as i:
                    for h in range(2):
                        copies(i, h, False)


def edge_loop(nc, records, table, sums, ident):
    with ExitStack() as ctx:
        def sb(name, shape, dt=F32):
            return ctx.enter_context(nc.sbuf_tensor(f"{name}_e", shape, dt))

        def ps(name):
            return ctx.enter_context(nc.psum_tensor(f"{name}_e", [P, BLOCK], F32))

        def sem(name):
            return ctx.enter_context(nc.semaphore(f"{name}_e"))

        rec = sb("rec", [P, 2, QUARTERS, PER_PART + 1, REC], I32)
        idx = sb("idx", [P, 2, TILES_PER_BLOCK], I32)
        goes_on = sb("goes_on", [P, 2, PER_PART, QUARTERS * FEAT], BF16)
        ident_b = sb("ident_b", [P, P], BF16)
        got = sb("got", [P, 2, TILES_PER_BLOCK, FEAT])
        weighed = sb("weighed", [P, 2, PER_PART, QUARTERS * FEAT])
        keep = sb("keep", [P, 2, BLOCK])
        running = sb("running", [P, 2, BLOCK])
        turned_sb = sb("turned_sb", [P, 2, QUARTERS, PER_PART, FEAT])

        ps_keep = [ps(f"ps_keep{h}") for h in range(2)]
        ps_msg = [ps(f"ps_msg{h}") for h in range(2)]
        ps_sum = [ps(f"ps_sum{h}") for h in range(2)]

        rec_in = [sem(f"rec_in{h}") for h in range(2)]
        gathered = [sem(f"gathered{h}") for h in range(2)]
        stored = [sem(f"stored{h}") for h in range(2)]
        prepared, weighed_ready = sem("prepared"), sem("weighed_ready")
        keep_turned, keep_ready, msg_ready = sem("keep_turned"), sem("keep_ready"), sem("msg_ready")
        scanned, sum_turned, sum_ready = sem("scanned"), sem("sum_turned"), sem("sum_ready")
        start = sem("start")
        pool_waited = sem("pool_waited")

        with nc.Block() as block:

            @block.sync
            def _(sp):
                def load(t, h):
                    sp.dma_start(
                        rec[:, h, :, :, :].rearrange("p q e r -> p q (e r)"),
                        bass.AP(records, t * (BLOCK * REC),
                                [[PER_PART * REC, P], [QEDGES * REC, QUARTERS], [1, (PER_PART + 1) * REC]])
                    ).then_inc(rec_in[h], 16)

                def store(t, h):
                    sp.wait_ge(sum_ready, t + 1)
                    sp.dma_start(
                        bass.AP(sums, t * (BLOCK * FEAT),
                                [[PER_PART * FEAT, P], [QEDGES * FEAT, QUARTERS], [1, PER_PART * FEAT]]),
                        turned_sb[:, h, :, :, :].rearrange("p q e f -> p q (e f)")).then_inc(stored[h], 16)

                load(0, 0)
                load(1, 1)
                with sp.Fori(0, BLOCKS // 2 - 1) as i:
                    for h in range(2):
                        t = 2 * i + h
                        sp.wait_ge(weighed_ready, t + 1)
                        load(t + 2, h)
                        store(t, h)
                for h in range(2):
                    store(BLOCKS - 2 + h, h)
                for h in range(2):
                    sp.wait_ge(stored[h], 16 * (BLOCKS // 2))

            @block.gpsimd
            def _(pool):
                def fetch(i, h, first):
                    t = 2 * i + h
                    pool.wait_ge(prepared, t + 1)
                    if not first:
                        pool.wait_ge(weighed_ready, t - 1)
                    pool.sem_inc(pool_waited, 1)
                    for k in range(TILES_PER_BLOCK):
                        pool.indirect_dma_start(
                            out=got[:, h, k, :], out_offset=None, in_=table.ap(),
                            in_offset=bass.IndirectOffsetOnAxis(ap=idx[:, h, k:k + 1], axis=0)
                        ).then_inc(gathered[h], 16)

                fetch(0, 0, True)
                fetch(0, 1, True)
                with pool.Fori(1, BLOCKS // 2) as i:
                    for h in range(2):
                        fetch(i, h, False)

            @block.vector
            def _(dve):
                nc.vector.memset(running[:, 1, BLOCK - 1:BLOCK], 0.0).then_inc(start, 1)
                nc.vector.tensor_copy(ident_b[:], ident[:]).then_inc(start, 1)
                dve.wait_ge(start, 2)

                def prepare_block(i, h, first):
                    t = 2 * i + h
                    dve.wait_ge(rec_in[h], 16 * i + 16)
                    r = rec[:, h, :, 1:, :].rearrange("p q e r -> p e q r")
                    before = rec[:, h, :, 0:PER_PART, :].rearrange("p q e r -> p e q r")

                    def quad(ap):
                        return ap.rearrange("p (e q) -> p e q", q=QUARTERS)

                    nc.vector.scalar_tensor_tensor(out=quad(idx[:, h, :]), in0=r[:, :, :, R_SRC], scalar=float(RELS),
                                                   in1=r[:, :, :, R_TYPE], op0=ALU.mult, op1=ALU.add)
                    if not first:
                        dve.wait_ge(keep_turned, t - 1)
                    wide = [P, PER_PART, QUARTERS, FEAT]
                    nc.vector.tensor_tensor(
                        goes_on[:, h, :, :].rearrange("p e (q f) -> p e q f", q=QUARTERS),
                        r[:, :, :, R_DST].unsqueeze(3).to_broadcast(wide),
                        before[:, :, :, R_DST].unsqueeze(3).to_broadcast(wide),
                        ALU.is_equal).then_inc(prepared, 1)

                def weigh(i, h):
                    t = 2 * i + h
                    dve.wait_ge(gathered[h], 16 * TILES_PER_BLOCK * (i + 1))
                    norm = rec[:, h, :, 1:, R_NORM].bitcast(F32).rearrange("p q e -> p e q")
                    nc.vector.tensor_tensor(
                        weighed[:, h, :, :].rearrange("p e (q f) -> p e q f", q=QUARTERS),
                        got[:, h, :, :].rearrange("p (e q) f -> p e q f", q=QUARTERS),
                        norm.unsqueeze(3).to_broadcast([P, PER_PART, QUARTERS, FEAT]),
                        ALU.mult).then_inc(weighed_ready, 1)

                def scan(i, h, first):
                    t = 2 * i + h
                    dve.wait_ge(keep_ready, t + 1)
                    dve.wait_ge(msg_ready, t + 1)
                    if not first:
                        dve.wait_ge(sum_turned, t - 1)
                    if not (first and h == 0):
                        dve.wait_ge(scanned, t)
                    nc.vector.tensor_tensor_scan(running[:, h, :], keep[:, h, :], ps_msg[h][:],
                                                 running[:, 1 - h, BLOCK - 1:BLOCK], ALU.mult, ALU.add
                                                 ).then_inc(scanned, 1)

                prepare_block(0, 0, True)
                prepare_block(0, 1, True)
                for h in range(2):
                    weigh(0, h)
                    prepare_block(1, h, False)
                    scan(0, h, True)
                with dve.Fori(1, BLOCKS // 2 - 1) as i:
                    for h in range(2):
                        weigh(i, h)
                        prepare_block(i + 1, h, False)
                        scan(i, h, False)
                for h in range(2):
                    weigh(BLOCKS // 2 - 1, h)
                    scan(BLOCKS // 2 - 1, h, False)

            @block.tensor
            def _(pe):
                def turn(i, h, first):
                    t = 2 * i + h
                    pe.wait_ge(prepared, t + 1)
                    if not first:
                        pe.wait_ge(keep_ready, t - 1)
                    for e in range(PER_PART):
                        mm = nc.tensor.matmul(ps_keep[h][:].rearrange("m (p e) -> m e p", e=PER_PART)[:, e, :],
                                              goes_on[:, h, e, :], ident_b[:],
                                              start=True, stop=True)
                    mm.then_inc(keep_turned, 1)
                    pe.wait_ge(weighed_ready, t + 1)
                    if not first:
                        pe.wait_ge(scanned, t - 1)
                    for e in range(PER_PART):
                        mm = nc.tensor.matmul(ps_msg[h][:].rearrange("m (p e) -> m e p", e=PER_PART)[:, e, :],
                                              weighed[:, h, e, :], ident[:], start=True, stop=True)
                    mm.then_inc(msg_ready, 1)
                    pe.wait_ge(scanned, t + 1)
                    if not first:
                        pe.wait_ge(sum_ready, t - 1)
                    for e in range(PER_PART):
                        mm = nc.tensor.transpose(ps_sum[h][:, e * P:(e + 1) * P],
                                                 running[:, h, :].rearrange("m (p e) -> m e p", e=PER_PART)[:, e, :],
                                                 ident[:])
                    mm.then_inc(sum_turned, 1)

                pe.wait_ge(start, 2)
                turn(0, 0, True)
                turn(0, 1, True)
                with pe.Fori(1, BLOCKS // 2) as i:
                    for h in range(2):
                        turn(i, h, False)

            @block.scalar
            def _(act):
                def copies(i, h, first):
                    t = 2 * i + h
                    act.wait_ge(keep_turned, t + 1)
                    if not first:
                        act.wait_ge(scanned, t - 1)
                    nc.scalar.copy(keep[:, h, :], ps_keep[h][:]).then_inc(keep_ready, 1)
                    act.wait_ge(sum_turned, t + 1)
                    if not first:
                        act.wait_ge(stored[h], 16 * i)
                    nc.scalar.copy(turned_sb[:, h, :, :, :].rearrange("p q e f -> p e q f"),
                                   ps_sum[h][:].rearrange("p (e q f) -> p e q f", e=PER_PART, q=QUARTERS)
                                   ).then_inc(sum_ready, 1)

                copies(0, 0, True)
                copies(0, 1, True)
                with act.Fori(1, BLOCKS // 2) as i:
                    for h in range(2):
                        copies(i, h, False)


def update_nodes(nc, accs, table2, x_sb, ident, w2_sb, eps_sb):
    with ExitStack() as ctx:
        def sb(name, shape, dt=F32):
            return ctx.enter_context(nc.sbuf_tensor(f"{name}_u", shape, dt))

        def ps(name):
            return ctx.enter_context(nc.psum_tensor(f"{name}_u", [P, 512], F32))

        def sem(name):
            return ctx.enter_context(nc.semaphore(f"{name}_u"))

        parts = sb("parts", [P, 2, COPIES, GCOLS])
        total = sb("total", [P, GCOLS])
        ln = ln_buffers(sb)
        ht = sb("ht", [P, 2, 2, P])
        rows_sb = sb("rows_sb", [P, GROUP, TAB2_NODE])
        ps_t = [ps(f"ps_t{i}") for i in range(2)]
        ps_w = [ps(f"ps_w{i}") for i in range(W_BANKS)]
        parts_in = [sem(f"parts_in{h}") for h in range(2)]
        totalled, x_ready = sem("totalled"), sem("x_ready")
        ln_step, var_ready, std_ready, h_ready = sem("ln_step"), sem("var_ready"), sem("std_ready"), sem("h_ready")
        turned, ht_ready, product, evacuated = sem("turned"), sem("ht_ready"), sem("product"), sem("evacuated")
        stored = [sem(f"stored{k}") for k in range(GROUP)]

        with nc.Block() as block:

            @block.sync
            def _(sp):
                def load(i, h, first):
                    j = 2 * i + h
                    if not first:
                        sp.wait_ge(totalled, j - 1)
                    for n, acc in enumerate(accs):
                        sp.dma_start(parts[:, h, n, :].rearrange("p (t f) -> p t f", f=FEAT),
                                     bass.AP(acc, j * (GROUP * P * FEAT), [[FEAT, P], [P * FEAT, GROUP], [1, FEAT]])
                                     ).then_inc(parts_in[h], 16)

                load(0, 0, True)
                load(0, 1, True)
                with sp.Fori(1, GROUPS // 2) as i:
                    for h in range(2):
                        load(i, h, False)

            @block.vector
            def _(dve):
                def update(i, h, first):
                    j = 2 * i + h
                    xg = x_sb[:, bass.ds(j * GCOLS, GCOLS)]
                    dve.wait_ge(parts_in[h], 16 * COPIES * (i + 1))
                    nc.vector.tensor_reduce(total[:], parts[:, h, :, :].rearrange("p n c -> p c n"), AX, ALU.add
                                            ).then_inc(totalled, 1)
                    dve.wait_ge(totalled, j + 1)
                    nc.vector.tensor_tensor(xg, xg, total[:], ALU.add).then_inc(x_ready, 1)
                    dve.wait_ge(x_ready, j + 1)
                    if not first:
                        dve.wait_ge(turned, j - 1)
                    ln_group(nc, dve, ln, xg, j, h, ln_step, var_ready, std_ready, h_ready)

                update(0, 0, True)
                update(0, 1, True)
                with dve.Fori(1, GROUPS // 2) as i:
                    for h in range(2):
                        update(i, h, False)

            @block.tensor
            def _(pe):
                def group(j, h, first):
                    turn_and_multiply(nc, pe, ln, ps_t, ps_w, ht, w2_sb, ident, j, h, first,
                                      h_ready, turned, ht_ready, product, evacuated)

                group_first(group)
                with pe.Fori(1, GROUPS // 2) as i:
                    for h in range(2):
                        group(2 * i + h, h, False)

            @block.scalar
            def _(act):
                def group(j, h, first, more=True):
                    table_rows(nc, act, ln, ps_t, ps_w, ht, rows_sb, eps_sb, table2, j, h, first, more,
                               var_ready, std_ready, turned, ht_ready, product, evacuated, stored)

                root(nc, act, ln, eps_sb, 0, 0, var_ready, std_ready)
                group_first(group)
                with act.Fori(1, GROUPS // 2 - 1) as i:
                    for h in range(2):
                        group(2 * i + h, h, False)
                group(GROUPS - 2, 0, False)
                group(GROUPS - 1, 1, False, more=False)
                for k in range(GROUP):
                    act.wait_ge(stored[k], 16 * GROUPS)


def node_loop(nc, records, sums, x_sb, last_edge, local_id, group_base, carry_id, out):
    with ExitStack() as ctx:
        def sb(name, shape, dt=F32):
            return ctx.enter_context(nc.sbuf_tensor(f"{name}_n", shape, dt))

        def ps(name):
            return ctx.enter_context(nc.psum_tensor(f"{name}_n", [P, 512], F32))

        def sem(name):
            return ctx.enter_context(nc.semaphore(f"{name}_n"))

        K = QUARTERS - 1
        ends_dst = sb("ends_dst", [K, 2, REC], I32)
        ends_sum = sb("ends_sum", [K, FEAT])
        same = sb("same", [K, 1])
        cut_id = sb("cut_id", [K, 1])
        idx = sb("idx", [P, 2, GROUP], I32)
        picked = sb("picked", [P, 2, GROUP, FEAT])
        owner = sb("owner", [K, 2, GROUP * P])
        new_x = sb("new_x", [P, 2, GCOLS])
        ps_carry = [ps(f"ps_carry{h}") for h in range(2)]

        ends_in, ends_step = sem("ends_in"), sem("ends_step")
        idx_ready, owner_ready, carry_ready = sem("idx_ready"), sem("owner_ready"), sem("carry_ready")
        picked_in = [sem(f"picked_in{h}") for h in range(2)]
        carried, x_ready = sem("carried"), sem("x_ready")
        pool_waited = sem("pool_waited")
        out_stored = [sem(f"out_stored{h}") for h in range(2)]

        with nc.Block() as block:

            @block.sync
            def _(sp):
                sp.dma_start(ends_dst[:].rearrange("k a r -> k (a r)"),
                             bass.AP(records, QEDGES * REC, [[QEDGES * REC, K], [1, 2 * REC]])).then_inc(ends_in, 16)
                sp.dma_start(ends_sum[:], bass.AP(sums, (QEDGES - 1) * FEAT, [[QEDGES * FEAT, K], [1, FEAT]])
                             ).then_inc(ends_in, 16)
                def store(i, h, tiles):
                    j = 2 * i + h
                    sp.wait_ge(x_ready, j + 1)
                    sp.dma_start(
                        bass.AP(out.tensor, j * (GROUP * P * FEAT), [[FEAT, P], [P * FEAT, tiles], [1, FEAT]]),
                        new_x[:, h, 0:tiles * FEAT].rearrange("p (t f) -> p t f", f=FEAT)
                    ).then_inc(out_stored[h], 16)

                with sp.Fori(0, GROUPS // 2 - 1) as i:
                    for h in range(2):
                        store(i, h, GROUP)
                store(GROUPS // 2 - 1, 0, GROUP)
                store(GROUPS // 2 - 1, 1, GROUP - 1)
                sp.dma_start(out[(TILES - 1) * P:NODES, :],
                             new_x[0:LAST_ROWS, 1, (GROUP - 1) * FEAT:]).then_inc(out_stored[1], 16)
                sp.wait_ge(out_stored[0], 16 * (GROUPS // 2))
                sp.wait_ge(out_stored[1], 16 * (GROUPS // 2) + 16)

            @block.gpsimd
            def _(pool):
                def fetch(i, h, first):
                    j = 2 * i + h
                    pool.wait_ge(idx_ready, j + 1)
                    if not first:
                        pool.wait_ge(x_ready, j - 1)
                    pool.sem_inc(pool_waited, 1)
                    for k in range(GROUP):
                        pool.indirect_dma_start(
                            out=picked[:, h, k, :], out_offset=None, in_=sums.ap(),
                            in_offset=bass.IndirectOffsetOnAxis(ap=idx[:, h, k:k + 1], axis=0)
                        ).then_inc(picked_in[h], 16)

                fetch(0, 0, True)
                fetch(0, 1, True)
                with pool.Fori(1, GROUPS // 2) as i:
                    for h in range(2):
                        fetch(i, h, False)

            @block.vector
            def _(dve):
                def indices(i, h):
                    nc.vector.tensor_copy(idx[:, h, :], last_edge[:, bass.ds((2 * i + h) * GROUP, GROUP)]
                                          ).then_inc(idx_ready, 1)

                def owners(i, h, first):
                    j = 2 * i + h
                    if not first:
                        dve.wait_ge(carry_ready, j - 1)
                    nc.vector.tensor_scalar(owner[:, h, :], local_id[:], carry_id[:, bass.ds(j, 1)], None,
                                            ALU.is_equal).then_inc(owner_ready, 1)

                def add(i, h, first):
                    j = 2 * i + h
                    xg = x_sb[:, bass.ds(j * GCOLS, GCOLS)]
                    dve.wait_ge(carry_ready, j + 1)
                    if not first:
                        dve.wait_ge(out_stored[h], 16 * i)
                    nc.vector.tensor_tensor(new_x[:, h, :], xg, ps_carry[h][:, 0:GCOLS], ALU.add).then_inc(carried, 1)
                    dve.wait_ge(carried, j + 1)
                    dve.wait_ge(picked_in[h], 16 * GROUP * (i + 1))
                    nc.vector.tensor_tensor(new_x[:, h, :], new_x[:, h, :],
                                            picked[:, h, :, :].rearrange("p t f -> p (t f)"),
                                            ALU.add).then_inc(x_ready, 1)

                indices(0, 0)
                indices(0, 1)
                dve.wait_ge(ends_in, 32)
                nc.vector.tensor_tensor(same[:], ends_dst[:, 0, R_DST:R_DST + 1], ends_dst[:, 1, R_DST:R_DST + 1],
                                        ALU.is_equal).then_inc(ends_step, 1)
                dve.wait_ge(ends_step, 1)
                nc.vector.scalar_tensor_tensor(out=cut_id[:], in0=ends_dst[:, 0, R_DST:R_DST + 1], scalar=1.0,
                                               in1=same[:], op0=ALU.add, op1=ALU.mult).then_inc(ends_step, 1)
                dve.wait_ge(ends_step, 2)
                nc.vector.tensor_scalar(cut_id[:], cut_id[:], -1.0, None, ALU.add).then_inc(ends_step, 1)
                dve.wait_ge(ends_step, 3)
                nc.vector.tensor_scalar(carry_id[:], group_base[:], cut_id[:, 0:1], None, ALU.add
                                        ).then_inc(ends_step, 1)
                dve.wait_ge(ends_step, 4)
                owners(0, 0, True)
                owners(0, 1, True)
                for h in range(2):
                    add(0, h, True)
                    indices(1, h)
                    owners(1, h, False)
                with dve.Fori(1, GROUPS // 2 - 1) as i:
                    for h in range(2):
                        add(i, h, False)
                        indices(i + 1, h)
                        owners(i + 1, h, False)
                for h in range(2):
                    add(GROUPS // 2 - 1, h, False)

            @block.tensor
            def _(pe):
                pe.wait_ge(ends_in, 32)

                def carry(j, h, first):
                    pe.wait_ge(owner_ready, j + 1)
                    if not first:
                        pe.wait_ge(carried, j - 1)
                    for k in range(GROUP):
                        mm = nc.tensor.matmul(ps_carry[h][:, k * FEAT:(k + 1) * FEAT],
                                              owner[:, h, k * P:(k + 1) * P], ends_sum[:], start=True, stop=True)
                    mm.then_inc(carry_ready, 1)

                carry(0, 0, True)
                carry(1, 1, True)
                with pe.Fori(1, GROUPS // 2) as i:
                    for h in range(2):
                        carry(2 * i + h, h, False)


_INS = ["x", "src", "dst", "edge_attr_2", "edge_type_16", "edge_weight1", "L0_gnn_weight", "L1_gnn_weight",
        "L1_gnn_w_comp"]


def kernel(**inputs):
    import concourse.bacc as _bacc
    from concourse.bass_utils import run_bass_kernel_spmd as _run

    nc = _bacc.Bacc("TRN2", target_bir_lowering=False, num_devices=1)
    arrays, args = {}, []
    for name in _INS:
        a = np.ascontiguousarray(inputs[name])
        arrays[f"in_{name}"] = a
        args.append(nc.dram_tensor(f"in_{name}", a.shape, mybir.dt.from_np(a.dtype), kind="ExternalInput").ap())
    out = nc.dram_tensor("out", (NODES, FEAT), F32, kind="ExternalOutput").ap()
    gnn_kernel(nc, *args, out)
    r = _run(nc, [arrays], core_ids=[0])
    return r.results[0]["out"]
```

```python
from contextlib import ExitStack

import numpy as np

import concourse.bass as bass
from concourse import mybir

ALU = mybir.AluOpType
ACT = mybir.ActivationFunctionType
AX = mybir.AxisListType.X
F32 = mybir.dt.float32
I32 = mybir.dt.int32
BF16 = mybir.dt.bfloat16

P = 128
FEAT = 32
NODES = 12500
EDGES = 412500
RELS = 16
BASES = 8
GRID = 4
EPS = 1e-5

TILES = -(-NODES // P)
LAST_ROWS = NODES - (TILES - 1) * P
GROUP = 7
GROUPS = TILES // GROUP
GCOLS = GROUP * FEAT
assert GROUPS * GROUP == TILES and GROUPS % 2 == 0

QUARTERS = 4
PER_PART = 4
BLOCK = P * PER_PART
TILES_PER_BLOCK = QUARTERS * PER_PART
BLOCKS = 2 * -(-EDGES // (2 * QUARTERS * BLOCK))
QEDGES = BLOCKS * BLOCK
PADDED = QUARTERS * QEDGES
assert PADDED >= EDGES

REC = 8
R_DST, R_SRC, R_TYPE, R_ATTR, R_NORM = 0, 1, 2, 3, 5

STAGE_CHUNKS = 18
STAGE_COLS = EDGES // P // STAGE_CHUNKS
STAGED = P * STAGE_CHUNKS * STAGE_COLS
TAIL_COLS = (PADDED - STAGED) // P
TAIL_ROWS, TAIL_REST = divmod(EDGES - STAGED, TAIL_COLS)
assert TAIL_COLS * P + STAGED == PADDED and STAGE_CHUNKS % 2 == 0

SPAN = 625
SPANS = EDGES // SPAN
assert SPAN * SPANS == EDGES

NODE_ROWS = TILES * P
ACC_WORDS = (NODE_ROWS + P) // P * FEAT
ZERO_STORES = 32
ZERO_WORDS = PADDED * FEAT // P // ZERO_STORES
assert ZERO_WORDS * ZERO_STORES * P == PADDED * FEAT and ZERO_WORDS >= ACC_WORDS
COPIES = 8
COPY_SET = 4
TAB2_NODE = RELS * FEAT
W_COLS = GRID * GRID * FEAT
W_BANKS = 4


def gnn_kernel(nc, x, src, dst, edge_attr, edge_type, edge_weight, w_basis, w_rel, w_comp, out):
    records = nc.dram_tensor("records", [PADDED + 1, REC], I32)
    h_table = nc.dram_tensor("h_table", [NODE_ROWS, FEAT], F32)
    placed = nc.dram_tensor("placed", [PADDED + NODE_ROWS, FEAT], F32)
    starts = nc.dram_tensor("starts", [QUARTERS, FEAT], F32)
    accs = [nc.dram_tensor(f"acc{n}", [NODE_ROWS + P, FEAT], F32) for n in range(COPIES)]
    table2 = nc.dram_tensor("table2", [TILES * P * RELS, FEAT], F32)
    sums = nc.dram_tensor("sums", [PADDED + 1, FEAT], F32)

    with ExitStack() as ctx:
        def sb(name, shape, dt=F32):
            return ctx.enter_context(nc.sbuf_tensor(name, shape, dt))

        def sem(name):
            return ctx.enter_context(nc.semaphore(name))

        x_sb = sb("x_sb", [P, TILES * FEAT])
        ident = sb("ident", [P, P])
        w1_sb = sb("w1_sb", [P, GRID * FEAT])
        spare_row = sb("spare_row", [P, 1])
        ident_b = sb("ident_b", [P, P], BF16)
        fours = sb("fours", [P, 2])
        limits = sb("limits", [P, 2])
        w2_sb = sb("w2_sb", [P, W_COLS])
        node_id = sb("node_id", [P, TILES])
        last_edge = sb("last_edge", [P, TILES], I32)
        local_id = sb("local_id", [QUARTERS - 1, GROUP * P])
        group_base = sb("group_base", [QUARTERS - 1, GROUPS])
        carry_id = sb("carry_id", [QUARTERS - 1, GROUPS])
        eps_sb = sb("eps_sb", [P, 1])

        prepare(nc, x, src, dst, edge_attr, edge_type, edge_weight, w_basis, w_rel, w_comp,
                records, sums, accs, x_sb, ident, w1_sb, w2_sb, node_id, last_edge, local_id,
                group_base, eps_sb, spare_row, ident_b, fours, limits, h_table, placed)
        scatter_loop(nc, records, h_table, placed, starts, accs, ident, ident_b, w1_sb, spare_row,
                     fours, limits)
        update_nodes(nc, accs, table2, x_sb, ident, w2_sb, eps_sb)
        edge_loop(nc, records, table2, sums, ident, ident_b)
        node_loop(nc, records, sums, x_sb, last_edge, local_id, group_base, carry_id, out)


def ln_buffers(sb):
    return dict(total=sb("ln_total", [P, GROUP]), cent=sb("ln_cent", [P, GROUP, FEAT]),
                square=sb("ln_square", [P, GROUP, FEAT]), var=sb("ln_var", [P, 2, GROUP]),
                std=sb("ln_std", [P, 2, GROUP]), rstd=sb("ln_rstd", [P, GROUP]),
                h=sb("ln_h", [P, 2, GCOLS]))


LN_STEPS = 5


def ln_group(nc, dve, ln, xg, j, h, ln_step, var_ready, std_ready, h_ready):
    b = j * LN_STEPS
    dve.sem_inc(ln_step, 1)
    xg3 = xg.rearrange("p (t f) -> p t f", f=FEAT)
    nc.vector.tensor_reduce(ln["total"][:], xg3, AX, ALU.add).then_inc(ln_step, 1)
    dve.wait_ge(ln_step, b + 2)
    nc.vector.scalar_tensor_tensor(
        out=ln["cent"][:], in0=ln["total"][:].unsqueeze(2).to_broadcast([P, GROUP, FEAT]),
        scalar=-1.0 / FEAT, in1=xg3, op0=ALU.mult, op1=ALU.add).then_inc(ln_step, 1)
    dve.wait_ge(ln_step, b + 3)
    nc.vector.tensor_tensor(ln["square"][:], ln["cent"][:], ln["cent"][:], ALU.mult).then_inc(ln_step, 1)
    dve.wait_ge(ln_step, b + 4)
    nc.vector.tensor_reduce(ln["var"][:, h, :], ln["square"][:], AX, ALU.add).then_inc(var_ready, 1)
    dve.wait_ge(std_ready, j + 1)
    nc.vector.reciprocal(ln["rstd"][:], ln["std"][:, h, :]).then_inc(ln_step, 1)
    dve.wait_ge(ln_step, b + 5)
    nc.vector.scalar_tensor_tensor(
        out=ln["h"][:, h, :].rearrange("p (t f) -> p t f", f=FEAT), in0=ln["cent"][:], scalar=0.0,
        in1=ln["rstd"][:].unsqueeze(2).to_broadcast([P, GROUP, FEAT]),
        op0=ALU.max, op1=ALU.mult).then_inc(h_ready, 1)
    dve.wait_ge(h_ready, j + 1)


def turn_and_multiply(nc, pe, ln, ps_t, ps_w, ht, w_sb, ident, j, h, first,
                      h_ready, turned, ht_ready, product, evacuated):
    pe.wait_ge(h_ready, j + 1)
    if not first:
        pe.wait_ge(ht_ready, j - 1)
    nc.tensor.transpose(ps_t[h][:, 0:P], ln["h"][:, h, 0:P], ident[:])
    nc.tensor.transpose(ps_t[h][0:GCOLS - P, P:2 * P], ln["h"][:, h, P:GCOLS], ident[:]).then_inc(turned, 1)
    pe.wait_ge(ht_ready, j + 1)
    for k in range(GROUP):
        if not first or j * GROUP + k >= W_BANKS:
            pe.wait_ge(evacuated, j * GROUP + k - (W_BANKS - 2))
        rows = slice(FEAT * (k % 4), FEAT * (k % 4) + FEAT)
        nc.tensor.matmul(ps_w[k % W_BANKS][:], ht[rows, h, k // 4, :], w_sb[rows, :],
                         start=True, stop=True).then_inc(product, 1)


def root(nc, act, ln, eps_sb, j, h, var_ready, std_ready):
    act.wait_ge(var_ready, j + 1)
    nc.scalar.activation(ln["std"][:, h, :], ln["var"][:, h, :], ACT.Sqrt, bias=eps_sb[:],
                         scale=1.0 / FEAT).then_inc(std_ready, 1)


def table_rows(nc, act, ln, ps_t, ps_w, ht, rows_sb, eps_sb, table, j, h, first, more,
               var_ready, std_ready, turned, ht_ready, product, evacuated, stored):
    act.wait_ge(turned, j + 1)
    if not first:
        act.wait_ge(product, (j - 1) * GROUP)
    nc.scalar.copy(ht[:, h, 0, :], ps_t[h][:, 0:P])
    nc.scalar.copy(ht[0:GCOLS - P, h, 1, :], ps_t[h][0:GCOLS - P, P:2 * P]).then_inc(ht_ready, 1)
    if more:
        root(nc, act, ln, eps_sb, j + 1, 1 - h, var_ready, std_ready)
    words = TAB2_NODE
    for k in range(GROUP):
        n = j * GROUP + k
        act.wait_ge(product, n + 1)
        if not first or j > 0:
            act.wait_ge(stored[k], 16 * j)
        last = nc.scalar.copy(rows_sb[:, k, :], ps_w[k % W_BANKS][:])
        last.then_inc(evacuated, 1)
        act.wait_ge(evacuated, n + 1)
        act.dma_start(
            bass.AP(table, n * P * words, [[words, P], [1, words]]),
            rows_sb[:, k, 0:words]).then_inc(stored[k], 16)


def prepare(nc, x, src, dst, edge_attr, edge_type, edge_weight, w_basis, w_rel, w_comp,
            records, sums, accs, x_sb, ident, w1_sb, w2_sb, node_id, last_edge, local_id,
            group_base, eps_sb, spare_row, ident_b, fours, limits, h_table, placed):
    with ExitStack() as ctx:
        def sb(name, shape, dt=F32):
            return ctx.enter_context(nc.sbuf_tensor(name, shape, dt))

        def ps(name, shape=(P, 512)):
            return ctx.enter_context(nc.psum_tensor(name, list(shape), F32))

        def sem(name):
            return ctx.enter_context(nc.semaphore(name))

        ln = ln_buffers(sb)
        zero_rows = sb("zero_rows", [P, ZERO_WORDS])
        spare_int = sb("spare_int", [P, 1], I32)
        raw_dst = sb("raw_dst", [P, 2, STAGE_COLS], I32)
        raw_src = sb("raw_src", [P, 2, STAGE_COLS], I32)
        raw_type = sb("raw_type", [P, 2, STAGE_COLS], I32)
        raw_attr = sb("raw_attr", [P, 2, 2 * STAGE_COLS])
        raw_norm = sb("raw_norm", [P, 2, STAGE_COLS])
        rec = sb("rec", [P, 2, STAGE_COLS, REC], I32)
        t_dst = sb("t_dst", [P, TAIL_COLS], I32)
        t_src = sb("t_src", [P, TAIL_COLS], I32)
        t_type = sb("t_type", [P, TAIL_COLS], I32)
        t_attr = sb("t_attr", [P, 2 * TAIL_COLS])
        t_norm = sb("t_norm", [P, TAIL_COLS])
        t_rec = sb("t_rec", [P, TAIL_COLS, REC], I32)
        lead = sb("lead", [1, REC], I32)
        zeros = sb("zeros", [1, FEAT])
        span_first = sb("span_first", [1, SPANS])
        span_int = sb("span_int", [1, SPANS], I32)
        ones_row = sb("ones_row", [1, P])
        span_all = sb("span_all", [P, SPANS])
        id_int = sb("id_int", [P, TILES], I32)
        local_int = sb("local_int", [QUARTERS - 1, GROUP * P], I32)
        base_int = sb("base_int", [QUARTERS - 1, GROUPS], I32)
        ids = sb("ids", [P, 2, GROUP])
        hits = sb("hits", [P, SPANS])
        span_no = sb("span_no", [P, 2, GROUP])
        span_base = sb("span_base", [P, 2, GROUP])
        span_idx = sb("span_idx", [P, 2, GROUP], I32)
        span_dst = sb("span_dst", [P, 2, GROUP, SPAN], I32)
        inside = sb("inside", [P, 2, GROUP])
        upto = sb("upto", [P, 1 + TILES])
        shift = sb("shift", [P, P])
        wrap = sb("wrap", [P, P])
        has = sb("has", [P, TILES])
        edge = sb("edge", [P, 2, TILES])
        quarter = sb("quarter", [P, 2, TILES])
        row = sb("row", [P, 2, TILES])
        spare = sb("spare", [P, 2, TILES])
        first_row = sb("first_row", [P, TILES], I32)
        h_all = sb("h_all", [P, TILES * FEAT])
        place_row = sb("place_row", [P, 2, GROUP], I32)
        place_h = sb("place_h", [P, 2, GROUP, FEAT])
        wr_sb = sb("wr_sb", [BASES, 2 * RELS, FEAT])
        wct = sb("wct", [BASES, RELS])
        wct_pad = sb("wct_pad", [BASES, 2, P])

        ps_t = [ps(f"ps_t{i}") for i in range(2)]
        ps_a, ps_b = ps("ps_a"), ps("ps_b")

        x_pad, x_in, w_in, span_in = sem("x_pad"), sem("x_in"), sem("w_in"), sem("span_in")
        raw_in = [sem(f"raw_in{i}") for i in range(2)]
        rec_out = [sem(f"rec_out{i}") for i in range(2)]
        rec_zero, rec_made = sem("rec_zero"), sem("rec_made")
        tail_zero, tail_in, tail_made, tail_out = sem("tail_zero"), sem("tail_in"), sem("tail_made"), sem("tail_out")
        const_step, ident_ready = sem("const_step"), sem("ident_ready")
        ln_step, var_ready, std_ready, h_ready = sem("ln_step"), sem("var_ready"), sem("std_ready"), sem("h_ready")
        h_stored = [sem(f"h_stored{h}") for h in range(2)]
        zero_ready, acc_zeroed = sem("zero_ready"), sem("acc_zeroed")
        spans_bcast, wrel_ready, setup, search = sem("spans_bcast"), sem("wrel_ready"), sem("setup"), sem("search")
        idx_ready, span_used = sem("idx_ready"), sem("span_used")
        span_got = [sem(f"span_got{i}") for i in range(2)]
        before_ready = sem("before_ready")
        pool_waited = sem("pool_waited")
        inside_step = sem("inside_step")
        counted = sem("counted")
        h_kept, place_zeroed, place_ready = sem("h_kept"), sem("place_zeroed"), sem("place_ready")
        placed_out = [sem(f"placed_out{h}") for h in range(2)]

        raw = [(raw_dst, dst, 1), (raw_src, src, 1), (raw_type, edge_type, 1),
               (raw_attr, edge_attr, 2), (raw_norm, edge_weight, 1)]
        tail = [(t_dst, dst, 1), (t_src, src, 1), (t_type, edge_type, 1), (t_attr, edge_attr, 2),
                (t_norm, edge_weight, 1)]

        with nc.Block() as block:

            @block.sync
            def _(sp):
                whole = (TILES - 1) * P
                sp.wait_ge(x_pad, 1)
                sp.dma_start(x_sb[:, 0:(TILES - 1) * FEAT].rearrange("p (t f) -> p t f", f=FEAT),
                             x[0:whole, :].rearrange("(t p) f -> p t f", p=P)).then_inc(x_in, 16)
                sp.dma_start(x_sb[0:LAST_ROWS, (TILES - 1) * FEAT:], x[whole:NODES, :]).then_inc(x_in, 16)
                for v in range(GRID):
                    sp.dma_start(w1_sb[FEAT * v:FEAT * v + FEAT, :].rearrange("i (u o) -> i u o", o=FEAT),
                                 w_basis[:, v, :, :].rearrange("u i o -> i u o")).then_inc(w_in, 16)
                sp.dma_start(wr_sb[:], bass.AP(w_rel.tensor, 0, [[FEAT, BASES], [BASES * FEAT, 2 * RELS], [1, FEAT]])
                             ).then_inc(w_in, 16)
                with nc.allow_non_contiguous_dma("128 words"):
                    sp.dma_start(wct[:], w_comp.rearrange("r b -> b r")).then_inc(w_in, 16)
                with nc.allow_non_contiguous_dma("the first destination of each span"):
                    sp.dma_start(span_int[:], bass.AP(dst.tensor, 0, [[SPAN * SPANS, 1], [SPAN, SPANS]])
                                 ).then_inc(span_in, 16)

                def load(c, h):
                    for tile, array, width in raw:
                        n = width * STAGE_COLS
                        sp.dma_start(tile[:, h, :], bass.AP(array.tensor, c * n, [[n * STAGE_CHUNKS, P], [1, n]])
                                     ).then_inc(raw_in[h], 16)

                def store(c, h):
                    sp.wait_ge(rec_made, c + 1)
                    n = REC * STAGE_COLS
                    sp.dma_start(bass.AP(records, REC + c * n, [[n * STAGE_CHUNKS, P], [1, n]]),
                                 rec[:, h, :, :].rearrange("p e r -> p (e r)")).then_inc(rec_out[h], 16)

                load(0, 0)
                load(1, 1)
                with sp.Fori(0, STAGE_CHUNKS // 2 - 1) as i:
                    for h in range(2):
                        store(2 * i + h, h)
                        load(2 * i + h + 2, h)
                for h in range(2):
                    store(STAGE_CHUNKS - 2 + h, h)

                sp.wait_ge(tail_zero, 5)
                for tile, array, width in tail:
                    n = width * TAIL_COLS
                    sp.dma_start(tile[0:TAIL_ROWS, :], bass.AP(array.tensor, width * STAGED, [[n, TAIL_ROWS], [1, n]])
                                 ).then_inc(tail_in, 16)
                    sp.dma_start(tile[TAIL_ROWS:TAIL_ROWS + 1, 0:width * TAIL_REST],
                                 bass.AP(array.tensor, width * STAGED + TAIL_ROWS * n, [[n, 1], [1, width * TAIL_REST]])
                                 ).then_inc(tail_in, 16)
                sp.wait_ge(tail_made, 8)
                sp.dma_start(bass.AP(records, REC * (STAGED + 1), [[REC * TAIL_COLS, P], [1, REC * TAIL_COLS]]),
                             t_rec[:, :, :].rearrange("p e r -> p (e r)")).then_inc(tail_out, 16)
                sp.dma_start(bass.AP(records, 0, [[REC, 1], [1, REC]]), lead[:]).then_inc(tail_out, 16)
                sp.dma_start(bass.AP(sums, PADDED * FEAT, [[FEAT, 1], [1, FEAT]]), zeros[:]).then_inc(tail_out, 16)
                sp.wait_ge(tail_out, 48)
                for h in range(2):
                    sp.wait_ge(rec_out[h], 16 * (STAGE_CHUNKS // 2))

            @block.gpsimd
            def _(pool):
                nc.gpsimd.memset(ident[:], 0.0).then_inc(const_step, 1)
                nc.gpsimd.memset(shift[:], 0.0).then_inc(const_step, 1)
                nc.gpsimd.memset(wrap[:], 0.0).then_inc(const_step, 1)
                nc.gpsimd.memset(fours[:], 0.0).then_inc(const_step, 1)
                pool.wait_ge(const_step, 4)
                for half in range(2):
                    nc.gpsimd.iota(fours[half * P // 2:(half + 1) * P // 2, half:half + 1].bitcast(I32),
                                   pattern=[[0, 1]], base=(127 + 64) << 23, channel_multiplier=-(2 << 23)
                                   ).then_inc(const_step, 1)
                    pool.wait_ge(const_step, 5 + half)
                nc.gpsimd.affine_select(out=ident[:], in_=ident[:], compare_op=ALU.not_equal, fill=1.0,
                                        base=0, pattern=[[-1, P]], channel_multiplier=1)
                nc.gpsimd.affine_select(out=shift[:], in_=shift[:], compare_op=ALU.not_equal, fill=1.0,
                                        base=1, pattern=[[-1, P]], channel_multiplier=1)
                nc.gpsimd.affine_select(out=wrap[:], in_=wrap[:], compare_op=ALU.not_equal, fill=1.0,
                                        base=1 - P, pattern=[[-1, P]], channel_multiplier=1)
                nc.gpsimd.iota(id_int[:], pattern=[[P, TILES]], base=0, channel_multiplier=1)
                nc.gpsimd.iota(local_int[:], pattern=[[1, GROUP * P]], base=0, channel_multiplier=0)
                nc.gpsimd.iota(spare_int[:], pattern=[[0, 1]], base=NODE_ROWS, channel_multiplier=1)
                nc.gpsimd.iota(base_int[:], pattern=[[-GROUP * P, GROUPS]], base=0,
                               channel_multiplier=0).then_inc(ident_ready, 1)
                nc.gpsimd.memset(rec[:].rearrange("p a e r -> p (a e r)"), 0).then_inc(rec_zero, 1)
                pool.wait_ge(rec_zero, 1)

                def make(i, h, first):
                    c = 2 * i + h
                    pool.wait_ge(raw_in[h], 80 * i + 80)
                    if not first:
                        pool.wait_ge(rec_out[h], 16 * i)
                    pool.sem_inc(pool_waited, 1)
                    r = rec[:, h, :, :]
                    rf = r.bitcast(F32)
                    nc.gpsimd.tensor_copy(r[:, :, R_DST], raw_dst[:, h, :])
                    nc.gpsimd.tensor_copy(r[:, :, R_SRC], raw_src[:, h, :])
                    nc.gpsimd.tensor_copy(r[:, :, R_TYPE], raw_type[:, h, :])
                    nc.gpsimd.tensor_copy(rf[:, :, R_ATTR:R_ATTR + 2],
                                          raw_attr[:, h, :].rearrange("p (e a) -> p e a", a=2))
                    nc.gpsimd.tensor_copy(rf[:, :, R_NORM], raw_norm[:, h, :]).then_inc(rec_made, 1)

                make(0, 0, True)
                make(0, 1, True)
                with pool.Fori(1, STAGE_CHUNKS // 2) as i:
                    for h in range(2):
                        make(i, h, False)

                nc.gpsimd.memset(t_dst[:], NODES).then_inc(tail_zero, 1)
                for tile in (t_src, t_type, t_attr, t_norm):
                    nc.gpsimd.memset(tile[:], 0).then_inc(tail_zero, 1)
                nc.gpsimd.memset(t_rec[:].rearrange("p e r -> p (e r)"), 0).then_inc(tail_made, 1)
                nc.gpsimd.memset(lead[:], -1).then_inc(tail_made, 1)
                nc.gpsimd.memset(zeros[:], 0.0).then_inc(tail_made, 1)
                pool.wait_ge(tail_made, 3)
                pool.wait_ge(tail_in, 160)
                nc.gpsimd.tensor_copy(t_rec[:, :, R_DST], t_dst[:]).then_inc(tail_made, 1)
                nc.gpsimd.tensor_copy(t_rec[:, :, R_SRC], t_src[:]).then_inc(tail_made, 1)
                nc.gpsimd.tensor_copy(t_rec[:, :, R_TYPE], t_type[:]).then_inc(tail_made, 1)
                nc.gpsimd.tensor_copy(t_rec[:].bitcast(F32)[:, :, R_ATTR:R_ATTR + 2],
                                      t_attr[:].rearrange("p (e a) -> p e a", a=2)).then_inc(tail_made, 1)
                nc.gpsimd.tensor_copy(t_rec[:].bitcast(F32)[:, :, R_NORM], t_norm[:]).then_inc(tail_made, 1)

                spans = dst.rearrange("(s e) -> s e", e=SPAN)

                def fetch(i, h, first):
                    pool.wait_ge(idx_ready, 2 * i + h + 1)
                    if not first:
                        pool.wait_ge(span_used, 2 * i + h - 1)
                    pool.sem_inc(pool_waited, 1)
                    for k in range(GROUP):
                        pool.indirect_dma_start(
                            out=span_dst[:, h, k, :], out_offset=None, in_=spans,
                            in_offset=bass.IndirectOffsetOnAxis(ap=span_idx[:, h, k:k + 1], axis=0)
                        ).then_inc(span_got[h], 16)

                def place(i, h):
                    pool.wait_ge(place_ready, 2 * i + h + 1)
                    pool.sem_inc(pool_waited, 1)
                    for k in range(GROUP):
                        pool.indirect_dma_start(
                            out=placed.ap(), out_offset=bass.IndirectOffsetOnAxis(ap=place_row[:, h, k:k + 1], axis=0),
                            in_=place_h[:, h, k, :], in_offset=None).then_inc(placed_out[h], 16)

                fetch(0, 0, True)
                fetch(0, 1, True)
                with pool.Fori(1, GROUPS // 2) as i:
                    for h in range(2):
                        fetch(i, h, False)
                pool.wait_ge(place_zeroed, 16 * ZERO_STORES)
                with pool.Fori(0, GROUPS // 2) as i:
                    for h in range(2):
                        place(i, h)
                for h in range(2):
                    pool.wait_ge(placed_out[h], 16 * GROUP * (GROUPS // 2))

            @block.vector
            def _(dve):
                nc.vector.memset(x_sb[:, (TILES - 1) * FEAT:], 0.0).then_inc(x_pad, 1)
                nc.vector.memset(eps_sb[:], EPS).then_inc(setup, 1)
                nc.vector.memset(ones_row[:], 1.0).then_inc(setup, 1)
                nc.vector.memset(upto[:, 0:1], 0.0).then_inc(setup, 1)
                nc.vector.memset(wct_pad[:].rearrange("b a c -> b (a c)"), 0.0).then_inc(setup, 1)
                nc.vector.memset(zero_rows[:], 0.0).then_inc(zero_ready, 1)
                dve.wait_ge(setup, 4)
                dve.wait_ge(ident_ready, 1)
                nc.vector.tensor_copy(node_id[:], id_int[:]).then_inc(setup, 1)
                nc.vector.tensor_copy(local_id[:], local_int[:]).then_inc(setup, 1)
                nc.vector.tensor_copy(spare_row[:], spare_int[:])
                nc.vector.tensor_copy(ident_b[:], ident[:])
                nc.vector.tensor_scalar(limits[:], fours[:], 2.0, None, ALU.mult)
                nc.vector.tensor_copy(group_base[:], base_int[:]).then_inc(setup, 1)
                dve.wait_ge(w_in, 96)
                for par in range(2):
                    last = nc.vector.tensor_copy(
                        wct_pad[:, par, :].rearrange("b (g q r) -> b g q r", g=4, q=2)[:, :, par, :],
                        wct[:].unsqueeze(1).to_broadcast([BASES, 4, RELS]))
                last.then_inc(setup, 1)
                dve.wait_ge(span_in, 16)
                nc.vector.tensor_copy(span_first[:], span_int[:]).then_inc(setup, 1)
                dve.wait_ge(x_in, 32)

                def normalise(j, h, first):
                    if not first:
                        dve.wait_ge(h_stored[h], 16 * (j - h) // 2)
                    ln_group(nc, dve, ln, x_sb[:, bass.ds(j * GCOLS, GCOLS)], j, h, ln_step,
                             var_ready, std_ready, h_ready)

                dve.wait_ge(wrel_ready, 1)
                nc.vector.tensor_copy(w2_sb[:], ps_a[:]).then_inc(setup, 1)
                dve.wait_ge(spans_bcast, 1)
                nc.vector.tensor_copy(span_all[:, 0:512], ps_b[:]).then_inc(setup, 1)
                nc.vector.tensor_copy(span_all[:, 512:SPANS], ps_t[1][:, 0:SPANS - 512]).then_inc(setup, 1)
                dve.wait_ge(setup, 12)
                normalise(0, 0, True)
                normalise(1, 1, True)

                steps = GROUP + 3

                def find_span(i, h, first):
                    j = 2 * i + h
                    nc.vector.tensor_copy(ids[:, h, :], node_id[:, bass.ds(j * GROUP, GROUP)]).then_inc(search, 1)
                    dve.wait_ge(search, j * steps + 1)
                    for k in range(GROUP):
                        nc.vector.tensor_scalar(hits[:], span_all[:], ids[:, h, k:k + 1], 0.0, ALU.is_le, ALU.add,
                                                accum_out=span_no[:, h, k:k + 1]).then_inc(search, 1)
                        dve.wait_ge(search, j * steps + k + 2)
                    nc.vector.tensor_scalar(span_no[:, h, :], span_no[:, h, :], -1.0, 0.0, ALU.add, ALU.max
                                            ).then_inc(search, 1)
                    dve.wait_ge(search, j * steps + GROUP + 2)
                    nc.vector.tensor_scalar(span_base[:, h, :], span_no[:, h, :], float(SPAN), None, ALU.mult
                                            ).then_inc(search, 1)
                    nc.vector.tensor_copy(span_idx[:, h, :], span_no[:, h, :]).then_inc(idx_ready, 1)

                def count_inside(i, h):
                    j = 2 * i + h
                    dve.wait_ge(span_got[h], 16 * GROUP * (i + 1))
                    for k in range(GROUP):
                        last = nc.vector.tensor_scalar(
                            hits[:, 0:SPAN], span_dst[:, h, k, :], ids[:, h, k:k + 1], 0.0, ALU.is_le, ALU.add,
                            accum_out=inside[:, h, k:k + 1])
                        if k < GROUP - 1:
                            last.then_inc(inside_step, 1)
                            dve.wait_ge(inside_step, j * (GROUP - 1) + k + 1)
                    last.then_inc(span_used, 1)
                    dve.wait_ge(span_used, j + 1)
                    nc.vector.tensor_tensor(upto[:, bass.ds(1 + j * GROUP, GROUP)], inside[:, h, :],
                                            span_base[:, h, :], ALU.add).then_inc(counted, 1)

                find_span(0, 0, True)
                find_span(0, 1, True)
                with dve.Fori(1, GROUPS // 2) as i:
                    for h in range(2):
                        normalise(2 * i + h, h, False)
                        count_inside(i - 1, h)
                        dve.wait_ge(counted, 2 * i + h - 1)
                        find_span(i, h, False)
                for h in range(2):
                    count_inside(GROUPS // 2 - 1, h)
                dve.wait_ge(counted, GROUPS)
                dve.wait_ge(before_ready, 1)
                nc.vector.memset(limits[0:P // 2, 1:2], 2.0 ** 120)
                nc.vector.tensor_tensor(has[:], upto[:, 1:], ps_b[:, 0:TILES], ALU.is_gt)
                nc.vector.tensor_copy(edge[:, 0, :], ps_b[:, 0:TILES])
                nc.vector.memset(spare[:, 1, :], float(PADDED))
                nc.vector.tensor_scalar(spare[:, 0, :], node_id[:], float(PADDED), None, ALU.add)
                nc.vector.tensor_scalar(edge[:, 1, :], upto[:, 1:], -1.0, None, ALU.add).then_inc(counted, 1)
                dve.wait_ge(counted, GROUPS + 1)
                nc.vector.tensor_scalar(quarter[:], edge[:], float(QEDGES), None, ALU.is_ge)
                nc.vector.scalar_tensor_tensor(out=row[:], in0=edge[:], scalar=float(QUARTERS), in1=spare[:],
                                               op0=ALU.mult, op1=ALU.subtract).then_inc(counted, 1)
                for q in range(2, QUARTERS):
                    dve.wait_ge(counted, GROUPS + q)
                    nc.vector.scalar_tensor_tensor(out=quarter[:], in0=edge[:], scalar=float(q * QEDGES), in1=quarter[:],
                                                   op0=ALU.is_ge, op1=ALU.add).then_inc(counted, 1)
                dve.wait_ge(counted, GROUPS + QUARTERS)
                nc.vector.scalar_tensor_tensor(out=row[:], in0=quarter[:], scalar=-float(QUARTERS * QEDGES - 1),
                                               in1=row[:], op0=ALU.mult, op1=ALU.add).then_inc(counted, 1)
                dve.wait_ge(counted, GROUPS + QUARTERS + 1)
                nc.vector.tensor_tensor(row[:], row[:], has[:].unsqueeze(1).to_broadcast([P, 2, TILES]), ALU.mult
                                        ).then_inc(counted, 1)
                dve.wait_ge(counted, GROUPS + QUARTERS + 2)
                nc.vector.tensor_tensor(first_row[:], row[:, 0, :], spare[:, 0, :], ALU.add)
                nc.vector.tensor_tensor(last_edge[:], row[:, 1, :], spare[:, 1, :], ALU.add).then_inc(counted, 1)
                dve.wait_ge(counted, GROUPS + QUARTERS + 3)
                dve.wait_ge(h_kept, GROUPS)

                def fill(i, h, first):
                    j = 2 * i + h
                    if not first:
                        dve.wait_ge(placed_out[h], 16 * GROUP * i)
                    nc.vector.tensor_copy(place_row[:, h, :], first_row[:, bass.ds(j * GROUP, GROUP)])
                    nc.vector.tensor_copy(place_h[:, h, :, :].rearrange("p t f -> p (t f)"),
                                          h_all[:, bass.ds(j * GCOLS, GCOLS)]).then_inc(place_ready, 1)

                fill(0, 0, True)
                fill(0, 1, True)
                with dve.Fori(1, GROUPS // 2) as i:
                    for h in range(2):
                        fill(i, h, False)

            @block.scalar
            def _(act):
                act.wait_ge(zero_ready, 1)
                for acc in accs:
                    act.dma_start(bass.AP(acc, 0, [[ACC_WORDS, P], [1, ACC_WORDS]]), zero_rows[:, 0:ACC_WORDS]
                                  ).then_inc(acc_zeroed, 16)
                with act.Fori(0, ZERO_STORES) as z:
                    act.dma_start(bass.AP(placed, z * (P * ZERO_WORDS), [[ZERO_WORDS, P], [1, ZERO_WORDS]]), zero_rows[:]
                                  ).then_inc(place_zeroed, 16)
                act.wait_ge(setup, 1)

                def store_h(j, h):
                    act.wait_ge(h_ready, j + 1)
                    nc.scalar.copy(h_all[:, bass.ds(j * GCOLS, GCOLS)], ln["h"][:, h, :]).then_inc(h_kept, 1)
                    act.wait_ge(h_kept, j + 1)
                    act.dma_start(bass.AP(h_table, j * (GROUP * P * FEAT), [[FEAT, P], [P * FEAT, GROUP], [1, FEAT]]),
                                  ln["h"][:, h, :].rearrange("p (t f) -> p t f", f=FEAT)).then_inc(h_stored[h], 16)

                with act.Fori(0, GROUPS // 2) as i:
                    for h in range(2):
                        root(nc, act, ln, eps_sb, 2 * i + h, h, var_ready, std_ready)
                        store_h(2 * i + h, h)
                for h in range(2):
                    act.wait_ge(h_stored[h], 16 * (GROUPS // 2))
                act.wait_ge(acc_zeroed, 16 * COPIES)

            @block.tensor
            def _(pe):
                pe.wait_ge(ident_ready, 1)
                pe.wait_ge(setup, 9)
                pe.wait_ge(w_in, 96)
                wr = wr_sb[:].rearrange("b (r q) o -> b q r o", q=2)
                nc.tensor.matmul(ps_a[:], wct_pad[:, 0, :], wr[:, 0, :, :], start=True, stop=False)
                nc.tensor.matmul(ps_a[:], wct_pad[:, 1, :], wr[:, 1, :, :], start=False, stop=True
                                 ).then_inc(wrel_ready, 1)
                nc.tensor.matmul(ps_b[:], ones_row[:], span_first[:, 0:512], start=True, stop=True)
                nc.tensor.matmul(ps_t[1][:, 0:SPANS - 512], ones_row[:], span_first[:, 512:SPANS],
                                 start=True, stop=True).then_inc(spans_bcast, 1)
                pe.wait_ge(setup, 12)
                pe.wait_ge(counted, GROUPS)
                nc.tensor.matmul(ps_b[:, 0:TILES], shift[:], upto[:, 1:], start=True, stop=False)
                nc.tensor.matmul(ps_b[:, 0:TILES], wrap[:], upto[:, 0:TILES], start=False, stop=True
                                 ).then_inc(before_ready, 1)


def group_first(group):
    group(0, 0, True)
    group(1, 1, True)


def from_block(t, n):
    return not isinstance(t, int) or t >= n


def scatter_loop(nc, records, h_table, placed, starts, accs, ident, ident_b, w1_sb, spare_row,
                 fours, limits):
    groups = TILES_PER_BLOCK // COPY_SET
    ROW = FEAT + 2
    with ExitStack() as ctx:
        def sb(name, shape, dt=F32):
            return ctx.enter_context(nc.sbuf_tensor(f"{name}_s", shape, dt))

        def ps(name):
            return ctx.enter_context(nc.psum_tensor(f"{name}_s", [P, BLOCK], F32))

        def sem(name):
            return ctx.enter_context(nc.semaphore(f"{name}_s"))

        rec = sb("rec", [P, 2, QUARTERS, PER_PART + 1, REC], I32)
        h_in = sb("h_in", [P, 2, PER_PART, QUARTERS * FEAT])
        goes_on = sb("goes_on", [P, 2, PER_PART, QUARTERS * FEAT], BF16)
        keep = sb("keep", [P, 2, BLOCK])
        running = sb("running", [P, 2, BLOCK])
        start_col = sb("start_col", [P, 1])
        start_int = sb("start_int", [QUARTERS, 1], I32)
        start_row = sb("start_row", [QUARTERS, FEAT])
        source = sb("source", [P, 2, TILES_PER_BLOCK])
        part_of = sb("part_of", [P, 2, TILES_PER_BLOCK], I32)
        source_b = sb("source_b", [P, 2, 2, TILES_PER_BLOCK], BF16)
        scaled = sb("scaled", [P, TILES_PER_BLOCK, 2])
        centre_int = sb("centre_int", [P, GRID], I32)
        centre = sb("centre", [P, GRID])
        rising = sb("rising", [P, 2 * TILES_PER_BLOCK, GRID])
        falling = sb("falling", [P, 2 * TILES_PER_BLOCK, GRID])
        tent = sb("tent", [P, 2, 2 * TILES_PER_BLOCK, GRID])
        spread = sb("spread", [P, 2, TILES_PER_BLOCK, GRID * FEAT])
        summed = sb("summed", [P, 2, TILES_PER_BLOCK, ROW])
        is_first = sb("is_first", [P, TILES_PER_BLOCK])
        moved = sb("moved", [P, TILES_PER_BLOCK])
        target = sb("target", [P, 2, TILES_PER_BLOCK], I32)
        spread_t = sb("spread_t", [P, 2, COPY_SET, P])
        scaled_w = sb("scaled_w", [P, 2, COPY_SET, GRID * FEAT])
        message = sb("message", [P, 2, COPY_SET, ROW])
        same = sb("same", [P, 2, COPY_SET, P])

        ps_keep, ps_place, ps_back = ps("ps_keep"), ps("ps_place"), ps("ps_back")
        ps_src, ps_t, ps_sum = ps("ps_src"), ps("ps_t"), ps("ps_sum")
        ps_z = [ps(f"ps_z{s}") for s in range(2)]

        rec_in = [sem(f"rec_in{h}") for h in range(2)]
        placed_in = [sem(f"placed_in{h}") for h in range(2)]
        added = [sem(f"added{s}") for s in range(2)]
        start_in, setup, prep_step, prepared = sem("start_in"), sem("setup"), sem("prep_step"), sem("prepared")
        keep_turned, keep_ready, placed_turned = sem("keep_turned"), sem("keep_ready"), sem("placed_turned")
        scanned, back_turned, spread_ready = sem("scanned"), sem("back_turned"), sem("spread_ready")
        src_ready, same_ready, turned, turned_copied = sem("src_ready"), sem("same_ready"), sem("turned"), sem("turned_copied")
        product, scaled_ready, message_ready = sem("product"), sem("scaled_ready"), sem("message_ready")
        set_summed, summed_ready = sem("set_summed"), sem("summed_ready")
        target_step, target_ready, pool_waited = sem("target_step"), sem("target_ready"), sem("pool_waited")
        PREP, TARGET = 7, 4

        def each_block(eng, work):
            for i in (0, 1):
                for h in range(2):
                    work(i, h)
            with eng.Fori(2, BLOCKS // 2 - 1) as i:
                for h in range(2):
                    work(i, h)
            for h in range(2):
                work(BLOCKS // 2 - 1, h)

        def has_next(t, n):
            return not isinstance(t, int) or t + n < BLOCKS

        with nc.Block() as block:

            @block.sync
            def _(sp):
                def load(t, h):
                    sp.dma_start(
                        rec[:, h, :, :, :].rearrange("p q e r -> p q (e r)"),
                        bass.AP(records, t * (BLOCK * REC),
                                [[PER_PART * REC, P], [QEDGES * REC, QUARTERS], [1, (PER_PART + 1) * REC]])
                    ).then_inc(rec_in[h], 16)
                    words = TILES_PER_BLOCK * FEAT
                    sp.dma_start(h_in[:, h, :, :].rearrange("p e c -> p (e c)"),
                                 bass.AP(placed, t * (P * words), [[words, P], [1, words]])).then_inc(placed_in[h], 16)

                def reload(i, h):
                    t = 2 * i + h
                    if has_next(t, 2):
                        sp.wait_ge(prepared, t + 1)
                        sp.wait_ge(placed_turned, t + 1)
                        load(t + 2, h)

                load(0, 0)
                load(1, 1)
                each_block(sp, reload)

            @block.gpsimd
            def _(pool):
                nc.gpsimd.iota(centre_int[:], pattern=[[1, GRID]], base=0, channel_multiplier=0).then_inc(setup, 1)
                with nc.allow_non_contiguous_dma("four words"):
                    pool.dma_start(start_int[:], bass.AP(records, REC + R_DST, [[QEDGES * REC, QUARTERS], [1, 1]])
                                   ).then_inc(start_in, 16)
                pool.wait_ge(start_in, 16)
                pool.indirect_dma_start(out=start_row[:], out_offset=None, in_=h_table.ap(),
                                        in_offset=bass.IndirectOffsetOnAxis(ap=start_int[:], axis=0)
                                        ).then_inc(start_in, 16)
                pool.wait_ge(start_in, 32)
                pool.dma_start(starts.ap(), start_row[:]).then_inc(start_in, 16)
                pool.wait_ge(start_in, 48)
                with nc.allow_non_contiguous_dma("128 words"):
                    pool.dma_start(start_col[:], bass.AP(starts, 0, [[1, P], [1, 1]])).then_inc(start_in, 16)

                def scatter(i, h):
                    t = 2 * i + h
                    pool.wait_ge(target_ready, t + 1)
                    for g in range(groups):
                        pool.wait_ge(summed_ready, groups * t + g + 1)
                        if g >= 2 or from_block(t, 1):
                            pool.wait_ge(added[g % 2], 16 * COPY_SET * (t * (groups // 2) + g // 2))
                        pool.sem_inc(pool_waited, 1)
                        for n in range(COPY_SET):
                            k = g * COPY_SET + n
                            pool.indirect_dma_start(
                                out=accs[(g % 2) * COPY_SET + n].ap(),
                                out_offset=bass.IndirectOffsetOnAxis(ap=target[:, h, k:k + 1], axis=0),
                                in_=summed[:, h, k, 0:FEAT], in_offset=None, compute_op=ALU.add
                            ).then_inc(added[g % 2], 16)

                each_block(pool, scatter)
                for s in range(2):
                    pool.wait_ge(added[s], 16 * COPY_SET * BLOCKS * (groups // 2))

            @block.vector
            def _(dve):
                dve.wait_ge(setup, 1)
                nc.vector.tensor_copy(centre[:], centre_int[:]).then_inc(setup, 1)
                for s in range(2):
                    nc.vector.tensor_copy(message[:, s, :, FEAT:], fours[:].unsqueeze(1).to_broadcast([P, COPY_SET, 2])
                                          ).then_inc(setup, 1)
                dve.wait_ge(setup, 4)

                def prepare_block(i, h):
                    t = 2 * i + h
                    b = t * PREP
                    dve.wait_ge(rec_in[h], 16 * i + 16)
                    r = rec[:, h, :, 1:, :].rearrange("p q e r -> p e q r")
                    before = rec[:, h, :, 0:PER_PART, :].rearrange("p q e r -> p e q r")
                    attr = r[:, :, :, R_ATTR:R_ATTR + 2].bitcast(F32)
                    wide = [P, 2 * TILES_PER_BLOCK, GRID]
                    per_feature = [P, PER_PART, QUARTERS, FEAT]

                    def quad(ap):
                        return ap.rearrange("p (e q) -> p e q", q=QUARTERS)

                    nc.vector.tensor_scalar(scaled[:].rearrange("p (e q) a -> p e q a", q=QUARTERS), attr,
                                            (GRID - 1) / 2, (GRID - 1) / 2, ALU.mult, ALU.add).then_inc(prep_step, 1)
                    nc.vector.tensor_scalar(quad(part_of[:, 0, :]), r[:, :, :, R_SRC], -P, None, ALU.bitwise_and)
                    nc.vector.tensor_scalar(quad(part_of[:, 1, :]), r[:, :, :, R_SRC], P - 1, None, ALU.bitwise_and
                                            ).then_inc(prep_step, 1)
                    dve.wait_ge(prep_step, b + 1)
                    nc.vector.tensor_tensor(rising[:], scaled[:].rearrange("p k a -> p (k a)").unsqueeze(2).to_broadcast(wide),
                                            centre[:].unsqueeze(1).to_broadcast(wide), ALU.subtract).then_inc(prep_step, 1)
                    nc.vector.tensor_copy(quad(source[:, h, :]), r[:, :, :, R_SRC])
                    dve.wait_ge(prep_step, b + 2)
                    if from_block(t, 2):
                        dve.wait_ge(src_ready, groups * (t - 1))
                    nc.vector.tensor_copy(source_b[:, h, :, :], part_of[:]).then_inc(prep_step, 1)
                    dve.wait_ge(prep_step, b + 3)
                    nc.vector.tensor_scalar(falling[:], rising[:], -1.0, 1.0, ALU.mult, ALU.add).then_inc(prep_step, 1)
                    if from_block(t, 2):
                        dve.wait_ge(keep_turned, t - 1)
                    nc.vector.tensor_tensor(
                        goes_on[:, h, :, :].rearrange("p e (q f) -> p e q f", q=QUARTERS),
                        r[:, :, :, R_DST].unsqueeze(3).to_broadcast(per_feature),
                        before[:, :, :, R_DST].unsqueeze(3).to_broadcast(per_feature), ALU.is_equal)
                    dve.wait_ge(prep_step, b + 5)
                    nc.vector.scalar_tensor_tensor(out=rising[:], in0=rising[:], scalar=1.0, in1=falling[:],
                                                   op0=ALU.add, op1=ALU.min).then_inc(prep_step, 1)
                    dve.wait_ge(prep_step, b + 6)
                    nc.vector.tensor_scalar(tent[:, h, :, :], rising[:], 0.0, None, ALU.max).then_inc(prep_step, 1)
                    dve.wait_ge(prep_step, b + 7)
                    dve.sem_inc(prepared, 1)

                def tent_of(h, a):
                    return tent[:, h, :, :].rearrange("p (k a) c -> p k a c", a=2)[:, :, a, :]

                def scan(t, h):
                    dve.wait_ge(keep_ready, t + 1)
                    dve.wait_ge(placed_turned, t + 1)
                    if from_block(t, 2):
                        dve.wait_ge(back_turned, t - 1)
                    if from_block(t, 1):
                        dve.wait_ge(scanned, t)
                        initial = running[:, 1 - h, BLOCK - 1:BLOCK]
                    else:
                        dve.wait_ge(start_in, 64)
                        initial = start_col[:]
                    nc.vector.tensor_tensor_scan(running[:, h, :], keep[:, h, :], ps_place[:], initial,
                                                 ALU.mult, ALU.add).then_inc(scanned, 1)

                def spread_rows(t, h):
                    dve.wait_ge(back_turned, t + 1)
                    if from_block(t, 2):
                        dve.wait_ge(turned, groups * (t - 1))
                    wide = [P, TILES_PER_BLOCK, GRID, FEAT]
                    nc.vector.tensor_tensor(
                        spread[:, h, :, :].rearrange("p k (v f) -> p k v f", f=FEAT),
                        ps_back[:].rearrange("p (k f) -> p k f", f=FEAT).unsqueeze(2).to_broadcast(wide),
                        tent_of(h, 1).unsqueeze(3).to_broadcast(wide), ALU.mult).then_inc(spread_ready, 1)

                def compare(t, h, g):
                    s, n = g % 2, groups * t + g
                    dve.wait_ge(src_ready, n + 1)
                    if g >= 2 or from_block(t, 1):
                        dve.wait_ge(set_summed, n - 1)
                    mine = source[:, h, g * COPY_SET:(g + 1) * COPY_SET]
                    nc.vector.tensor_tensor(same[:, s, :, :], ps_src[:].rearrange("p (n e) -> p n e", n=COPY_SET),
                                            mine.unsqueeze(2).to_broadcast([P, COPY_SET, P]), ALU.is_equal
                                            ).then_inc(same_ready, 1)

                def scale(t, h, g):
                    s, n = g % 2, groups * t + g
                    dve.wait_ge(product, n + 1)
                    wide = [P, COPY_SET, GRID, FEAT]
                    nc.vector.tensor_tensor(
                        scaled_w[:, s, :, :].rearrange("p n (u f) -> p n u f", f=FEAT),
                        ps_z[s][:].rearrange("p (n u f) -> p n u f", n=COPY_SET, f=FEAT),
                        tent_of(h, 0)[:, g * COPY_SET:(g + 1) * COPY_SET, :].unsqueeze(3).to_broadcast(wide),
                        ALU.mult).then_inc(scaled_ready, 1)
                    dve.wait_ge(scaled_ready, n + 1)
                    nc.vector.tensor_reduce(message[:, s, :, 0:FEAT],
                                            scaled_w[:, s, :, :].rearrange("p n (u f) -> p n f u", f=FEAT), AX, ALU.add
                                            ).then_inc(message_ready, 1)

                def find_moves(h):
                    nc.vector.tensor_scalar(moved[:], source[:, h, :], spare_row[:, 0:1], None, ALU.subtract
                                            ).then_inc(target_step, 1)

                def find_targets(t, h):
                    b = t * TARGET
                    dve.wait_ge(summed_ready, groups * (t + 1))
                    nc.vector.tensor_scalar(is_first[:], summed[:, h, :, FEAT], limits[:, 0:1], None, ALU.is_le
                                            ).then_inc(target_step, 1)
                    dve.wait_ge(target_step, b + 2)
                    nc.vector.scalar_tensor_tensor(out=is_first[:], in0=summed[:, h, :, FEAT + 1], scalar=limits[:, 1:2],
                                                   in1=is_first[:], op0=ALU.is_le, op1=ALU.mult).then_inc(target_step, 1)
                    dve.wait_ge(target_step, b + 3)
                    nc.vector.tensor_tensor(moved[:], moved[:], is_first[:], ALU.mult).then_inc(target_step, 1)
                    dve.wait_ge(target_step, b + 4)
                    if from_block(t, 2):
                        for s in range(2):
                            dve.wait_ge(added[s], 16 * COPY_SET * (groups // 2) * (t - 1))
                    nc.vector.tensor_scalar(target[:, h, :], moved[:], spare_row[:, 0:1], None, ALU.add
                                            ).then_inc(target_ready, 1)

                def block_work(i, h):
                    t = 2 * i + h
                    compare(t, h, 0)
                    if has_next(t, 1):
                        scan(t + 1, 1 - h)
                    compare(t, h, 1)
                    scale(t, h, 0)
                    if has_next(t, 1):
                        spread_rows(t + 1, 1 - h)
                    for g in range(2, groups):
                        compare(t, h, g)
                        scale(t, h, g - 1)
                    scale(t, h, groups - 1)
                    find_moves(h)
                    if has_next(t, 2):
                        prepare_block(i + 1, h)
                    find_targets(t, h)

                prepare_block(0, 0)
                prepare_block(0, 1)
                scan(0, 0)
                spread_rows(0, 0)
                each_block(dve, block_work)

            @block.tensor
            def _(pe):
                def lead(i, h):
                    t = 2 * i + h
                    pe.wait_ge(prepared, t + 1)
                    if from_block(t, 1):
                        pe.wait_ge(keep_ready, t)
                    for e in range(PER_PART):
                        mm = nc.tensor.matmul(ps_keep[:].rearrange("m (p e) -> m e p", e=PER_PART)[:, e, :],
                                              goes_on[:, h, e, :], ident_b[:], start=True, stop=True)
                    mm.then_inc(keep_turned, 1)
                    pe.wait_ge(placed_in[h], 16 * i + 16)
                    if from_block(t, 1):
                        pe.wait_ge(scanned, t)
                    for e in range(PER_PART):
                        mm = nc.tensor.matmul(ps_place[:].rearrange("m (p e) -> m e p", e=PER_PART)[:, e, :],
                                              h_in[:, h, e, :], ident[:], start=True, stop=True)
                    mm.then_inc(placed_turned, 1)

                def back(t, h):
                    pe.wait_ge(scanned, t + 1)
                    if from_block(t, 1):
                        pe.wait_ge(spread_ready, t)
                    for e in range(PER_PART):
                        mm = nc.tensor.transpose(ps_back[:, e * P:(e + 1) * P],
                                                 running[:, h, :].rearrange("m (p e) -> m e p", e=PER_PART)[:, e, :],
                                                 ident[:])
                    mm.then_inc(back_turned, 1)

                def turn(t, h, g):
                    s, n = g % 2, groups * t + g
                    if g >= 1 or from_block(t, 1):
                        pe.wait_ge(same_ready, n)
                    for m in range(COPY_SET):
                        k = g * COPY_SET + m
                        for part in range(2):
                            mm = nc.tensor.matmul(ps_src[:, m * P:(m + 1) * P],
                                                  source_b[:, h, part, k:k + 1].to_broadcast([P, P]), ident_b[:],
                                                  start=(part == 0), stop=(part == 1))
                    mm.then_inc(src_ready, 1)
                    pe.wait_ge(spread_ready, t + 1)
                    if g >= 1 or from_block(t, 1):
                        pe.wait_ge(turned_copied, n)
                    for m in range(COPY_SET):
                        mm = nc.tensor.transpose(ps_t[:, m * P:(m + 1) * P],
                                                 spread[:, h, g * COPY_SET + m, :], ident[:])
                    mm.then_inc(turned, 1)

                def multiply(t, g):
                    s, n = g % 2, groups * t + g
                    pe.wait_ge(turned_copied, n + 1)
                    if g >= 2 or from_block(t, 1):
                        pe.wait_ge(scaled_ready, n - 1)
                    for m in range(COPY_SET):
                        mm = nc.tensor.matmul(ps_z[s][:, m * P:(m + 1) * P], spread_t[:, s, m, :], w1_sb[:],
                                              start=True, stop=True)
                    mm.then_inc(product, 1)

                def add_up(t, g):
                    s, n = g % 2, groups * t + g
                    pe.wait_ge(message_ready, n + 1)
                    pe.wait_ge(same_ready, n + 1)
                    if g >= 1 or from_block(t, 1):
                        pe.wait_ge(summed_ready, n)
                    for m in range(COPY_SET):
                        mm = nc.tensor.matmul(ps_sum[:, m * ROW:(m + 1) * ROW],
                                              same[:, s, m, :], message[:, s, m, :], start=True, stop=True)
                    mm.then_inc(set_summed, 1)

                def block_work(i, h):
                    t = 2 * i + h
                    if has_next(t, 1):
                        lead(i + h, 1 - h)
                    for g in range(groups + 2):
                        if g < groups:
                            turn(t, h, g)
                        if 1 <= g <= groups:
                            multiply(t, g - 1)
                        if g == 1 and has_next(t, 1):
                            back(t + 1, 1 - h)
                        if g >= 2:
                            add_up(t, g - 2)

                pe.wait_ge(setup, 4)
                lead(0, 0)
                back(0, 0)
                each_block(pe, block_work)

            @block.scalar
            def _(act):
                def copy_keep(t, h):
                    act.wait_ge(keep_turned, t + 1)
                    if from_block(t, 2):
                        act.wait_ge(scanned, t - 1)
                    nc.scalar.copy(keep[:, h, :], ps_keep[:]).then_inc(keep_ready, 1)

                def copy_turned(t, g):
                    s, n = g % 2, groups * t + g
                    act.wait_ge(turned, n + 1)
                    if g >= 2 or from_block(t, 1):
                        act.wait_ge(product, n - 1)
                    nc.scalar.copy(spread_t[:, s, :, :].rearrange("p n e -> p (n e)"), ps_t[:]
                                   ).then_inc(turned_copied, 1)

                def copy_sums(t, h, g):
                    s, n = g % 2, groups * t + g
                    act.wait_ge(set_summed, n + 1)
                    if g == 0 and from_block(t, 2):
                        for half in range(2):
                            act.wait_ge(added[half], 16 * COPY_SET * (groups // 2) * (t - 1))
                    nc.scalar.copy(summed[:, h, g * COPY_SET:(g + 1) * COPY_SET, :].rearrange("p n c -> p (n c)"),
                                   ps_sum[:, 0:COPY_SET * ROW]).then_inc(summed_ready, 1)

                def copies(i, h):
                    t = 2 * i + h
                    if has_next(t, 1):
                        copy_keep(t + 1, 1 - h)
                    for g in range(groups + 2):
                        if g < groups:
                            copy_turned(t, g)
                        if g >= 2:
                            copy_sums(t, h, g - 2)

                copy_keep(0, 0)
                each_block(act, copies)


def edge_loop(nc, records, table, sums, ident, ident_b):
    with ExitStack() as ctx:
        def sb(name, shape, dt=F32):
            return ctx.enter_context(nc.sbuf_tensor(f"{name}_e", shape, dt))

        def ps(name):
            return ctx.enter_context(nc.psum_tensor(f"{name}_e", [P, BLOCK], F32))

        def sem(name):
            return ctx.enter_context(nc.semaphore(f"{name}_e"))

        rec = sb("rec", [P, 2, QUARTERS, PER_PART + 1, REC], I32)
        idx = sb("idx", [P, 2, TILES_PER_BLOCK], I32)
        goes_on = sb("goes_on", [P, 2, PER_PART, QUARTERS * FEAT], BF16)
        got = sb("got", [P, 2, TILES_PER_BLOCK, FEAT])
        weighed = sb("weighed", [P, 2, PER_PART, QUARTERS * FEAT])
        keep = sb("keep", [P, 2, BLOCK])
        running = sb("running", [P, 2, BLOCK])
        turned_sb = sb("turned_sb", [P, 2, TILES_PER_BLOCK * FEAT])

        ps_keep = [ps(f"ps_keep{h}") for h in range(2)]
        ps_msg = [ps(f"ps_msg{h}") for h in range(2)]
        ps_sum = [ps(f"ps_sum{h}") for h in range(2)]

        rec_in = [sem(f"rec_in{h}") for h in range(2)]
        gathered = [sem(f"gathered{h}") for h in range(2)]
        stored = [sem(f"stored{h}") for h in range(2)]
        prepared, weighed_ready = sem("prepared"), sem("weighed_ready")
        keep_turned, keep_ready, msg_ready = sem("keep_turned"), sem("keep_ready"), sem("msg_ready")
        scanned, sum_turned, sum_ready = sem("scanned"), sem("sum_turned"), sem("sum_ready")
        start = sem("start")
        pool_waited = sem("pool_waited")

        with nc.Block() as block:

            @block.sync
            def _(sp):
                def load(t, h):
                    sp.dma_start(
                        rec[:, h, :, :, :].rearrange("p q e r -> p q (e r)"),
                        bass.AP(records, t * (BLOCK * REC),
                                [[PER_PART * REC, P], [QEDGES * REC, QUARTERS], [1, (PER_PART + 1) * REC]])
                    ).then_inc(rec_in[h], 16)

                def store(t, h):
                    sp.wait_ge(sum_ready, t + 1)
                    words = TILES_PER_BLOCK * FEAT
                    sp.dma_start(bass.AP(sums, t * (P * words), [[words, P], [1, words]]), turned_sb[:, h, :]
                                 ).then_inc(stored[h], 16)

                load(0, 0)
                load(1, 1)
                with sp.Fori(0, BLOCKS // 2 - 1) as i:
                    for h in range(2):
                        t = 2 * i + h
                        sp.wait_ge(weighed_ready, t + 1)
                        load(t + 2, h)
                        store(t, h)
                for h in range(2):
                    store(BLOCKS - 2 + h, h)
                for h in range(2):
                    sp.wait_ge(stored[h], 16 * (BLOCKS // 2))

            @block.gpsimd
            def _(pool):
                def fetch(i, h, first):
                    t = 2 * i + h
                    pool.wait_ge(prepared, t + 1)
                    if not first:
                        pool.wait_ge(weighed_ready, t - 1)
                    pool.sem_inc(pool_waited, 1)
                    for k in range(TILES_PER_BLOCK):
                        pool.indirect_dma_start(
                            out=got[:, h, k, :], out_offset=None, in_=table.ap(),
                            in_offset=bass.IndirectOffsetOnAxis(ap=idx[:, h, k:k + 1], axis=0)
                        ).then_inc(gathered[h], 16)

                fetch(0, 0, True)
                fetch(0, 1, True)
                with pool.Fori(1, BLOCKS // 2) as i:
                    for h in range(2):
                        fetch(i, h, False)

            @block.vector
            def _(dve):
                nc.vector.memset(running[:, 1, BLOCK - 1:BLOCK], 0.0).then_inc(start, 1)
                dve.wait_ge(start, 1)

                def prepare_block(i, h, first):
                    t = 2 * i + h
                    dve.wait_ge(rec_in[h], 16 * i + 16)
                    r = rec[:, h, :, 1:, :].rearrange("p q e r -> p e q r")
                    before = rec[:, h, :, 0:PER_PART, :].rearrange("p q e r -> p e q r")

                    def quad(ap):
                        return ap.rearrange("p (e q) -> p e q", q=QUARTERS)

                    nc.vector.scalar_tensor_tensor(out=quad(idx[:, h, :]), in0=r[:, :, :, R_SRC], scalar=float(RELS),
                                                   in1=r[:, :, :, R_TYPE], op0=ALU.mult, op1=ALU.add)
                    if not first:
                        dve.wait_ge(keep_turned, t - 1)
                    wide = [P, PER_PART, QUARTERS, FEAT]
                    nc.vector.tensor_tensor(
                        goes_on[:, h, :, :].rearrange("p e (q f) -> p e q f", q=QUARTERS),
                        r[:, :, :, R_DST].unsqueeze(3).to_broadcast(wide),
                        before[:, :, :, R_DST].unsqueeze(3).to_broadcast(wide),
                        ALU.is_equal).then_inc(prepared, 1)

                def weigh(i, h):
                    t = 2 * i + h
                    dve.wait_ge(gathered[h], 16 * TILES_PER_BLOCK * (i + 1))
                    norm = rec[:, h, :, 1:, R_NORM].bitcast(F32).rearrange("p q e -> p e q")
                    nc.vector.tensor_tensor(
                        weighed[:, h, :, :].rearrange("p e (q f) -> p e q f", q=QUARTERS),
                        got[:, h, :, :].rearrange("p (e q) f -> p e q f", q=QUARTERS),
                        norm.unsqueeze(3).to_broadcast([P, PER_PART, QUARTERS, FEAT]),
                        ALU.mult).then_inc(weighed_ready, 1)

                def scan(i, h, first):
                    t = 2 * i + h
                    dve.wait_ge(keep_ready, t + 1)
                    dve.wait_ge(msg_ready, t + 1)
                    if not first:
                        dve.wait_ge(sum_turned, t - 1)
                    if not (first and h == 0):
                        dve.wait_ge(scanned, t)
                    nc.vector.tensor_tensor_scan(running[:, h, :], keep[:, h, :], ps_msg[h][:],
                                                 running[:, 1 - h, BLOCK - 1:BLOCK], ALU.mult, ALU.add
                                                 ).then_inc(scanned, 1)

                prepare_block(0, 0, True)
                prepare_block(0, 1, True)
                for h in range(2):
                    weigh(0, h)
                    prepare_block(1, h, False)
                    scan(0, h, True)
                with dve.Fori(1, BLOCKS // 2 - 1) as i:
                    for h in range(2):
                        weigh(i, h)
                        prepare_block(i + 1, h, False)
                        scan(i, h, False)
                for h in range(2):
                    weigh(BLOCKS // 2 - 1, h)
                    scan(BLOCKS // 2 - 1, h, False)

            @block.tensor
            def _(pe):
                def turn(i, h, first):
                    t = 2 * i + h
                    pe.wait_ge(prepared, t + 1)
                    if not first:
                        pe.wait_ge(keep_ready, t - 1)
                    for e in range(PER_PART):
                        mm = nc.tensor.matmul(ps_keep[h][:].rearrange("m (p e) -> m e p", e=PER_PART)[:, e, :],
                                              goes_on[:, h, e, :], ident_b[:],
                                              start=True, stop=True)
                    mm.then_inc(keep_turned, 1)
                    pe.wait_ge(weighed_ready, t + 1)
                    if not first:
                        pe.wait_ge(scanned, t - 1)
                    for e in range(PER_PART):
                        mm = nc.tensor.matmul(ps_msg[h][:].rearrange("m (p e) -> m e p", e=PER_PART)[:, e, :],
                                              weighed[:, h, e, :], ident[:], start=True, stop=True)
                    mm.then_inc(msg_ready, 1)
                    pe.wait_ge(scanned, t + 1)
                    if not first:
                        pe.wait_ge(sum_ready, t - 1)
                    for e in range(PER_PART):
                        mm = nc.tensor.transpose(ps_sum[h][:, e * P:(e + 1) * P],
                                                 running[:, h, :].rearrange("m (p e) -> m e p", e=PER_PART)[:, e, :],
                                                 ident[:])
                    mm.then_inc(sum_turned, 1)

                turn(0, 0, True)
                turn(0, 1, True)
                with pe.Fori(1, BLOCKS // 2) as i:
                    for h in range(2):
                        turn(i, h, False)

            @block.scalar
            def _(act):
                def copies(i, h, first):
                    t = 2 * i + h
                    act.wait_ge(keep_turned, t + 1)
                    if not first:
                        act.wait_ge(scanned, t - 1)
                    nc.scalar.copy(keep[:, h, :], ps_keep[h][:]).then_inc(keep_ready, 1)
                    act.wait_ge(sum_turned, t + 1)
                    if not first:
                        act.wait_ge(stored[h], 16 * i)
                    nc.scalar.copy(turned_sb[:, h, :], ps_sum[h][:]).then_inc(sum_ready, 1)

                copies(0, 0, True)
                copies(0, 1, True)
                with act.Fori(1, BLOCKS // 2) as i:
                    for h in range(2):
                        copies(i, h, False)


def update_nodes(nc, accs, table2, x_sb, ident, w2_sb, eps_sb):
    with ExitStack() as ctx:
        def sb(name, shape, dt=F32):
            return ctx.enter_context(nc.sbuf_tensor(f"{name}_u", shape, dt))

        def ps(name):
            return ctx.enter_context(nc.psum_tensor(f"{name}_u", [P, 512], F32))

        def sem(name):
            return ctx.enter_context(nc.semaphore(f"{name}_u"))

        parts = sb("parts", [P, 2, COPIES, GCOLS])
        total = sb("total", [P, GCOLS])
        ln = ln_buffers(sb)
        ht = sb("ht", [P, 2, 2, P])
        rows_sb = sb("rows_sb", [P, GROUP, TAB2_NODE])
        ps_t = [ps(f"ps_t{i}") for i in range(2)]
        ps_w = [ps(f"ps_w{i}") for i in range(W_BANKS)]
        parts_in = [sem(f"parts_in{h}") for h in range(2)]
        totalled, x_ready = sem("totalled"), sem("x_ready")
        ln_step, var_ready, std_ready, h_ready = sem("ln_step"), sem("var_ready"), sem("std_ready"), sem("h_ready")
        turned, ht_ready, product, evacuated = sem("turned"), sem("ht_ready"), sem("product"), sem("evacuated")
        stored = [sem(f"stored{k}") for k in range(GROUP)]

        with nc.Block() as block:

            @block.sync
            def _(sp):
                def load(i, h, first):
                    j = 2 * i + h
                    if not first:
                        sp.wait_ge(totalled, j - 1)
                    for n, acc in enumerate(accs):
                        sp.dma_start(parts[:, h, n, :].rearrange("p (t f) -> p t f", f=FEAT),
                                     bass.AP(acc, j * (GROUP * P * FEAT), [[FEAT, P], [P * FEAT, GROUP], [1, FEAT]])
                                     ).then_inc(parts_in[h], 16)

                load(0, 0, True)
                load(0, 1, True)
                with sp.Fori(1, GROUPS // 2) as i:
                    for h in range(2):
                        load(i, h, False)

            @block.vector
            def _(dve):
                def update(i, h, first):
                    j = 2 * i + h
                    xg = x_sb[:, bass.ds(j * GCOLS, GCOLS)]
                    dve.wait_ge(parts_in[h], 16 * COPIES * (i + 1))
                    nc.vector.tensor_reduce(total[:], parts[:, h, :, :].rearrange("p n c -> p c n"), AX, ALU.add
                                            ).then_inc(totalled, 1)
                    dve.wait_ge(totalled, j + 1)
                    nc.vector.tensor_tensor(xg, xg, total[:], ALU.add).then_inc(x_ready, 1)
                    dve.wait_ge(x_ready, j + 1)
                    if not first:
                        dve.wait_ge(turned, j - 1)
                    ln_group(nc, dve, ln, xg, j, h, ln_step, var_ready, std_ready, h_ready)

                update(0, 0, True)
                update(0, 1, True)
                with dve.Fori(1, GROUPS // 2) as i:
                    for h in range(2):
                        update(i, h, False)

            @block.tensor
            def _(pe):
                def group(j, h, first):
                    turn_and_multiply(nc, pe, ln, ps_t, ps_w, ht, w2_sb, ident, j, h, first,
                                      h_ready, turned, ht_ready, product, evacuated)

                group_first(group)
                with pe.Fori(1, GROUPS // 2) as i:
                    for h in range(2):
                        group(2 * i + h, h, False)

            @block.scalar
            def _(act):
                def group(j, h, first, more=True):
                    table_rows(nc, act, ln, ps_t, ps_w, ht, rows_sb, eps_sb, table2, j, h, first, more,
                               var_ready, std_ready, turned, ht_ready, product, evacuated, stored)

                root(nc, act, ln, eps_sb, 0, 0, var_ready, std_ready)
                group_first(group)
                with act.Fori(1, GROUPS // 2 - 1) as i:
                    for h in range(2):
                        group(2 * i + h, h, False)
                group(GROUPS - 2, 0, False)
                group(GROUPS - 1, 1, False, more=False)
                for k in range(GROUP):
                    act.wait_ge(stored[k], 16 * GROUPS)


def node_loop(nc, records, sums, x_sb, last_edge, local_id, group_base, carry_id, out):
    with ExitStack() as ctx:
        def sb(name, shape, dt=F32):
            return ctx.enter_context(nc.sbuf_tensor(f"{name}_n", shape, dt))

        def ps(name):
            return ctx.enter_context(nc.psum_tensor(f"{name}_n", [P, 512], F32))

        def sem(name):
            return ctx.enter_context(nc.semaphore(f"{name}_n"))

        K = QUARTERS - 1
        ends_dst = sb("ends_dst", [K, 2, REC], I32)
        ends_sum = sb("ends_sum", [K, FEAT])
        same = sb("same", [K, 1])
        cut_id = sb("cut_id", [K, 1])
        idx = sb("idx", [P, 2, GROUP], I32)
        picked = sb("picked", [P, 2, GROUP, FEAT])
        owner = sb("owner", [K, 2, GROUP * P])
        new_x = sb("new_x", [P, 2, GCOLS])
        ps_carry = [ps(f"ps_carry{h}") for h in range(2)]

        ends_in, ends_step = sem("ends_in"), sem("ends_step")
        idx_ready, owner_ready, carry_ready = sem("idx_ready"), sem("owner_ready"), sem("carry_ready")
        picked_in = [sem(f"picked_in{h}") for h in range(2)]
        carried, x_ready = sem("carried"), sem("x_ready")
        pool_waited = sem("pool_waited")
        out_stored = [sem(f"out_stored{h}") for h in range(2)]

        with nc.Block() as block:

            @block.sync
            def _(sp):
                sp.dma_start(ends_dst[:].rearrange("k a r -> k (a r)"),
                             bass.AP(records, QEDGES * REC, [[QEDGES * REC, K], [1, 2 * REC]])).then_inc(ends_in, 16)
                sp.dma_start(ends_sum[:], bass.AP(sums, QUARTERS * (QEDGES - 1) * FEAT, [[FEAT, K], [1, FEAT]])
                             ).then_inc(ends_in, 16)
                def store(i, h, tiles):
                    j = 2 * i + h
                    sp.wait_ge(x_ready, j + 1)
                    sp.dma_start(
                        bass.AP(out.tensor, j * (GROUP * P * FEAT), [[FEAT, P], [P * FEAT, tiles], [1, FEAT]]),
                        new_x[:, h, 0:tiles * FEAT].rearrange("p (t f) -> p t f", f=FEAT)
                    ).then_inc(out_stored[h], 16)

                with sp.Fori(0, GROUPS // 2 - 1) as i:
                    for h in range(2):
                        store(i, h, GROUP)
                store(GROUPS // 2 - 1, 0, GROUP)
                store(GROUPS // 2 - 1, 1, GROUP - 1)
                sp.dma_start(out[(TILES - 1) * P:NODES, :],
                             new_x[0:LAST_ROWS, 1, (GROUP - 1) * FEAT:]).then_inc(out_stored[1], 16)
                sp.wait_ge(out_stored[0], 16 * (GROUPS // 2))
                sp.wait_ge(out_stored[1], 16 * (GROUPS // 2) + 16)

            @block.gpsimd
            def _(pool):
                def fetch(i, h, first):
                    j = 2 * i + h
                    pool.wait_ge(idx_ready, j + 1)
                    if not first:
                        pool.wait_ge(x_ready, j - 1)
                    pool.sem_inc(pool_waited, 1)
                    for k in range(GROUP):
                        pool.indirect_dma_start(
                            out=picked[:, h, k, :], out_offset=None, in_=sums.ap(),
                            in_offset=bass.IndirectOffsetOnAxis(ap=idx[:, h, k:k + 1], axis=0)
                        ).then_inc(picked_in[h], 16)

                fetch(0, 0, True)
                fetch(0, 1, True)
                with pool.Fori(1, GROUPS // 2) as i:
                    for h in range(2):
                        fetch(i, h, False)

            @block.vector
            def _(dve):
                def indices(i, h):
                    nc.vector.tensor_copy(idx[:, h, :], last_edge[:, bass.ds((2 * i + h) * GROUP, GROUP)]
                                          ).then_inc(idx_ready, 1)

                def owners(i, h, first):
                    j = 2 * i + h
                    if not first:
                        dve.wait_ge(carry_ready, j - 1)
                    nc.vector.tensor_scalar(owner[:, h, :], local_id[:], carry_id[:, bass.ds(j, 1)], None,
                                            ALU.is_equal).then_inc(owner_ready, 1)

                def add(i, h, first):
                    j = 2 * i + h
                    xg = x_sb[:, bass.ds(j * GCOLS, GCOLS)]
                    dve.wait_ge(carry_ready, j + 1)
                    if not first:
                        dve.wait_ge(out_stored[h], 16 * i)
                    nc.vector.tensor_tensor(new_x[:, h, :], xg, ps_carry[h][:, 0:GCOLS], ALU.add).then_inc(carried, 1)
                    dve.wait_ge(carried, j + 1)
                    dve.wait_ge(picked_in[h], 16 * GROUP * (i + 1))
                    nc.vector.tensor_tensor(new_x[:, h, :], new_x[:, h, :],
                                            picked[:, h, :, :].rearrange("p t f -> p (t f)"),
                                            ALU.add).then_inc(x_ready, 1)

                indices(0, 0)
                indices(0, 1)
                dve.wait_ge(ends_in, 32)
                nc.vector.tensor_tensor(same[:], ends_dst[:, 0, R_DST:R_DST + 1], ends_dst[:, 1, R_DST:R_DST + 1],
                                        ALU.is_equal).then_inc(ends_step, 1)
                dve.wait_ge(ends_step, 1)
                nc.vector.scalar_tensor_tensor(out=cut_id[:], in0=ends_dst[:, 0, R_DST:R_DST + 1], scalar=1.0,
                                               in1=same[:], op0=ALU.add, op1=ALU.mult).then_inc(ends_step, 1)
                dve.wait_ge(ends_step, 2)
                nc.vector.tensor_scalar(cut_id[:], cut_id[:], -1.0, None, ALU.add).then_inc(ends_step, 1)
                dve.wait_ge(ends_step, 3)
                nc.vector.tensor_scalar(carry_id[:], group_base[:], cut_id[:, 0:1], None, ALU.add
                                        ).then_inc(ends_step, 1)
                dve.wait_ge(ends_step, 4)
                owners(0, 0, True)
                owners(0, 1, True)
                for h in range(2):
                    add(0, h, True)
                    indices(1, h)
                    owners(1, h, False)
                with dve.Fori(1, GROUPS // 2 - 1) as i:
                    for h in range(2):
                        add(i, h, False)
                        indices(i + 1, h)
                        owners(i + 1, h, False)
                for h in range(2):
                    add(GROUPS // 2 - 1, h, False)

            @block.tensor
            def _(pe):
                pe.wait_ge(ends_in, 32)

                def carry(j, h, first):
                    pe.wait_ge(owner_ready, j + 1)
                    if not first:
                        pe.wait_ge(carried, j - 1)
                    for k in range(GROUP):
                        mm = nc.tensor.matmul(ps_carry[h][:, k * FEAT:(k + 1) * FEAT],
                                              owner[:, h, k * P:(k + 1) * P], ends_sum[:], start=True, stop=True)
                    mm.then_inc(carry_ready, 1)

                carry(0, 0, True)
                carry(1, 1, True)
                with pe.Fori(1, GROUPS // 2) as i:
                    for h in range(2):
                        carry(2 * i + h, h, False)


_INS = ["x", "src", "dst", "edge_attr_2", "edge_type_16", "edge_weight1", "L0_gnn_weight", "L1_gnn_weight",
        "L1_gnn_w_comp"]


def kernel(**inputs):
    import concourse.bacc as _bacc
    from concourse.bass_utils import run_bass_kernel_spmd as _run

    nc = _bacc.Bacc("TRN2", target_bir_lowering=False, num_devices=1)
    arrays, args = {}, []
    for name in _INS:
        a = np.ascontiguousarray(inputs[name])
        arrays[f"in_{name}"] = a
        args.append(nc.dram_tensor(f"in_{name}", a.shape, mybir.dt.from_np(a.dtype), kind="ExternalInput").ap())
    out = nc.dram_tensor("out", (NODES, FEAT), F32, kind="ExternalOutput").ap()
    gnn_kernel(nc, *args, out)
    r = _run(nc, [arrays], core_ids=[0])
    return r.results[0]["out"]
```

```python
from contextlib import ExitStack

import numpy as np

import concourse.bass as bass
from concourse import mybir

ALU = mybir.AluOpType
ACT = mybir.ActivationFunctionType
AX = mybir.AxisListType.X
F32 = mybir.dt.float32
I32 = mybir.dt.int32
BF16 = mybir.dt.bfloat16

P = 128
FEAT = 32
NODES = 12500
EDGES = 412500
RELS = 16
BASES = 8
GRID = 4
EPS = 1e-5

TILES = -(-NODES // P)
LAST_ROWS = NODES - (TILES - 1) * P
GROUP = 7
GROUPS = TILES // GROUP
GCOLS = GROUP * FEAT
assert GROUPS * GROUP == TILES and GROUPS % 2 == 0

QUARTERS = 4
PER_PART = 4
BLOCK = P * PER_PART
TILES_PER_BLOCK = QUARTERS * PER_PART
BLOCKS = 2 * -(-EDGES // (2 * QUARTERS * BLOCK))
QEDGES = BLOCKS * BLOCK
PADDED = QUARTERS * QEDGES
assert PADDED >= EDGES

REC = 8
R_DST, R_SRC, R_TYPE, R_ATTR, R_NORM = 0, 1, 2, 3, 5

STAGE_CHUNKS = 14
STAGE_COLS = EDGES // P // STAGE_CHUNKS
STAGED = P * STAGE_CHUNKS * STAGE_COLS
TAIL_COLS = (PADDED - STAGED) // P
TAIL_ROWS, TAIL_REST = divmod(EDGES - STAGED, TAIL_COLS)
assert TAIL_COLS * P + STAGED == PADDED and STAGE_CHUNKS == GROUPS

ORDER_PARTS = 125
ORDER_COLS = EDGES // ORDER_PARTS
assert ORDER_COLS * ORDER_PARTS == EDGES

SPAN = 132
PART_SPANS = ORDER_COLS // SPAN
assert PART_SPANS * SPAN == ORDER_COLS

NODE_ROWS = TILES * P
ACC_WORDS = (NODE_ROWS + P) // P * FEAT
ZERO_STORES = 128
ZERO_WORDS = PADDED * FEAT // P // ZERO_STORES
GROUP_STORES = ZERO_STORES // GROUPS
ACC_PARTS = 4
PART_WORDS = ACC_WORDS // ACC_PARTS
assert ZERO_WORDS * ZERO_STORES * P == PADDED * FEAT
assert PART_WORDS * ACC_PARTS == ACC_WORDS and ZERO_WORDS >= PART_WORDS
COPIES = 8
COPY_SET = 4
ADD_SET = 2
ADD_SETS = COPIES // ADD_SET
ADD_ROUNDS = TILES_PER_BLOCK // COPIES
TAB2_NODE = RELS * FEAT
W_COLS = GRID * GRID * FEAT
W_BANKS = 4
T_BANKS = -(-GROUP // 2)


def gnn_kernel(nc, x, src, dst, edge_attr, edge_type, edge_weight, w_basis, w_rel, w_comp, out):
    records = nc.dram_tensor("records", [PADDED + 1, REC], I32)
    h_table = nc.dram_tensor("h_table", [NODE_ROWS, FEAT], F32)
    placed = nc.dram_tensor("placed", [PADDED + NODE_ROWS, FEAT], F32)
    starts = nc.dram_tensor("starts", [QUARTERS, FEAT], F32)
    accs = [nc.dram_tensor(f"acc{n}", [NODE_ROWS + P, FEAT], F32) for n in range(COPIES)]
    table2 = nc.dram_tensor("table2", [TILES * P * RELS, FEAT], F32)
    sums = nc.dram_tensor("sums", [PADDED + 1, FEAT], F32)

    with ExitStack() as ctx:
        def sb(name, shape, dt=F32):
            return ctx.enter_context(nc.sbuf_tensor(name, shape, dt))

        def sem(name):
            return ctx.enter_context(nc.semaphore(name))

        x_sb = sb("x_sb", [P, TILES * FEAT])
        ident = sb("ident", [P, P])
        w1_sb = sb("w1_sb", [P, GRID * FEAT])
        spare_row = sb("spare_row", [P, 1])
        ident_b = sb("ident_b", [P, P], BF16)
        in_order = sb("in_order", [1, 1], I32)
        lower = sb("lower", [P, P])
        fours = sb("fours", [P, 2])
        limits = sb("limits", [P, 2])
        w2_sb = sb("w2_sb", [P, W_COLS])
        node_id = sb("node_id", [P, TILES])
        last_edge = sb("last_edge", [P, TILES], I32)
        local_id = sb("local_id", [QUARTERS - 1, GROUP * P])
        group_base = sb("group_base", [QUARTERS - 1, GROUPS])
        carry_id = sb("carry_id", [QUARTERS - 1, GROUPS])
        eps_sb = sb("eps_sb", [P, 1])

        prepare(nc, x, src, dst, edge_attr, edge_type, edge_weight, w_basis, w_rel, w_comp,
                records, sums, accs, x_sb, ident, w1_sb, w2_sb, node_id, last_edge, local_id,
                group_base, eps_sb, spare_row, ident_b, in_order, lower, fours, limits,
                h_table, placed)
        ordered_scatter_loop(nc, in_order, records, h_table, placed, starts, accs, ident, ident_b, w1_sb,
                             spare_row, fours, limits)
        any_order_loop(nc, 1, in_order, records, h_table, accs, ident, w1_sb, spare_row, lower)
        update_nodes(nc, accs, table2, x_sb, ident_b, w2_sb, eps_sb)
        ordered_edge_loop(nc, in_order, records, table2, sums, ident, ident_b)
        any_order_loop(nc, 2, in_order, records, table2, accs, ident, w1_sb, spare_row, lower)
        ordered_finish(nc, in_order, records, sums, x_sb, last_edge, local_id, group_base, carry_id, out)
        any_order_finish(nc, in_order, accs, x, x_sb, out)


def ln_buffers(sb):
    return dict(total=sb("ln_total", [P, GROUP]), cent=sb("ln_cent", [P, GROUP, FEAT]),
                square=sb("ln_square", [P, GROUP, FEAT]), var=sb("ln_var", [P, 2, GROUP]),
                std=sb("ln_std", [P, 2, GROUP]), rstd=sb("ln_rstd", [P, GROUP]),
                h=sb("ln_h", [P, 2, GCOLS]))


LN_STEPS = 5


def ln_group(nc, dve, ln, xg, j, h, ln_step, var_ready, std_ready, h_ready):
    b = j * LN_STEPS
    dve.sem_inc(ln_step, 1)
    xg3 = xg.rearrange("p (t f) -> p t f", f=FEAT)
    nc.vector.tensor_reduce(ln["total"][:], xg3, AX, ALU.add).then_inc(ln_step, 1)
    dve.wait_ge(ln_step, b + 2)
    nc.vector.scalar_tensor_tensor(
        out=ln["cent"][:], in0=ln["total"][:].unsqueeze(2).to_broadcast([P, GROUP, FEAT]),
        scalar=-1.0 / FEAT, in1=xg3, op0=ALU.mult, op1=ALU.add).then_inc(ln_step, 1)
    dve.wait_ge(ln_step, b + 3)
    nc.vector.tensor_tensor(ln["square"][:], ln["cent"][:], ln["cent"][:], ALU.mult).then_inc(ln_step, 1)
    dve.wait_ge(ln_step, b + 4)
    nc.vector.tensor_reduce(ln["var"][:, h, :], ln["square"][:], AX, ALU.add).then_inc(var_ready, 1)
    dve.wait_ge(std_ready, j + 1)
    nc.vector.reciprocal(ln["rstd"][:], ln["std"][:, h, :]).then_inc(ln_step, 1)
    dve.wait_ge(ln_step, b + 5)
    nc.vector.scalar_tensor_tensor(
        out=ln["h"][:, h, :].rearrange("p (t f) -> p t f", f=FEAT), in0=ln["cent"][:], scalar=0.0,
        in1=ln["rstd"][:].unsqueeze(2).to_broadcast([P, GROUP, FEAT]),
        op0=ALU.max, op1=ALU.mult).then_inc(h_ready, 1)
    dve.wait_ge(h_ready, j + 1)


def place_of(k, a):
    first = (k % 2 * 2 + a) * P
    return k // 2, slice(first, first + P)


def turn_and_multiply(nc, pe, pieces, ps_t, ps_w, ht, w_pieces, ident_b, j, h, first,
                      split_ready, turned, ht_ready, product, evacuated):
    pe.wait_ge(split_ready, j + 1)
    if not first or j > 0:
        pe.wait_ge(ht_ready, j)
    for k in range(GROUP):
        for a in range(2):
            bank, cols = place_of(k, a)
            mm = nc.tensor.matmul(ps_t[bank][:, cols], pieces[:, h, k, a, :], ident_b[:], start=True, stop=True)
    mm.then_inc(turned, 1)
    pe.wait_ge(ht_ready, j + 1)
    for k in range(GROUP):
        if not first or j * GROUP + k >= W_BANKS:
            pe.wait_ge(evacuated, j * GROUP + k - (W_BANKS - 2))
        for a in range(2):
            bank, cols = place_of(k, a)
            mm = nc.tensor.matmul(ps_w[k % W_BANKS][:], ht[:, h, bank, cols], w_pieces[:, a, :],
                                  start=(a == 0), stop=(a == 1))
        mm.then_inc(product, 1)


def root(nc, act, ln, eps_sb, j, h, var_ready, std_ready):
    act.wait_ge(var_ready, j + 1)
    nc.scalar.activation(ln["std"][:, h, :], ln["var"][:, h, :], ACT.Sqrt, bias=eps_sb[:],
                         scale=1.0 / FEAT).then_inc(std_ready, 1)


def table_rows(nc, act, ln, ps_t, ps_w, ht, rows_sb, eps_sb, j, h, first, more,
               var_ready, std_ready, turned, ht_ready, product, evacuated, stored):
    act.wait_ge(turned, j + 1)
    if not first:
        act.wait_ge(product, (j - 1) * GROUP)
    for bank in range(T_BANKS):
        used = min(4 * P, (2 * GROUP - 4 * bank) * P)
        last = nc.scalar.copy(ht[:, h, bank, 0:used], ps_t[bank][:, 0:used])
    last.then_inc(ht_ready, 1)
    if more:
        root(nc, act, ln, eps_sb, j + 1, 1 - h, var_ready, std_ready)
    for k in range(GROUP):
        act.wait_ge(product, j * GROUP + k + 1)
        if not first or j > 0:
            act.wait_ge(stored[k], 16 * j)
        nc.scalar.copy(rows_sb[:, k, :], ps_w[k % W_BANKS][:]).then_inc(evacuated, 1)


def prepare(nc, x, src, dst, edge_attr, edge_type, edge_weight, w_basis, w_rel, w_comp,
            records, sums, accs, x_sb, ident, w1_sb, w2_sb, node_id, last_edge, local_id,
            group_base, eps_sb, spare_row, ident_b, in_order, lower, fours, limits,
                h_table, placed):
    with ExitStack() as ctx:
        def sb(name, shape, dt=F32):
            return ctx.enter_context(nc.sbuf_tensor(name, shape, dt))

        def ps(name, shape=(P, 512)):
            return ctx.enter_context(nc.psum_tensor(name, list(shape), F32))

        sems = []

        def sem(name):
            sems.append(nc.alloc_semaphore(name))
            return sems[-1]

        ln = ln_buffers(sb)
        zero_rows = sb("zero_rows", [P, ZERO_WORDS])
        spare_int = sb("spare_int", [P, 1], I32)
        raw_dst = sb("raw_dst", [P, 2, STAGE_COLS], I32)
        raw_src = sb("raw_src", [P, 2, STAGE_COLS], I32)
        raw_type = sb("raw_type", [P, 2, STAGE_COLS], I32)
        raw_attr = sb("raw_attr", [P, 2, 2 * STAGE_COLS])
        raw_norm = sb("raw_norm", [P, 2, STAGE_COLS])
        rec = sb("rec", [P, 2, STAGE_COLS, REC], I32)
        t_dst = sb("t_dst", [P, TAIL_COLS], I32)
        t_src = sb("t_src", [P, TAIL_COLS], I32)
        t_type = sb("t_type", [P, TAIL_COLS], I32)
        t_attr = sb("t_attr", [P, 2 * TAIL_COLS])
        t_norm = sb("t_norm", [P, TAIL_COLS])
        t_rec = sb("t_rec", [P, TAIL_COLS, REC], I32)
        lead = sb("lead", [1, REC], I32)
        zeros = sb("zeros", [1, FEAT])
        first_lo = sb("first_lo", [P, PART_SPANS], I32)
        first_hi = sb("first_hi", [P, PART_SPANS], I32)
        column = sb("column", [P, P], I32)
        tile_base = sb("tile_base", [P, TILES], I32)
        not_past = sb("not_past", [P, PART_SPANS, P], BF16)
        in_tile = sb("in_tile", [P, PART_SPANS, TILES], BF16)
        in_lower = sb("in_lower", [P, PART_SPANS, TILES], BF16)
        ones_b = sb("ones_b", [P, P], BF16)
        id_int = sb("id_int", [P, TILES], I32)
        local_int = sb("local_int", [QUARTERS - 1, GROUP * P], I32)
        base_int = sb("base_int", [QUARTERS - 1, GROUPS], I32)
        ids = sb("ids", [P, 2, GROUP])
        hits = sb("hits", [P, SPAN])
        span_no = sb("span_no", [P, TILES])
        span_base = sb("span_base", [P, TILES])
        span_idx = sb("span_idx", [P, 2, GROUP], I32)
        span_dst = sb("span_dst", [P, 2, GROUP, SPAN], I32)
        inside = sb("inside", [P, 2, GROUP])
        upto = sb("upto", [P, 1 + TILES])
        shift = sb("shift", [P, P])
        wrap = sb("wrap", [P, P])
        has = sb("has", [P, TILES])
        edge = sb("edge", [P, 2, TILES])
        quarter = sb("quarter", [P, 2, TILES])
        row = sb("row", [P, 2, TILES])
        spare = sb("spare", [P, 2, TILES])
        first_row = sb("first_row", [P, TILES], I32)
        h_all = sb("h_all", [P, TILES * FEAT])
        place_row = sb("place_row", [P, 2, GROUP], I32)
        place_h = sb("place_h", [P, 2, GROUP, FEAT])
        dst_all = sb("dst_all", [P, ORDER_COLS + 1], I32)
        falls = sb("falls", [P, ORDER_COLS])
        n_falls = sb("n_falls", [P, 1])
        ones = sb("ones", [P, P])
        ordered = sb("ordered", [P, 1])
        wr_sb = sb("wr_sb", [BASES, 2 * RELS, FEAT])
        wct = sb("wct", [BASES, RELS])
        wct_pad = sb("wct_pad", [BASES, 2, P])

        ps_spans, ps_a, ps_b = ps("ps_spans"), ps("ps_a"), ps("ps_b")

        x_pad, x_in, w_in = sem("x_pad"), sem("x_in"), sem("w_in")
        raw_in = [sem(f"raw_in{i}") for i in range(2)]
        rec_out = [sem(f"rec_out{i}") for i in range(2)]
        rec_zero, rec_made = sem("rec_zero"), sem("rec_made")
        tail_zero, tail_in, tail_made, tail_out = sem("tail_zero"), sem("tail_in"), sem("tail_made"), sem("tail_out")
        const_step, ident_ready = sem("const_step"), sem("ident_ready")
        ln_step, var_ready, std_ready, h_ready = sem("ln_step"), sem("var_ready"), sem("std_ready"), sem("h_ready")
        h_stored = sem("h_stored")
        zero_ready, acc_zeroed = sem("zero_ready"), sem("acc_zeroed")
        spans_marked, spans_counted = sem("spans_marked"), sem("spans_counted")
        wrel_ready, setup, search = sem("wrel_ready"), sem("setup"), sem("search")
        idx_ready, span_used = sem("idx_ready"), sem("span_used")
        span_got = [sem(f"span_got{i}") for i in range(2)]
        before_ready = sem("before_ready")
        pool_waited = sem("pool_waited")
        inside_step = sem("inside_step")
        counted = sem("counted")
        order_set, order_in, order_step, order_ready = sem("order_set"), sem("order_in"), sem("order_step"), sem("order_ready")
        h_kept, place_zeroed, place_ready = sem("h_kept"), sem("place_zeroed"), sem("place_ready")
        placed_out = [sem(f"placed_out{h}") for h in range(2)]

        raw = [(raw_dst, dst, 1), (raw_src, src, 1), (raw_type, edge_type, 1),
               (raw_attr, edge_attr, 2), (raw_norm, edge_weight, 1)]
        tail = [(t_dst, dst, 1), (t_src, src, 1), (t_type, edge_type, 1), (t_attr, edge_attr, 2),
                (t_norm, edge_weight, 1)]

        with nc.Block() as block:

            @block.sync
            def _(sp):
                sp.wait_ge(order_set, 1)
                sp.dma_start(dst_all[0:ORDER_PARTS - 1, :],
                             bass.AP(dst.tensor, 0, [[ORDER_COLS, ORDER_PARTS - 1], [1, ORDER_COLS + 1]])
                             ).then_inc(order_in, 16)
                sp.dma_start(dst_all[ORDER_PARTS - 1:ORDER_PARTS, 0:ORDER_COLS],
                             bass.AP(dst.tensor, (ORDER_PARTS - 1) * ORDER_COLS, [[ORDER_COLS, 1], [1, ORDER_COLS]])
                             ).then_inc(order_in, 16)
                whole = (TILES - 1) * P
                sp.wait_ge(x_pad, 1)
                sp.dma_start(x_sb[:, 0:(TILES - 1) * FEAT].rearrange("p (t f) -> p t f", f=FEAT),
                             x[0:whole, :].rearrange("(t p) f -> p t f", p=P)).then_inc(x_in, 16)
                sp.dma_start(x_sb[0:LAST_ROWS, (TILES - 1) * FEAT:], x[whole:NODES, :]).then_inc(x_in, 16)
                for v in range(GRID):
                    sp.dma_start(w1_sb[FEAT * v:FEAT * v + FEAT, :].rearrange("i (u o) -> i u o", o=FEAT),
                                 w_basis[:, v, :, :].rearrange("u i o -> i u o")).then_inc(w_in, 16)
                sp.dma_start(wr_sb[:], bass.AP(w_rel.tensor, 0, [[FEAT, BASES], [BASES * FEAT, 2 * RELS], [1, FEAT]])
                             ).then_inc(w_in, 16)
                with nc.allow_non_contiguous_dma("128 words"):
                    sp.dma_start(wct[:], w_comp.rearrange("r b -> b r")).then_inc(w_in, 16)

                def load(c, h):
                    for tile, array, width in raw:
                        n = width * STAGE_COLS
                        sp.dma_start(tile[:, h, :], bass.AP(array.tensor, c * n, [[n * STAGE_CHUNKS, P], [1, n]])
                                     ).then_inc(raw_in[h], 16)

                def store(c, h):
                    sp.wait_ge(rec_made, c + 1)
                    n = REC * STAGE_COLS
                    sp.dma_start(bass.AP(records, REC + c * n, [[n * STAGE_CHUNKS, P], [1, n]]),
                                 rec[:, h, :, :].rearrange("p e r -> p (e r)")).then_inc(rec_out[h], 16)

                load(0, 0)
                load(1, 1)
                sp.wait_ge(tail_zero, 5)
                for tile, array, width in tail:
                    n = width * TAIL_COLS
                    sp.dma_start(tile[0:TAIL_ROWS, :], bass.AP(array.tensor, width * STAGED, [[n, TAIL_ROWS], [1, n]])
                                 ).then_inc(tail_in, 16)
                    sp.dma_start(tile[TAIL_ROWS:TAIL_ROWS + 1, 0:width * TAIL_REST],
                                 bass.AP(array.tensor, width * STAGED + TAIL_ROWS * n, [[n, 1], [1, width * TAIL_REST]])
                                 ).then_inc(tail_in, 16)
                with sp.Fori(0, STAGE_CHUNKS // 2 - 1) as i:
                    for h in range(2):
                        store(2 * i + h, h)
                        load(2 * i + h + 2, h)
                for h in range(2):
                    store(STAGE_CHUNKS - 2 + h, h)

                sp.wait_ge(h_kept, GROUPS)
                sp.dma_start(bass.AP(h_table, 0, [[FEAT, P], [P * FEAT, TILES], [1, FEAT]]),
                             h_all[:].rearrange("p (t f) -> p t f", f=FEAT)).then_inc(h_stored, 16)
                sp.wait_ge(tail_made, 8)
                sp.dma_start(bass.AP(records, REC * (STAGED + 1), [[REC * TAIL_COLS, P], [1, REC * TAIL_COLS]]),
                             t_rec[:, :, :].rearrange("p e r -> p (e r)")).then_inc(tail_out, 16)
                sp.dma_start(bass.AP(records, 0, [[REC, 1], [1, REC]]), lead[:]).then_inc(tail_out, 16)
                sp.dma_start(bass.AP(sums, PADDED * FEAT, [[FEAT, 1], [1, FEAT]]), zeros[:]).then_inc(tail_out, 16)
                sp.wait_ge(tail_out, 48)
                sp.wait_ge(h_stored, 16)
                for h in range(2):
                    sp.wait_ge(rec_out[h], 16 * (STAGE_CHUNKS // 2))

            @block.gpsimd
            def _(pool):
                nc.gpsimd.memset(ident[:], 0.0).then_inc(const_step, 1)
                nc.gpsimd.memset(shift[:], 0.0).then_inc(const_step, 1)
                nc.gpsimd.memset(wrap[:], 0.0).then_inc(const_step, 1)
                nc.gpsimd.memset(fours[:], 0.0).then_inc(const_step, 1)
                nc.gpsimd.memset(lower[:], 1.0).then_inc(const_step, 1)
                pool.wait_ge(const_step, 5)
                for half in range(2):
                    nc.gpsimd.iota(fours[half * P // 2:(half + 1) * P // 2, half:half + 1].bitcast(I32),
                                   pattern=[[0, 1]], base=(127 + 64) << 23, channel_multiplier=-(2 << 23)
                                   ).then_inc(const_step, 1)
                    pool.wait_ge(const_step, 6 + half)
                nc.gpsimd.affine_select(out=ident[:], in_=ident[:], compare_op=ALU.not_equal, fill=1.0,
                                        base=0, pattern=[[-1, P]], channel_multiplier=1)
                nc.gpsimd.affine_select(out=shift[:], in_=shift[:], compare_op=ALU.not_equal, fill=1.0,
                                        base=1, pattern=[[-1, P]], channel_multiplier=1)
                nc.gpsimd.affine_select(out=wrap[:], in_=wrap[:], compare_op=ALU.not_equal, fill=1.0,
                                        base=1 - P, pattern=[[-1, P]], channel_multiplier=1)
                nc.gpsimd.iota(id_int[:], pattern=[[P, TILES]], base=0, channel_multiplier=1)
                nc.gpsimd.iota(column[:], pattern=[[1, P]], base=0, channel_multiplier=0)
                nc.gpsimd.iota(tile_base[:], pattern=[[P, TILES]], base=0, channel_multiplier=0)
                nc.gpsimd.iota(local_int[:], pattern=[[1, GROUP * P]], base=0, channel_multiplier=0)
                nc.gpsimd.iota(spare_int[:], pattern=[[0, 1]], base=NODE_ROWS, channel_multiplier=1)
                nc.gpsimd.affine_select(out=lower[:], in_=lower[:], compare_op=ALU.is_gt, fill=0.0,
                                        base=0, pattern=[[-1, P]], channel_multiplier=1)
                nc.gpsimd.iota(base_int[:], pattern=[[-GROUP * P, GROUPS]], base=0,
                               channel_multiplier=0).then_inc(ident_ready, 1)
                nc.gpsimd.memset(rec[:].rearrange("p a e r -> p (a e r)"), 0).then_inc(rec_zero, 1)

                nc.gpsimd.memset(t_dst[:], NODES).then_inc(tail_zero, 1)
                for tile in (t_src, t_type, t_attr, t_norm):
                    nc.gpsimd.memset(tile[:], 0).then_inc(tail_zero, 1)
                nc.gpsimd.memset(t_rec[:].rearrange("p e r -> p (e r)"), 0).then_inc(tail_made, 1)
                nc.gpsimd.memset(lead[:], -1).then_inc(tail_made, 1)
                nc.gpsimd.memset(zeros[:], 0.0).then_inc(tail_made, 1)

                spans = dst.rearrange("(s e) -> s e", e=SPAN)

                def fetch(i, h, first):
                    pool.wait_ge(idx_ready, 2 * i + h + 1)
                    if not first:
                        pool.wait_ge(span_used, 2 * i + h - 1)
                    pool.sem_inc(pool_waited, 1)
                    for k in range(GROUP):
                        pool.indirect_dma_start(
                            out=span_dst[:, h, k, :], out_offset=None, in_=spans,
                            in_offset=bass.IndirectOffsetOnAxis(ap=span_idx[:, h, k:k + 1], axis=0)
                        ).then_inc(span_got[h], 16)

                def place(i, h):
                    pool.wait_ge(place_ready, 2 * i + h + 1)
                    pool.sem_inc(pool_waited, 1)
                    for k in range(GROUP):
                        pool.indirect_dma_start(
                            out=placed.ap(), out_offset=bass.IndirectOffsetOnAxis(ap=place_row[:, h, k:k + 1], axis=0),
                            in_=place_h[:, h, k, :], in_offset=None).then_inc(placed_out[h], 16)

                fetch(0, 0, True)
                fetch(0, 1, True)
                with pool.Fori(1, GROUPS // 2) as i:
                    for h in range(2):
                        fetch(i, h, False)

                pool.wait_ge(place_zeroed, 16 * ZERO_STORES)
                with pool.Fori(0, GROUPS // 2) as i:
                    for h in range(2):
                        place(i, h)
                pool.wait_ge(tail_made, 3)
                pool.wait_ge(tail_in, 160)
                nc.gpsimd.tensor_copy(t_rec[:, :, R_DST], t_dst[:]).then_inc(tail_made, 1)
                nc.gpsimd.tensor_copy(t_rec[:, :, R_SRC], t_src[:]).then_inc(tail_made, 1)
                nc.gpsimd.tensor_copy(t_rec[:, :, R_TYPE], t_type[:]).then_inc(tail_made, 1)
                nc.gpsimd.tensor_copy(t_rec[:].bitcast(F32)[:, :, R_ATTR:R_ATTR + 2],
                                      t_attr[:].rearrange("p (e a) -> p e a", a=2)).then_inc(tail_made, 1)
                nc.gpsimd.tensor_copy(t_rec[:].bitcast(F32)[:, :, R_NORM], t_norm[:]).then_inc(tail_made, 1)
                for h in range(2):
                    pool.wait_ge(placed_out[h], 16 * GROUP * (GROUPS // 2))

            @block.vector
            def _(dve):
                nc.vector.memset(x_sb[:, (TILES - 1) * FEAT:], 0.0).then_inc(x_pad, 1)
                nc.vector.memset(ones[:], 1.0)
                nc.vector.memset(ones_b[:], 1.0)
                nc.vector.memset(dst_all[:, ORDER_COLS:], NODES).then_inc(order_set, 1)
                nc.vector.memset(eps_sb[:], EPS).then_inc(setup, 1)
                nc.vector.memset(upto[:, 0:1], 0.0).then_inc(setup, 1)
                nc.vector.memset(wct_pad[:].rearrange("b a c -> b (a c)"), 0.0).then_inc(setup, 1)
                nc.vector.memset(zero_rows[:], 0.0).then_inc(zero_ready, 1)
                dve.wait_ge(setup, 3)
                dve.wait_ge(ident_ready, 1)
                nc.vector.tensor_copy(node_id[:], id_int[:]).then_inc(setup, 1)
                nc.vector.tensor_copy(local_id[:], local_int[:]).then_inc(setup, 1)
                nc.vector.tensor_copy(spare_row[:], spare_int[:])
                nc.vector.tensor_copy(ident_b[:], ident[:])
                nc.vector.tensor_scalar(limits[:], fours[:], 2.0, None, ALU.mult)
                nc.vector.tensor_copy(group_base[:], base_int[:]).then_inc(setup, 1)
                dve.wait_ge(order_in, 32)
                firsts = dst_all[0:ORDER_PARTS, 0:ORDER_COLS].rearrange("p (s e) -> p s e", e=SPAN)[:, :, 0]
                nc.vector.tensor_scalar(first_lo[0:ORDER_PARTS, :], firsts, P - 1, None, ALU.bitwise_and)
                nc.vector.tensor_scalar(first_hi[0:ORDER_PARTS, :], firsts, -P, None, ALU.bitwise_and
                                        ).then_inc(spans_marked, 1)
                dve.wait_ge(spans_marked, 1)
                wide = [ORDER_PARTS, PART_SPANS, P]
                nc.vector.tensor_tensor(not_past[0:ORDER_PARTS, :, :], first_lo[0:ORDER_PARTS, :].unsqueeze(2).to_broadcast(wide),
                                        column[0:ORDER_PARTS, :].unsqueeze(1).to_broadcast(wide), ALU.is_le)
                wide = [ORDER_PARTS, PART_SPANS, TILES]
                hi = first_hi[0:ORDER_PARTS, :].unsqueeze(2).to_broadcast(wide)
                bases = tile_base[0:ORDER_PARTS, :].unsqueeze(1).to_broadcast(wide)
                nc.vector.tensor_tensor(in_tile[0:ORDER_PARTS, :, :], hi, bases, ALU.is_equal)
                nc.vector.tensor_tensor(in_lower[0:ORDER_PARTS, :, :], hi, bases, ALU.is_lt).then_inc(spans_marked, 1)
                nc.vector.tensor_tensor(falls[0:ORDER_PARTS, :], dst_all[0:ORDER_PARTS, 1:],
                                        dst_all[0:ORDER_PARTS, 0:ORDER_COLS], ALU.is_lt).then_inc(order_step, 1)
                dve.wait_ge(order_step, 1)
                nc.vector.tensor_reduce(n_falls[0:ORDER_PARTS, :], falls[0:ORDER_PARTS, :], AX, ALU.add
                                        ).then_inc(order_step, 1)
                dve.wait_ge(spans_counted, 1)
                nc.vector.tensor_scalar(span_no[:], ps_spans[:, 0:TILES], -1.0, 0.0, ALU.add, ALU.max).then_inc(search, 1)
                dve.wait_ge(search, 1)
                nc.vector.tensor_scalar(span_base[:], span_no[:], float(SPAN), None, ALU.mult).then_inc(search, 1)

                def indices(i, h):
                    nodes = bass.ds((2 * i + h) * GROUP, GROUP)
                    nc.vector.tensor_copy(ids[:, h, :], node_id[:, nodes])
                    nc.vector.tensor_copy(span_idx[:, h, :], span_no[:, nodes]).then_inc(idx_ready, 1)

                indices(0, 0)
                indices(0, 1)
                dve.wait_ge(w_in, 96)
                for par in range(2):
                    last = nc.vector.tensor_copy(
                        wct_pad[:, par, :].rearrange("b (g q r) -> b g q r", g=4, q=2)[:, :, par, :],
                        wct[:].unsqueeze(1).to_broadcast([BASES, 4, RELS]))
                last.then_inc(setup, 1)
                dve.wait_ge(x_in, 32)

                def normalise(j, h, first):
                    if not first:
                        dve.wait_ge(h_kept, j - 1)
                    ln_group(nc, dve, ln, x_sb[:, bass.ds(j * GCOLS, GCOLS)], j, h, ln_step,
                             var_ready, std_ready, h_ready)

                dve.wait_ge(wrel_ready, 1)
                nc.vector.tensor_copy(w2_sb[:], ps_a[:]).then_inc(setup, 1)
                dve.wait_ge(setup, 8)
                dve.wait_ge(rec_zero, 1)

                def make(i, h, first):
                    dve.wait_ge(raw_in[h], 80 * i + 80)
                    if not first:
                        dve.wait_ge(rec_out[h], 16 * i)
                    r = rec[:, h, :, :]
                    rf = r.bitcast(F32)
                    nc.vector.tensor_copy(r[:, :, R_DST], raw_dst[:, h, :])
                    nc.vector.tensor_copy(r[:, :, R_SRC], raw_src[:, h, :])
                    nc.vector.tensor_copy(r[:, :, R_TYPE], raw_type[:, h, :])
                    nc.vector.tensor_copy(rf[:, :, R_ATTR:R_ATTR + 2],
                                          raw_attr[:, h, :].rearrange("p (e a) -> p e a", a=2))
                    nc.vector.tensor_copy(rf[:, :, R_NORM], raw_norm[:, h, :]).then_inc(rec_made, 1)

                for h in range(2):
                    normalise(h, h, True)

                def count_inside(i, h):
                    j = 2 * i + h
                    dve.wait_ge(span_got[h], 16 * GROUP * (i + 1))
                    for k in range(GROUP):
                        last = nc.vector.tensor_scalar(
                            hits[:], span_dst[:, h, k, :], ids[:, h, k:k + 1], 0.0, ALU.is_le, ALU.add,
                            accum_out=inside[:, h, k:k + 1])
                        if k < GROUP - 1:
                            last.then_inc(inside_step, 1)
                            dve.wait_ge(inside_step, j * (GROUP - 1) + k + 1)
                    last.then_inc(span_used, 1)
                    dve.wait_ge(span_used, j + 1)
                    nc.vector.tensor_tensor(upto[:, bass.ds(1 + j * GROUP, GROUP)], inside[:, h, :],
                                            span_base[:, bass.ds(j * GROUP, GROUP)], ALU.add).then_inc(counted, 1)

                with dve.Fori(1, GROUPS // 2) as i:
                    for h in range(2):
                        count_inside(i - 1, h)
                        dve.wait_ge(counted, 2 * i + h - 1)
                        indices(i, h)
                        normalise(2 * i + h, h, False)
                for h in range(2):
                    count_inside(GROUPS // 2 - 1, h)
                dve.wait_ge(counted, GROUPS)
                dve.wait_ge(before_ready, 1)
                dve.wait_ge(order_ready, 1)
                nc.vector.tensor_scalar(ordered[:], ps_a[:, 0:1], 0.0, None, ALU.is_equal)
                nc.vector.tensor_scalar(in_order[:], ps_a[0:1, 0:1], 0.0, None, ALU.is_equal)
                nc.vector.memset(limits[0:P // 2, 1:2], 2.0 ** 120)
                nc.vector.tensor_tensor(has[:], upto[:, 1:], ps_b[:, 0:TILES], ALU.is_gt)
                nc.vector.tensor_copy(edge[:, 0, :], ps_b[:, 0:TILES])
                nc.vector.memset(spare[:, 1, :], float(PADDED))
                nc.vector.tensor_scalar(spare[:, 0, :], node_id[:], float(PADDED), None, ALU.add)
                nc.vector.tensor_scalar(edge[:, 1, :], upto[:, 1:], -1.0, None, ALU.add).then_inc(counted, 1)
                dve.wait_ge(counted, GROUPS + 1)
                nc.vector.tensor_scalar(quarter[:], edge[:], float(QEDGES), None, ALU.is_ge)
                nc.vector.scalar_tensor_tensor(out=row[:], in0=edge[:], scalar=float(QUARTERS), in1=spare[:],
                                               op0=ALU.mult, op1=ALU.subtract).then_inc(counted, 1)
                for q in range(2, QUARTERS):
                    dve.wait_ge(counted, GROUPS + q)
                    nc.vector.scalar_tensor_tensor(out=quarter[:], in0=edge[:], scalar=float(q * QEDGES), in1=quarter[:],
                                                   op0=ALU.is_ge, op1=ALU.add).then_inc(counted, 1)
                dve.wait_ge(counted, GROUPS + QUARTERS)
                nc.vector.scalar_tensor_tensor(out=row[:], in0=quarter[:], scalar=-float(QUARTERS * QEDGES - 1),
                                               in1=row[:], op0=ALU.mult, op1=ALU.add).then_inc(counted, 1)
                dve.wait_ge(counted, GROUPS + QUARTERS + 1)
                nc.vector.scalar_tensor_tensor(out=row[:], in0=row[:], scalar=ordered[:, 0:1],
                                               in1=has[:].unsqueeze(1).to_broadcast([P, 2, TILES]),
                                               op0=ALU.mult, op1=ALU.mult).then_inc(counted, 1)
                dve.wait_ge(counted, GROUPS + QUARTERS + 2)
                nc.vector.tensor_tensor(first_row[:], row[:, 0, :], spare[:, 0, :], ALU.add)
                nc.vector.tensor_tensor(last_edge[:], row[:, 1, :], spare[:, 1, :], ALU.add).then_inc(counted, 1)
                dve.wait_ge(counted, GROUPS + QUARTERS + 3)
                dve.wait_ge(h_kept, GROUPS)

                def fill(i, h, first):
                    j = 2 * i + h
                    if not first:
                        dve.wait_ge(placed_out[h], 16 * GROUP * i)
                    nc.vector.tensor_copy(place_row[:, h, :], first_row[:, bass.ds(j * GROUP, GROUP)])
                    nc.vector.tensor_copy(place_h[:, h, :, :].rearrange("p t f -> p (t f)"),
                                          h_all[:, bass.ds(j * GCOLS, GCOLS)]).then_inc(place_ready, 1)

                fill(0, 0, True)
                fill(0, 1, True)
                for h in range(2):
                    make(0, h, True)
                with dve.Fori(1, GROUPS // 2) as i:
                    for h in range(2):
                        fill(i, h, False)
                        make(i, h, False)

            @block.scalar
            def _(act):
                act.wait_ge(zero_ready, 1)
                act.wait_ge(x_in, 32)
                act.wait_ge(order_in, 32)
                act.wait_ge(setup, 1)

                def zero_rows_of(z):
                    act.dma_start(bass.AP(placed, z * (P * ZERO_WORDS), [[ZERO_WORDS, P], [1, ZERO_WORDS]]), zero_rows[:]
                                  ).then_inc(place_zeroed, 16)

                def keep_h(j, h):
                    act.wait_ge(h_ready, j + 1)
                    nc.scalar.copy(h_all[:, bass.ds(j * GCOLS, GCOLS)], ln["h"][:, h, :]).then_inc(h_kept, 1)

                with act.Fori(0, GROUPS // 2) as i:
                    for h in range(2):
                        j = 2 * i + h
                        root(nc, act, ln, eps_sb, j, h, var_ready, std_ready)
                        keep_h(j, h)
                        for n in range(GROUP_STORES):
                            zero_rows_of(j * GROUP_STORES + n)
                for z in range(GROUPS * GROUP_STORES, ZERO_STORES):
                    zero_rows_of(z)
                for acc in accs:
                    for n in range(ACC_PARTS):
                        act.dma_start(bass.AP(acc, n * PART_WORDS, [[ACC_WORDS, P], [1, PART_WORDS]]),
                                      zero_rows[:, 0:PART_WORDS]).then_inc(acc_zeroed, 16)
                act.wait_ge(acc_zeroed, 16 * COPIES * ACC_PARTS)

            @block.tensor
            def _(pe):
                pe.wait_ge(ident_ready, 1)
                pe.wait_ge(spans_marked, 2)
                for r in range(PART_SPANS):
                    nc.tensor.matmul(ps_spans[:, 0:TILES], not_past[0:ORDER_PARTS, r, :], in_tile[0:ORDER_PARTS, r, :],
                                     start=(r == 0), stop=False)
                    mm = nc.tensor.matmul(ps_spans[:, 0:TILES], ones_b[0:ORDER_PARTS, :], in_lower[0:ORDER_PARTS, r, :],
                                          start=False, stop=(r == PART_SPANS - 1))
                mm.then_inc(spans_counted, 1)
                pe.wait_ge(setup, 7)
                pe.wait_ge(w_in, 96)
                wr = wr_sb[:].rearrange("b (r q) o -> b q r o", q=2)
                nc.tensor.matmul(ps_a[:], wct_pad[:, 0, :], wr[:, 0, :, :], start=True, stop=False)
                nc.tensor.matmul(ps_a[:], wct_pad[:, 1, :], wr[:, 1, :, :], start=False, stop=True
                                 ).then_inc(wrel_ready, 1)
                pe.wait_ge(setup, 8)
                pe.wait_ge(order_step, 2)
                nc.tensor.matmul(ps_a[:, 0:1], ones[0:ORDER_PARTS, :], n_falls[0:ORDER_PARTS, :], start=True, stop=True
                                 ).then_inc(order_ready, 1)
                pe.wait_ge(counted, GROUPS)
                nc.tensor.matmul(ps_b[:, 0:TILES], shift[:], upto[:, 1:], start=True, stop=False)
                nc.tensor.matmul(ps_b[:, 0:TILES], wrap[:], upto[:, 0:TILES], start=False, stop=True
                                 ).then_inc(before_ready, 1)

        nc.clear_and_free_semaphores(sems)
        nc.all_engine_barrier()


def group_first(group):
    group(0, 0, True)
    group(1, 1, True)


def from_block(t, n):
    return not isinstance(t, int) or t >= n


def ordered_scatter_loop(nc, in_order, records, h_table, placed, starts, accs, ident, ident_b, w1_sb, spare_row,
                         fours, limits):
    groups = TILES_PER_BLOCK // COPY_SET
    ROW = FEAT + 2
    with ExitStack() as ctx:
        def sb(name, shape, dt=F32):
            return ctx.enter_context(nc.sbuf_tensor(f"{name}_s", shape, dt))

        def ps(name):
            return ctx.enter_context(nc.psum_tensor(f"{name}_s", [P, BLOCK], F32))

        def sem(name):
            return ctx.enter_context(nc.semaphore(f"{name}_s"))

        rec = sb("rec", [P, 2, QUARTERS, PER_PART + 1, REC], I32)
        h_in = sb("h_in", [P, 2, PER_PART, QUARTERS * FEAT])
        goes_on = sb("goes_on", [P, 2, PER_PART, QUARTERS * FEAT], BF16)
        keep = sb("keep", [P, 2, BLOCK])
        running = sb("running", [P, 2, BLOCK])
        start_col = sb("start_col", [P, 1])
        start_int = sb("start_int", [QUARTERS, 1], I32)
        start_row = sb("start_row", [QUARTERS, FEAT])
        source = sb("source", [P, 2, TILES_PER_BLOCK])
        part_of = sb("part_of", [P, 2, TILES_PER_BLOCK], I32)
        source_b = sb("source_b", [P, 2, 2, TILES_PER_BLOCK], BF16)
        scaled = sb("scaled", [P, TILES_PER_BLOCK, 2])
        centre_int = sb("centre_int", [P, GRID], I32)
        centre = sb("centre", [P, GRID])
        rising = sb("rising", [P, 2 * TILES_PER_BLOCK, GRID])
        falling = sb("falling", [P, 2 * TILES_PER_BLOCK, GRID])
        tent = sb("tent", [P, 2, 2 * TILES_PER_BLOCK, GRID])
        spread = sb("spread", [P, 2, TILES_PER_BLOCK, GRID * FEAT])
        summed = sb("summed", [P, 2, TILES_PER_BLOCK, ROW])
        is_first = sb("is_first", [P, TILES_PER_BLOCK])
        moved = sb("moved", [P, TILES_PER_BLOCK])
        target = sb("target", [P, 2, TILES_PER_BLOCK], I32)
        spread_t = sb("spread_t", [P, 2, COPY_SET, P])
        scaled_w = sb("scaled_w", [P, 2, COPY_SET, GRID * FEAT])
        message = sb("message", [P, 2, COPY_SET, ROW])
        same = sb("same", [P, groups, COPY_SET, P])

        ps_keep, ps_place, ps_back = ps("ps_keep"), ps("ps_place"), ps("ps_back")
        ps_src, ps_t, ps_sum = ps("ps_src"), ps("ps_t"), ps("ps_sum")
        ps_z = [ps(f"ps_z{s}") for s in range(2)]

        rec_in = [sem(f"rec_in{h}") for h in range(2)]
        placed_in = [sem(f"placed_in{h}") for h in range(2)]
        added = [sem(f"added{s}") for s in range(ADD_SETS)]
        start_in, setup, prep_step, prepared = sem("start_in"), sem("setup"), sem("prep_step"), sem("prepared")
        keep_turned, keep_ready, placed_turned = sem("keep_turned"), sem("keep_ready"), sem("placed_turned")
        scanned, back_turned, spread_ready = sem("scanned"), sem("back_turned"), sem("spread_ready")
        src_ready, same_ready, turned, turned_copied = sem("src_ready"), sem("same_ready"), sem("turned"), sem("turned_copied")
        product, scaled_ready, message_ready = sem("product"), sem("scaled_ready"), sem("message_ready")
        set_summed, summed_ready = sem("set_summed"), sem("summed_ready")
        target_step, target_ready, pool_waited = sem("target_step"), sem("target_ready"), sem("pool_waited")
        PREP, TARGET = 7, 4

        def each_block(eng, work):
            for i in (0, 1):
                for h in range(2):
                    work(i, h)
            with eng.Fori(2, BLOCKS // 2 - 1) as i:
                for h in range(2):
                    work(i, h)
            for h in range(2):
                work(BLOCKS // 2 - 1, h)

        def has_next(t, n):
            return not isinstance(t, int) or t + n < BLOCKS

        with nc.Block() as block:

            @block.sync
            def _(sp):
                with sp.If(sp.value_load(in_order[0:1, 0:1]) > 0):
                    def load(t, h):
                        sp.dma_start(
                            rec[:, h, :, :, :].rearrange("p q e r -> p q (e r)"),
                            bass.AP(records, t * (BLOCK * REC),
                                    [[PER_PART * REC, P], [QEDGES * REC, QUARTERS], [1, (PER_PART + 1) * REC]])
                        ).then_inc(rec_in[h], 16)
                        words = TILES_PER_BLOCK * FEAT
                        sp.dma_start(h_in[:, h, :, :].rearrange("p e c -> p (e c)"),
                                     bass.AP(placed, t * (P * words), [[words, P], [1, words]])).then_inc(placed_in[h], 16)

                    def reload(i, h):
                        t = 2 * i + h
                        if has_next(t, 2):
                            sp.wait_ge(prepared, t + 1)
                            sp.wait_ge(placed_turned, t + 1)
                            load(t + 2, h)

                    load(0, 0)
                    load(1, 1)
                    each_block(sp, reload)

            @block.gpsimd
            def _(pool):
                with pool.If(pool.value_load(in_order[0:1, 0:1]) > 0):
                    nc.gpsimd.iota(centre_int[:], pattern=[[1, GRID]], base=0, channel_multiplier=0).then_inc(setup, 1)
                    with nc.allow_non_contiguous_dma("four words"):
                        pool.dma_start(start_int[:], bass.AP(records, REC + R_DST, [[QEDGES * REC, QUARTERS], [1, 1]])
                                       ).then_inc(start_in, 16)
                    pool.wait_ge(start_in, 16)
                    pool.indirect_dma_start(out=start_row[:], out_offset=None, in_=h_table.ap(),
                                            in_offset=bass.IndirectOffsetOnAxis(ap=start_int[:], axis=0)
                                            ).then_inc(start_in, 16)
                    pool.wait_ge(start_in, 32)
                    pool.dma_start(starts.ap(), start_row[:]).then_inc(start_in, 16)
                    pool.wait_ge(start_in, 48)
                    with nc.allow_non_contiguous_dma("128 words"):
                        pool.dma_start(start_col[:], bass.AP(starts, 0, [[1, P], [1, 1]])).then_inc(start_in, 16)

                    def scatter(i, h):
                        t = 2 * i + h
                        pool.wait_ge(target_ready, t + 1)
                        for g in range(TILES_PER_BLOCK // ADD_SET):
                            s = g % ADD_SETS
                            if g % (COPY_SET // ADD_SET) == 0:
                                pool.wait_ge(summed_ready, groups * t + g // (COPY_SET // ADD_SET) + 1)
                            if g >= ADD_SETS or from_block(t, 1):
                                pool.wait_ge(added[s], 16 * ADD_SET * (t * ADD_ROUNDS + g // ADD_SETS))
                            pool.sem_inc(pool_waited, 1)
                            for n in range(ADD_SET):
                                k = g * ADD_SET + n
                                pool.indirect_dma_start(
                                    out=accs[s * ADD_SET + n].ap(),
                                    out_offset=bass.IndirectOffsetOnAxis(ap=target[:, h, k:k + 1], axis=0),
                                    in_=summed[:, h, k, 0:FEAT], in_offset=None, compute_op=ALU.add
                                ).then_inc(added[s], 16)

                    each_block(pool, scatter)
                    for s in range(ADD_SETS):
                        pool.wait_ge(added[s], 16 * ADD_SET * BLOCKS * ADD_ROUNDS)

            @block.vector
            def _(dve):
                with dve.If(dve.value_load(in_order[0:1, 0:1]) > 0):
                    dve.wait_ge(setup, 1)
                    nc.vector.tensor_copy(centre[:], centre_int[:]).then_inc(setup, 1)
                    for s in range(2):
                        nc.vector.tensor_copy(message[:, s, :, FEAT:], fours[:].unsqueeze(1).to_broadcast([P, COPY_SET, 2])
                                              ).then_inc(setup, 1)
                    dve.wait_ge(setup, 4)

                    def prepare_block(i, h):
                        t = 2 * i + h
                        b = t * PREP
                        dve.wait_ge(rec_in[h], 16 * i + 16)
                        r = rec[:, h, :, 1:, :].rearrange("p q e r -> p e q r")
                        before = rec[:, h, :, 0:PER_PART, :].rearrange("p q e r -> p e q r")
                        attr = r[:, :, :, R_ATTR:R_ATTR + 2].bitcast(F32)
                        wide = [P, 2 * TILES_PER_BLOCK, GRID]
                        per_feature = [P, PER_PART, QUARTERS, FEAT]

                        def quad(ap):
                            return ap.rearrange("p (e q) -> p e q", q=QUARTERS)

                        nc.vector.tensor_scalar(scaled[:].rearrange("p (e q) a -> p e q a", q=QUARTERS), attr,
                                                (GRID - 1) / 2, (GRID - 1) / 2, ALU.mult, ALU.add).then_inc(prep_step, 1)
                        nc.vector.tensor_scalar(quad(part_of[:, 0, :]), r[:, :, :, R_SRC], -P, None, ALU.bitwise_and)
                        nc.vector.tensor_scalar(quad(part_of[:, 1, :]), r[:, :, :, R_SRC], P - 1, None, ALU.bitwise_and
                                                ).then_inc(prep_step, 1)
                        dve.wait_ge(prep_step, b + 1)
                        nc.vector.tensor_tensor(rising[:], scaled[:].rearrange("p k a -> p (k a)").unsqueeze(2).to_broadcast(wide),
                                                centre[:].unsqueeze(1).to_broadcast(wide), ALU.subtract).then_inc(prep_step, 1)
                        nc.vector.tensor_copy(quad(source[:, h, :]), r[:, :, :, R_SRC])
                        dve.wait_ge(prep_step, b + 2)
                        if from_block(t, 2):
                            dve.wait_ge(src_ready, groups * (t - 1))
                        nc.vector.tensor_copy(source_b[:, h, :, :], part_of[:]).then_inc(prep_step, 1)
                        dve.wait_ge(prep_step, b + 3)
                        nc.vector.tensor_scalar(falling[:], rising[:], -1.0, 1.0, ALU.mult, ALU.add).then_inc(prep_step, 1)
                        if from_block(t, 2):
                            dve.wait_ge(keep_turned, t - 1)
                        nc.vector.tensor_tensor(
                            goes_on[:, h, :, :].rearrange("p e (q f) -> p e q f", q=QUARTERS),
                            r[:, :, :, R_DST].unsqueeze(3).to_broadcast(per_feature),
                            before[:, :, :, R_DST].unsqueeze(3).to_broadcast(per_feature), ALU.is_equal)
                        dve.wait_ge(prep_step, b + 5)
                        nc.vector.scalar_tensor_tensor(out=rising[:], in0=rising[:], scalar=1.0, in1=falling[:],
                                                       op0=ALU.add, op1=ALU.min).then_inc(prep_step, 1)
                        dve.wait_ge(prep_step, b + 6)
                        nc.vector.tensor_scalar(tent[:, h, :, :], rising[:], 0.0, None, ALU.max).then_inc(prep_step, 1)
                        dve.wait_ge(prep_step, b + 7)
                        dve.sem_inc(prepared, 1)

                    def tent_of(h, a):
                        return tent[:, h, :, :].rearrange("p (k a) c -> p k a c", a=2)[:, :, a, :]

                    def scan(t, h):
                        dve.wait_ge(keep_ready, t + 1)
                        dve.wait_ge(placed_turned, t + 1)
                        if from_block(t, 2):
                            dve.wait_ge(back_turned, t - 1)
                        if from_block(t, 1):
                            dve.wait_ge(scanned, t)
                            initial = running[:, 1 - h, BLOCK - 1:BLOCK]
                        else:
                            dve.wait_ge(start_in, 64)
                            initial = start_col[:]
                        nc.vector.tensor_tensor_scan(running[:, h, :], keep[:, h, :], ps_place[:], initial,
                                                     ALU.mult, ALU.add).then_inc(scanned, 1)

                    def spread_rows(t, h):
                        dve.wait_ge(back_turned, t + 1)
                        if from_block(t, 2):
                            dve.wait_ge(turned, groups * (t - 1))
                        wide = [P, TILES_PER_BLOCK, GRID, FEAT]
                        nc.vector.tensor_tensor(
                            spread[:, h, :, :].rearrange("p k (v f) -> p k v f", f=FEAT),
                            ps_back[:].rearrange("p (k f) -> p k f", f=FEAT).unsqueeze(2).to_broadcast(wide),
                            tent_of(h, 1).unsqueeze(3).to_broadcast(wide), ALU.mult).then_inc(spread_ready, 1)

                    def compare(t, h, g):
                        n = groups * t + g
                        dve.wait_ge(src_ready, n + 1)
                        if from_block(t, 1):
                            dve.wait_ge(set_summed, n - groups + 1)
                        mine = source[:, h, g * COPY_SET:(g + 1) * COPY_SET]
                        nc.vector.tensor_tensor(same[:, g, :, :], ps_src[:].rearrange("p (n e) -> p n e", n=COPY_SET),
                                                mine.unsqueeze(2).to_broadcast([P, COPY_SET, P]), ALU.is_equal
                                                ).then_inc(same_ready, 1)

                    def scale(t, h, g):
                        s, n = g % 2, groups * t + g
                        dve.wait_ge(product, n + 1)
                        wide = [P, COPY_SET, GRID, FEAT]
                        nc.vector.tensor_tensor(
                            scaled_w[:, s, :, :].rearrange("p n (u f) -> p n u f", f=FEAT),
                            ps_z[s][:].rearrange("p (n u f) -> p n u f", n=COPY_SET, f=FEAT),
                            tent_of(h, 0)[:, g * COPY_SET:(g + 1) * COPY_SET, :].unsqueeze(3).to_broadcast(wide),
                            ALU.mult).then_inc(scaled_ready, 1)
                        dve.wait_ge(scaled_ready, n + 1)
                        if g >= 2 or from_block(t, 1):
                            dve.wait_ge(set_summed, n - 1)
                        nc.vector.tensor_reduce(message[:, s, :, 0:FEAT],
                                                scaled_w[:, s, :, :].rearrange("p n (u f) -> p n f u", f=FEAT), AX, ALU.add
                                                ).then_inc(message_ready, 1)

                    def find_moves(h):
                        nc.vector.tensor_scalar(moved[:], source[:, h, :], spare_row[:, 0:1], None, ALU.subtract
                                                ).then_inc(target_step, 1)

                    def find_targets(t, h):
                        b = t * TARGET
                        dve.wait_ge(summed_ready, groups * (t + 1))
                        nc.vector.tensor_scalar(is_first[:], summed[:, h, :, FEAT], limits[:, 0:1], None, ALU.is_le
                                                ).then_inc(target_step, 1)
                        dve.wait_ge(target_step, b + 2)
                        nc.vector.scalar_tensor_tensor(out=is_first[:], in0=summed[:, h, :, FEAT + 1], scalar=limits[:, 1:2],
                                                       in1=is_first[:], op0=ALU.is_le, op1=ALU.mult).then_inc(target_step, 1)
                        dve.wait_ge(target_step, b + 3)
                        nc.vector.tensor_tensor(moved[:], moved[:], is_first[:], ALU.mult).then_inc(target_step, 1)
                        dve.wait_ge(target_step, b + 4)
                        if from_block(t, 2):
                            for s in range(ADD_SETS):
                                dve.wait_ge(added[s], 16 * ADD_SET * ADD_ROUNDS * (t - 1))
                        nc.vector.tensor_scalar(target[:, h, :], moved[:], spare_row[:, 0:1], None, ALU.add
                                                ).then_inc(target_ready, 1)

                    def block_work(i, h):
                        t = 2 * i + h
                        for g in range(1, groups):
                            compare(t, h, g)
                            scale(t, h, g - 1)
                            if g == 2 and has_next(t, 1):
                                scan(t + 1, 1 - h)
                        if has_next(t, 1):
                            spread_rows(t + 1, 1 - h)
                        scale(t, h, groups - 1)
                        if has_next(t, 1):
                            compare(t + 1, 1 - h, 0)
                        find_moves(h)
                        if has_next(t, 2):
                            prepare_block(i + 1, h)
                        find_targets(t, h)

                    prepare_block(0, 0)
                    prepare_block(0, 1)
                    scan(0, 0)
                    spread_rows(0, 0)
                    compare(0, 0, 0)
                    each_block(dve, block_work)

            @block.tensor
            def _(pe):
                with pe.If(pe.value_load(in_order[0:1, 0:1]) > 0):
                    def lead(i, h):
                        t = 2 * i + h
                        pe.wait_ge(prepared, t + 1)
                        if from_block(t, 1):
                            pe.wait_ge(keep_ready, t)
                        for e in range(PER_PART):
                            mm = nc.tensor.matmul(ps_keep[:].rearrange("m (p e) -> m e p", e=PER_PART)[:, e, :],
                                                  goes_on[:, h, e, :], ident_b[:], start=True, stop=True)
                        mm.then_inc(keep_turned, 1)
                        pe.wait_ge(placed_in[h], 16 * i + 16)
                        if from_block(t, 1):
                            pe.wait_ge(scanned, t)
                        for e in range(PER_PART):
                            mm = nc.tensor.matmul(ps_place[:].rearrange("m (p e) -> m e p", e=PER_PART)[:, e, :],
                                                  h_in[:, h, e, :], ident[:], start=True, stop=True)
                        mm.then_inc(placed_turned, 1)

                    def back(t, h):
                        pe.wait_ge(scanned, t + 1)
                        if from_block(t, 1):
                            pe.wait_ge(spread_ready, t)
                        for e in range(PER_PART):
                            mm = nc.tensor.transpose(ps_back[:, e * P:(e + 1) * P],
                                                     running[:, h, :].rearrange("m (p e) -> m e p", e=PER_PART)[:, e, :],
                                                     ident[:])
                        mm.then_inc(back_turned, 1)

                    def turn(t, h, g):
                        s, n = g % 2, groups * t + g
                        if g >= 1 or from_block(t, 1):
                            pe.wait_ge(same_ready, n)
                        for m in range(COPY_SET):
                            k = g * COPY_SET + m
                            for part in range(2):
                                mm = nc.tensor.matmul(ps_src[:, m * P:(m + 1) * P],
                                                      source_b[:, h, part, k:k + 1].to_broadcast([P, P]), ident_b[:],
                                                      start=(part == 0), stop=(part == 1))
                        mm.then_inc(src_ready, 1)
                        pe.wait_ge(spread_ready, t + 1)
                        if g >= 1 or from_block(t, 1):
                            pe.wait_ge(turned_copied, n)
                        for m in range(COPY_SET):
                            mm = nc.tensor.transpose(ps_t[:, m * P:(m + 1) * P],
                                                     spread[:, h, g * COPY_SET + m, :], ident[:])
                        mm.then_inc(turned, 1)

                    def multiply(t, g):
                        s, n = g % 2, groups * t + g
                        pe.wait_ge(turned_copied, n + 1)
                        if g >= 2 or from_block(t, 1):
                            pe.wait_ge(scaled_ready, n - 1)
                        for m in range(COPY_SET):
                            mm = nc.tensor.matmul(ps_z[s][:, m * P:(m + 1) * P], spread_t[:, s, m, :], w1_sb[:],
                                                  start=True, stop=True)
                        mm.then_inc(product, 1)

                    def add_up(t, g):
                        s, n = g % 2, groups * t + g
                        pe.wait_ge(message_ready, n + 1)
                        pe.wait_ge(same_ready, n + 1)
                        if g >= 1 or from_block(t, 1):
                            pe.wait_ge(summed_ready, n)
                        for m in range(COPY_SET):
                            mm = nc.tensor.matmul(ps_sum[:, m * ROW:(m + 1) * ROW],
                                                  same[:, g, m, :], message[:, s, m, :], start=True, stop=True)
                        mm.then_inc(set_summed, 1)

                    def block_work(i, h):
                        t = 2 * i + h
                        for g in range(1, groups):
                            turn(t, h, g)
                            multiply(t, g - 1)
                            if g == 1 and has_next(t, 1):
                                lead(i + h, 1 - h)
                            if g == 3 and has_next(t, 1):
                                back(t + 1, 1 - h)
                            if g >= 2:
                                add_up(t, g - 2)
                        multiply(t, groups - 1)
                        add_up(t, groups - 2)
                        if has_next(t, 1):
                            turn(t + 1, 1 - h, 0)
                        add_up(t, groups - 1)

                    pe.wait_ge(setup, 4)
                    lead(0, 0)
                    back(0, 0)
                    turn(0, 0, 0)
                    each_block(pe, block_work)

            @block.scalar
            def _(act):
                with act.If(act.value_load(in_order[0:1, 0:1]) > 0):
                    def copy_keep(t, h):
                        act.wait_ge(keep_turned, t + 1)
                        if from_block(t, 2):
                            act.wait_ge(scanned, t - 1)
                        nc.scalar.copy(keep[:, h, :], ps_keep[:]).then_inc(keep_ready, 1)

                    def copy_turned(t, g):
                        s, n = g % 2, groups * t + g
                        act.wait_ge(turned, n + 1)
                        if g >= 2 or from_block(t, 1):
                            act.wait_ge(product, n - 1)
                        nc.scalar.copy(spread_t[:, s, :, :].rearrange("p n e -> p (n e)"), ps_t[:]
                                       ).then_inc(turned_copied, 1)

                    def copy_sums(t, h, g):
                        s, n = g % 2, groups * t + g
                        act.wait_ge(set_summed, n + 1)
                        if g == 0 and from_block(t, 2):
                            for a in range(ADD_SETS):
                                act.wait_ge(added[a], 16 * ADD_SET * ADD_ROUNDS * (t - 1))
                        nc.scalar.copy(summed[:, h, g * COPY_SET:(g + 1) * COPY_SET, :].rearrange("p n c -> p (n c)"),
                                       ps_sum[:, 0:COPY_SET * ROW]).then_inc(summed_ready, 1)

                    def copies(i, h):
                        t = 2 * i + h
                        for g in range(1, groups + 1):
                            if g < groups or has_next(t, 1):
                                copy_turned(t, g)
                            if g == 1 and has_next(t, 1):
                                copy_keep(t + 1, 1 - h)
                            if g >= 2:
                                copy_sums(t, h, g - 2)
                        copy_sums(t, h, groups - 1)

                    copy_keep(0, 0)
                    copy_turned(0, 0)
                    each_block(act, copies)


def ordered_edge_loop(nc, in_order, records, table, sums, ident, ident_b):
    with ExitStack() as ctx:
        def sb(name, shape, dt=F32):
            return ctx.enter_context(nc.sbuf_tensor(f"{name}_e", shape, dt))

        def ps(name):
            return ctx.enter_context(nc.psum_tensor(f"{name}_e", [P, BLOCK], F32))

        def sem(name):
            return ctx.enter_context(nc.semaphore(f"{name}_e"))

        rec = sb("rec", [P, 2, QUARTERS, PER_PART + 1, REC], I32)
        idx = sb("idx", [P, 2, TILES_PER_BLOCK], I32)
        goes_on = sb("goes_on", [P, 2, PER_PART, QUARTERS * FEAT], BF16)
        got = sb("got", [P, 2, TILES_PER_BLOCK, FEAT])
        weighed = sb("weighed", [P, 2, PER_PART, QUARTERS * FEAT])
        keep = sb("keep", [P, 2, BLOCK])
        running = sb("running", [P, 2, BLOCK])
        turned_sb = sb("turned_sb", [P, 2, TILES_PER_BLOCK * FEAT])

        ps_keep = [ps(f"ps_keep{h}") for h in range(2)]
        ps_msg = [ps(f"ps_msg{h}") for h in range(2)]
        ps_sum = [ps(f"ps_sum{h}") for h in range(2)]

        rec_in = [sem(f"rec_in{h}") for h in range(2)]
        gathered = [sem(f"gathered{h}") for h in range(2)]
        stored = [sem(f"stored{h}") for h in range(2)]
        prepared, weighed_ready = sem("prepared"), sem("weighed_ready")
        keep_turned, keep_ready, msg_ready = sem("keep_turned"), sem("keep_ready"), sem("msg_ready")
        scanned, sum_turned, sum_ready = sem("scanned"), sem("sum_turned"), sem("sum_ready")
        start = sem("start")
        pool_waited = sem("pool_waited")

        with nc.Block() as block:

            @block.sync
            def _(sp):
                with sp.If(sp.value_load(in_order[0:1, 0:1]) > 0):
                    def load(t, h):
                        sp.dma_start(
                            rec[:, h, :, :, :].rearrange("p q e r -> p q (e r)"),
                            bass.AP(records, t * (BLOCK * REC),
                                    [[PER_PART * REC, P], [QEDGES * REC, QUARTERS], [1, (PER_PART + 1) * REC]])
                        ).then_inc(rec_in[h], 16)

                    def store(t, h):
                        sp.wait_ge(sum_ready, t + 1)
                        words = TILES_PER_BLOCK * FEAT
                        sp.dma_start(bass.AP(sums, t * (P * words), [[words, P], [1, words]]), turned_sb[:, h, :]
                                     ).then_inc(stored[h], 16)

                    load(0, 0)
                    load(1, 1)
                    with sp.Fori(0, BLOCKS // 2 - 1) as i:
                        for h in range(2):
                            t = 2 * i + h
                            sp.wait_ge(weighed_ready, t + 1)
                            load(t + 2, h)
                            store(t, h)
                    for h in range(2):
                        store(BLOCKS - 2 + h, h)
                    for h in range(2):
                        sp.wait_ge(stored[h], 16 * (BLOCKS // 2))

            @block.gpsimd
            def _(pool):
                with pool.If(pool.value_load(in_order[0:1, 0:1]) > 0):
                    def fetch(i, h, first):
                        t = 2 * i + h
                        pool.wait_ge(prepared, t + 1)
                        if not first:
                            pool.wait_ge(weighed_ready, t - 1)
                        pool.sem_inc(pool_waited, 1)
                        for k in range(TILES_PER_BLOCK):
                            pool.indirect_dma_start(
                                out=got[:, h, k, :], out_offset=None, in_=table.ap(),
                                in_offset=bass.IndirectOffsetOnAxis(ap=idx[:, h, k:k + 1], axis=0)
                            ).then_inc(gathered[h], 16)

                    fetch(0, 0, True)
                    fetch(0, 1, True)
                    with pool.Fori(1, BLOCKS // 2) as i:
                        for h in range(2):
                            fetch(i, h, False)

            @block.vector
            def _(dve):
                with dve.If(dve.value_load(in_order[0:1, 0:1]) > 0):
                    nc.vector.memset(running[:, 1, BLOCK - 1:BLOCK], 0.0).then_inc(start, 1)
                    dve.wait_ge(start, 1)

                    def prepare_block(i, h, first):
                        t = 2 * i + h
                        dve.wait_ge(rec_in[h], 16 * i + 16)
                        r = rec[:, h, :, 1:, :].rearrange("p q e r -> p e q r")
                        before = rec[:, h, :, 0:PER_PART, :].rearrange("p q e r -> p e q r")

                        def quad(ap):
                            return ap.rearrange("p (e q) -> p e q", q=QUARTERS)

                        nc.vector.scalar_tensor_tensor(out=quad(idx[:, h, :]), in0=r[:, :, :, R_SRC], scalar=float(RELS),
                                                       in1=r[:, :, :, R_TYPE], op0=ALU.mult, op1=ALU.add)
                        if not first:
                            dve.wait_ge(keep_turned, t - 1)
                        wide = [P, PER_PART, QUARTERS, FEAT]
                        nc.vector.tensor_tensor(
                            goes_on[:, h, :, :].rearrange("p e (q f) -> p e q f", q=QUARTERS),
                            r[:, :, :, R_DST].unsqueeze(3).to_broadcast(wide),
                            before[:, :, :, R_DST].unsqueeze(3).to_broadcast(wide),
                            ALU.is_equal).then_inc(prepared, 1)

                    def weigh(i, h):
                        t = 2 * i + h
                        dve.wait_ge(gathered[h], 16 * TILES_PER_BLOCK * (i + 1))
                        norm = rec[:, h, :, 1:, R_NORM].bitcast(F32).rearrange("p q e -> p e q")
                        nc.vector.tensor_tensor(
                            weighed[:, h, :, :].rearrange("p e (q f) -> p e q f", q=QUARTERS),
                            got[:, h, :, :].rearrange("p (e q) f -> p e q f", q=QUARTERS),
                            norm.unsqueeze(3).to_broadcast([P, PER_PART, QUARTERS, FEAT]),
                            ALU.mult).then_inc(weighed_ready, 1)

                    def scan(i, h, first):
                        t = 2 * i + h
                        dve.wait_ge(keep_ready, t + 1)
                        dve.wait_ge(msg_ready, t + 1)
                        if not first:
                            dve.wait_ge(sum_turned, t - 1)
                        if not (first and h == 0):
                            dve.wait_ge(scanned, t)
                        nc.vector.tensor_tensor_scan(running[:, h, :], keep[:, h, :], ps_msg[h][:],
                                                     running[:, 1 - h, BLOCK - 1:BLOCK], ALU.mult, ALU.add
                                                     ).then_inc(scanned, 1)

                    prepare_block(0, 0, True)
                    prepare_block(0, 1, True)
                    for h in range(2):
                        weigh(0, h)
                        prepare_block(1, h, False)
                        scan(0, h, True)
                    with dve.Fori(1, BLOCKS // 2 - 1) as i:
                        for h in range(2):
                            weigh(i, h)
                            prepare_block(i + 1, h, False)
                            scan(i, h, False)
                    for h in range(2):
                        weigh(BLOCKS // 2 - 1, h)
                        scan(BLOCKS // 2 - 1, h, False)

            @block.tensor
            def _(pe):
                with pe.If(pe.value_load(in_order[0:1, 0:1]) > 0):
                    def turn(i, h, first):
                        t = 2 * i + h
                        pe.wait_ge(prepared, t + 1)
                        if not first:
                            pe.wait_ge(keep_ready, t - 1)
                        for e in range(PER_PART):
                            mm = nc.tensor.matmul(ps_keep[h][:].rearrange("m (p e) -> m e p", e=PER_PART)[:, e, :],
                                                  goes_on[:, h, e, :], ident_b[:],
                                                  start=True, stop=True)
                        mm.then_inc(keep_turned, 1)
                        pe.wait_ge(weighed_ready, t + 1)
                        if not first:
                            pe.wait_ge(scanned, t - 1)
                        for e in range(PER_PART):
                            mm = nc.tensor.matmul(ps_msg[h][:].rearrange("m (p e) -> m e p", e=PER_PART)[:, e, :],
                                                  weighed[:, h, e, :], ident[:], start=True, stop=True)
                        mm.then_inc(msg_ready, 1)
                        pe.wait_ge(scanned, t + 1)
                        if not first:
                            pe.wait_ge(sum_ready, t - 1)
                        for e in range(PER_PART):
                            mm = nc.tensor.transpose(ps_sum[h][:, e * P:(e + 1) * P],
                                                     running[:, h, :].rearrange("m (p e) -> m e p", e=PER_PART)[:, e, :],
                                                     ident[:])
                        mm.then_inc(sum_turned, 1)

                    turn(0, 0, True)
                    turn(0, 1, True)
                    with pe.Fori(1, BLOCKS // 2) as i:
                        for h in range(2):
                            turn(i, h, False)

            @block.scalar
            def _(act):
                with act.If(act.value_load(in_order[0:1, 0:1]) > 0):
                    def copies(i, h, first):
                        t = 2 * i + h
                        act.wait_ge(keep_turned, t + 1)
                        if not first:
                            act.wait_ge(scanned, t - 1)
                        nc.scalar.copy(keep[:, h, :], ps_keep[h][:]).then_inc(keep_ready, 1)
                        act.wait_ge(sum_turned, t + 1)
                        if not first:
                            act.wait_ge(stored[h], 16 * i)
                        nc.scalar.copy(turned_sb[:, h, :], ps_sum[h][:]).then_inc(sum_ready, 1)

                    copies(0, 0, True)
                    copies(0, 1, True)
                    with act.Fori(1, BLOCKS // 2) as i:
                        for h in range(2):
                            copies(i, h, False)


def any_order_loop(nc, layer, in_order, records, table, accs, ident, w1_sb, spare_row, lower):
    groups = TILES_PER_BLOCK // COPY_SET
    with ExitStack() as ctx:
        def sb(name, shape, dt=F32):
            return ctx.enter_context(nc.sbuf_tensor(f"{name}_g{layer}", shape, dt))

        def ps(name):
            return ctx.enter_context(nc.psum_tensor(f"{name}_g{layer}", [P, BLOCK], F32))

        def sem(name):
            return ctx.enter_context(nc.semaphore(f"{name}_g{layer}"))

        rec = sb("rec", [P, 2, QUARTERS, PER_PART, REC], I32)
        idx = sb("idx", [P, 2, TILES_PER_BLOCK], I32)
        source = sb("source", [P, 2, TILES_PER_BLOCK])
        norm = sb("norm", [P, 2, TILES_PER_BLOCK])
        weighed = sb("weighed", [P, 2, TILES_PER_BLOCK, FEAT])
        scaled = sb("scaled", [P, TILES_PER_BLOCK, 2])
        centre_int = sb("centre_int", [P, GRID], I32)
        centre = sb("centre", [P, GRID])
        rising = sb("rising", [P, 2 * TILES_PER_BLOCK, GRID])
        falling = sb("falling", [P, 2 * TILES_PER_BLOCK, GRID])
        tent = sb("tent", [P, 2, 2 * TILES_PER_BLOCK, GRID])
        got = sb("got", [P, 2, TILES_PER_BLOCK, FEAT])
        spread = sb("spread", [P, 2, TILES_PER_BLOCK, GRID * FEAT])
        spread_t = sb("spread_t", [P, 2, COPY_SET, P])
        scaled_w = sb("scaled_w", [P, 2, COPY_SET, GRID * FEAT])
        same = sb("same", [P, 2, COPY_SET, P])
        earlier = sb("earlier", [P, COPY_SET, P])
        n_earlier = sb("n_earlier", [P, TILES_PER_BLOCK])
        to_spare = sb("to_spare", [P, TILES_PER_BLOCK])
        target = sb("target", [P, 2, TILES_PER_BLOCK], I32)
        summed = sb("summed", [P, 2, TILES_PER_BLOCK, FEAT])

        ps_src = [ps(f"ps_src{s}") for s in range(2)]
        ps_t = [ps(f"ps_t{s}") for s in range(2)]
        ps_z = [ps(f"ps_z{s}") for s in range(2)]
        ps_sum = [ps(f"ps_sum{h}") for h in range(2)]

        rec_in = [sem(f"rec_in{h}") for h in range(2)]
        gathered = [sem(f"gathered{h}") for h in range(2)]
        added = [sem(f"added{s}") for s in range(2)]
        setup, prep_step, prepared, spread_ready = sem("setup"), sem("prep_step"), sem("prepared"), sem("spread_ready")
        src_ready, same_ready, turned, turned_copied = sem("src_ready"), sem("same_ready"), sem("turned"), sem("turned_copied")
        product, scaled_ready, set_summed, summed_ready = sem("product"), sem("scaled_ready"), sem("set_summed"), sem("summed_ready")
        target_step, target_ready, pool_waited = sem("target_step"), sem("target_ready"), sem("pool_waited")
        PREP, TARGET = 5, 3

        with nc.Block() as block:

            @block.sync
            def _(sp):
                with sp.If(sp.value_load(in_order[0:1, 0:1]) == 0):
                    def load(t, h):
                        sp.dma_start(
                            rec[:, h, :, :, :].rearrange("p q e r -> p q (e r)"),
                            bass.AP(records, t * (BLOCK * REC) + REC,
                                    [[PER_PART * REC, P], [QEDGES * REC, QUARTERS], [1, PER_PART * REC]])
                        ).then_inc(rec_in[h], 16)

                    load(0, 0)
                    load(1, 1)
                    with sp.Fori(0, BLOCKS // 2 - 1) as i:
                        for h in range(2):
                            sp.wait_ge(prepared, 2 * i + h + 1)
                            load(2 * i + h + 2, h)

            @block.gpsimd
            def _(pool):
                with pool.If(pool.value_load(in_order[0:1, 0:1]) == 0):
                    nc.gpsimd.iota(centre_int[:], pattern=[[1, GRID]], base=0, channel_multiplier=0).then_inc(setup, 1)

                    def fetch(i, h, first):
                        t = 2 * i + h
                        pool.wait_ge(prepared, t + 1)
                        if not first:
                            pool.wait_ge(spread_ready, t - 1)
                        pool.sem_inc(pool_waited, 1)
                        for k in range(TILES_PER_BLOCK):
                            pool.indirect_dma_start(
                                out=got[:, h, k, :], out_offset=None, in_=table.ap(),
                                in_offset=bass.IndirectOffsetOnAxis(ap=idx[:, h, k:k + 1], axis=0)
                            ).then_inc(gathered[h], 16)

                    def scatter(i, h, first):
                        t = 2 * i + h
                        pool.wait_ge(target_ready, t + 1)
                        pool.wait_ge(summed_ready, t + 1)
                        for g in range(groups):
                            if not (first and h == 0 and g < 2):
                                pool.wait_ge(added[g % 2], 16 * COPY_SET * (t * (groups // 2) + g // 2))
                            pool.sem_inc(pool_waited, 1)
                            for n in range(COPY_SET):
                                k = g * COPY_SET + n
                                pool.indirect_dma_start(
                                    out=accs[(g % 2) * COPY_SET + n].ap(),
                                    out_offset=bass.IndirectOffsetOnAxis(ap=target[:, h, k:k + 1], axis=0),
                                    in_=summed[:, h, k, :], in_offset=None, compute_op=ALU.add
                                ).then_inc(added[g % 2], 16)

                    fetch(0, 0, True)
                    fetch(0, 1, True)
                    scatter(0, 0, True)
                    fetch(1, 0, False)
                    scatter(0, 1, True)
                    fetch(1, 1, False)
                    with pool.Fori(1, BLOCKS // 2 - 1) as i:
                        for h in range(2):
                            scatter(i, h, False)
                            fetch(i + 1, h, False)
                    for h in range(2):
                        scatter(BLOCKS // 2 - 1, h, False)
                    for s in range(2):
                        pool.wait_ge(added[s], 16 * COPY_SET * BLOCKS * (groups // 2))

            @block.vector
            def _(dve):
                with dve.If(dve.value_load(in_order[0:1, 0:1]) == 0):
                    dve.wait_ge(setup, 1)
                    nc.vector.tensor_copy(centre[:], centre_int[:]).then_inc(setup, 1)
                    dve.wait_ge(setup, 2)

                    def prepare_block(i, h, first):
                        t = 2 * i + h
                        b = t * PREP
                        dve.wait_ge(rec_in[h], 16 * i + 16)
                        r = rec[:, h, :, :, :].rearrange("p q e r -> p e q r")
                        attr = r[:, :, :, R_ATTR:R_ATTR + 2].bitcast(F32)
                        wide = [P, 2 * TILES_PER_BLOCK, GRID]

                        def quad(ap):
                            return ap.rearrange("p (e q) -> p e q", q=QUARTERS)

                        if layer == 2:
                            nc.vector.scalar_tensor_tensor(out=quad(idx[:, h, :]), in0=r[:, :, :, R_SRC], scalar=float(RELS),
                                                           in1=r[:, :, :, R_TYPE], op0=ALU.mult, op1=ALU.add)
                            nc.vector.tensor_copy(quad(norm[:, h, :]), r[:, :, :, R_NORM].bitcast(F32))
                            if not first:
                                dve.wait_ge(src_ready, groups * (t - 1))
                            nc.vector.tensor_copy(quad(source[:, h, :]), r[:, :, :, R_DST]).then_inc(prep_step, 1)
                            dve.wait_ge(prep_step, t + 1)
                            dve.sem_inc(prepared, 1)
                            return
                        nc.vector.tensor_scalar(scaled[:].rearrange("p (e q) a -> p e q a", q=QUARTERS), attr,
                                                (GRID - 1) / 2, (GRID - 1) / 2, ALU.mult, ALU.add).then_inc(prep_step, 1)
                        nc.vector.tensor_copy(quad(idx[:, h, :]), r[:, :, :, R_DST])
                        dve.wait_ge(prep_step, b + 1)
                        nc.vector.tensor_tensor(rising[:], scaled[:].rearrange("p k a -> p (k a)").unsqueeze(2).to_broadcast(wide),
                                                centre[:].unsqueeze(1).to_broadcast(wide), ALU.subtract).then_inc(prep_step, 1)
                        if not first:
                            dve.wait_ge(src_ready, groups * (t - 1))
                        nc.vector.tensor_copy(quad(source[:, h, :]), r[:, :, :, R_SRC])
                        dve.wait_ge(prep_step, b + 2)
                        nc.vector.tensor_scalar(falling[:], rising[:], -1.0, 1.0, ALU.mult, ALU.add).then_inc(prep_step, 1)
                        dve.wait_ge(prep_step, b + 3)
                        nc.vector.scalar_tensor_tensor(out=rising[:], in0=rising[:], scalar=1.0, in1=falling[:],
                                                       op0=ALU.add, op1=ALU.min).then_inc(prep_step, 1)
                        dve.wait_ge(prep_step, b + 4)
                        nc.vector.tensor_scalar(tent[:, h, :, :], rising[:], 0.0, None, ALU.max).then_inc(prep_step, 1)
                        dve.wait_ge(prep_step, b + 5)
                        dve.sem_inc(prepared, 1)

                    def tent_of(h, a):
                        return tent[:, h, :, :].rearrange("p (k a) c -> p k a c", a=2)[:, :, a, :]

                    def block_work(i, h, first):
                        t = 2 * i + h
                        dve.wait_ge(gathered[h], 16 * TILES_PER_BLOCK * (i + 1))
                        if layer == 1:
                            if not first:
                                dve.wait_ge(turned, groups * (t - 1))
                            wide = [P, TILES_PER_BLOCK, GRID, FEAT]
                            nc.vector.tensor_tensor(
                                spread[:, h, :, :].rearrange("p k (v f) -> p k v f", f=FEAT),
                                got[:, h, :, :].unsqueeze(2).to_broadcast(wide),
                                tent_of(h, 1).unsqueeze(3).to_broadcast(wide), ALU.mult).then_inc(spread_ready, 1)
                        else:
                            if not first:
                                dve.wait_ge(set_summed, groups * (t - 1))
                            nc.vector.tensor_tensor(
                                weighed[:, h, :, :], got[:, h, :, :],
                                norm[:, h, :].unsqueeze(2).to_broadcast([P, TILES_PER_BLOCK, FEAT]),
                                ALU.mult).then_inc(spread_ready, 1)

                        def compare(g):
                            s, n = g % 2, groups * t + g
                            dve.wait_ge(src_ready, n + 1)
                            if not (first and h == 0 and g < 2):
                                dve.wait_ge(set_summed, n - 1)
                            mine = source[:, h, g * COPY_SET:(g + 1) * COPY_SET]
                            nc.vector.tensor_tensor(same[:, s, :, :], ps_src[s][:].rearrange("p (n e) -> p n e", n=COPY_SET),
                                                    mine.unsqueeze(2).to_broadcast([P, COPY_SET, P]), ALU.is_equal)
                            if not (first and h == 0 and g < 1):
                                dve.wait_ge(same_ready, n)
                            for m in range(COPY_SET):
                                k = g * COPY_SET + m
                                last = nc.vector.scalar_tensor_tensor(
                                    out=earlier[:, m, :], in0=ps_src[s][:, m * P:(m + 1) * P], scalar=source[:, h, k:k + 1],
                                    in1=lower[:], op0=ALU.is_equal, op1=ALU.mult, accum_out=n_earlier[:, k:k + 1])
                            last.then_inc(same_ready, 1)

                        def scale(g):
                            s, n = g % 2, groups * t + g
                            dve.wait_ge(product, n + 1)
                            if not (first and h == 0 and g < 2):
                                dve.wait_ge(set_summed, n - 1)
                            wide = [P, COPY_SET, GRID, FEAT]
                            nc.vector.tensor_tensor(
                                scaled_w[:, s, :, :].rearrange("p n (u f) -> p n u f", f=FEAT),
                                ps_z[s][:].rearrange("p (n u f) -> p n u f", n=COPY_SET, f=FEAT),
                                tent_of(h, 0)[:, g * COPY_SET:(g + 1) * COPY_SET, :].unsqueeze(3).to_broadcast(wide),
                                ALU.mult).then_inc(scaled_ready, 1)

                        for g in range(groups):
                            compare(g)
                            if layer == 1 and g > 0:
                                scale(g - 1)
                        if layer == 1:
                            scale(groups - 1)

                        b = t * TARGET
                        if not first:
                            for s in range(2):
                                dve.wait_ge(added[s], 16 * COPY_SET * (groups // 2) * (t - 1))
                        dve.wait_ge(same_ready, groups * (t + 1))
                        nc.vector.tensor_scalar(to_spare[:], source[:, h, :], -1.0, spare_row[:, 0:1], ALU.mult, ALU.add
                                                ).then_inc(target_step, 1)
                        dve.wait_ge(target_step, b + 1)
                        nc.vector.scalar_tensor_tensor(out=to_spare[:], in0=n_earlier[:], scalar=0.0, in1=to_spare[:],
                                                       op0=ALU.is_gt, op1=ALU.mult).then_inc(target_step, 1)
                        dve.wait_ge(target_step, b + 2)
                        nc.vector.tensor_tensor(target[:, h, :], to_spare[:], source[:, h, :], ALU.add
                                                ).then_inc(target_ready, 1)
                        dve.wait_ge(target_ready, t + 1)
                        dve.sem_inc(target_step, 1)

                    prepare_block(0, 0, True)
                    prepare_block(0, 1, True)
                    for h in range(2):
                        block_work(0, h, True)
                        prepare_block(1, h, False)
                    with dve.Fori(1, BLOCKS // 2 - 1) as i:
                        for h in range(2):
                            block_work(i, h, False)
                            prepare_block(i + 1, h, False)
                    for h in range(2):
                        block_work(BLOCKS // 2 - 1, h, False)

            @block.tensor
            def _(pe):
                with pe.If(pe.value_load(in_order[0:1, 0:1]) == 0):
                    def turn(i, h, g, first):
                        t = 2 * i + h
                        s, n = g % 2, groups * t + g
                        fresh = first and h == 0 and g < 2
                        pe.wait_ge(prepared, t + 1)
                        if not fresh:
                            pe.wait_ge(same_ready, n - 1)
                        for m in range(COPY_SET):
                            k = g * COPY_SET + m
                            mm = nc.tensor.matmul(ps_src[s][:, m * P:(m + 1) * P],
                                                  source[:, h, k:k + 1].to_broadcast([P, P]), ident[:],
                                                  start=True, stop=True)
                        mm.then_inc(src_ready, 1)
                        if layer == 2:
                            return
                        pe.wait_ge(spread_ready, t + 1)
                        if not fresh:
                            pe.wait_ge(turned_copied, n - 1)
                        for m in range(COPY_SET):
                            mm = nc.tensor.transpose(ps_t[s][:, m * P:(m + 1) * P],
                                                     spread[:, h, g * COPY_SET + m, :], ident[:])
                        mm.then_inc(turned, 1)

                    def multiply(i, h, g, first):
                        t = 2 * i + h
                        s, n = g % 2, groups * t + g
                        pe.wait_ge(turned_copied, n + 1)
                        if not (first and h == 0 and g < 2):
                            pe.wait_ge(scaled_ready, n - 1)
                        for m in range(COPY_SET):
                            mm = nc.tensor.matmul(ps_z[s][:, m * P:(m + 1) * P], spread_t[:, s, m, :], w1_sb[:],
                                                  start=True, stop=True)
                        mm.then_inc(product, 1)

                    def add_up(i, h, g, first):
                        t = 2 * i + h
                        s, n = g % 2, groups * t + g
                        if layer == 1:
                            pe.wait_ge(scaled_ready, n + 1)
                        else:
                            pe.wait_ge(spread_ready, t + 1)
                        pe.wait_ge(same_ready, n + 1)
                        if not first and g == 0:
                            pe.wait_ge(summed_ready, t - 1)
                        for m in range(COPY_SET):
                            k = g * COPY_SET + m
                            if layer == 2:
                                mm = nc.tensor.matmul(ps_sum[h][:, k * FEAT:(k + 1) * FEAT], same[:, s, m, :],
                                                      weighed[:, h, k, :], start=True, stop=True)
                                continue
                            for u in range(GRID):
                                mm = nc.tensor.matmul(ps_sum[h][:, k * FEAT:(k + 1) * FEAT], same[:, s, m, :],
                                                      scaled_w[:, s, m, u * FEAT:(u + 1) * FEAT],
                                                      start=(u == 0), stop=(u == GRID - 1))
                        mm.then_inc(set_summed, 1)

                    def block_work(i, h, first):
                        for g in range(groups + 2):
                            if g < groups:
                                turn(i, h, g, first)
                            if layer == 1 and 1 <= g <= groups:
                                multiply(i, h, g - 1, first)
                            if g >= 2:
                                add_up(i, h, g - 2, first)

                    block_work(0, 0, True)
                    block_work(0, 1, True)
                    with pe.Fori(1, BLOCKS // 2) as i:
                        for h in range(2):
                            block_work(i, h, False)

            @block.scalar
            def _(act):
                with act.If(act.value_load(in_order[0:1, 0:1]) == 0):
                    def copies(i, h, first):
                        t = 2 * i + h
                        for g in range(groups if layer == 1 else 0):
                            s, n = g % 2, groups * t + g
                            act.wait_ge(turned, n + 1)
                            if not (first and h == 0 and g < 2):
                                act.wait_ge(product, n - 1)
                            nc.scalar.copy(spread_t[:, s, :, :].rearrange("p n e -> p (n e)"), ps_t[s][:]
                                           ).then_inc(turned_copied, 1)
                        act.wait_ge(set_summed, groups * (t + 1))
                        if not first:
                            for s in range(2):
                                act.wait_ge(added[s], 16 * COPY_SET * (groups // 2) * (t - 1))
                        nc.scalar.copy(summed[:, h, :, :].rearrange("p k f -> p (k f)"), ps_sum[h][:]
                                       ).then_inc(summed_ready, 1)

                    copies(0, 0, True)
                    copies(0, 1, True)
                    with act.Fori(1, BLOCKS // 2) as i:
                        for h in range(2):
                            copies(i, h, False)


def update_nodes(nc, accs, table2, x_sb, ident_b, w2_sb, eps_sb):
    with ExitStack() as ctx:
        def sb(name, shape, dt=F32):
            return ctx.enter_context(nc.sbuf_tensor(f"{name}_u", shape, dt))

        def ps(name):
            return ctx.enter_context(nc.psum_tensor(f"{name}_u", [P, 512], F32))

        def sem(name):
            return ctx.enter_context(nc.semaphore(f"{name}_u"))

        parts = sb("parts", [P, 2, COPIES, GCOLS])
        total = sb("total", [P, GCOLS])
        ln = ln_buffers(sb)
        w_split = sb("w_split", [P, 3, W_COLS], BF16)
        w_rest = sb("w_rest", [P, 2, W_COLS])
        w_pieces = sb("w_pieces", [P, 2, W_COLS], BF16)
        pieces = sb("pieces", [P, 2, GROUP, 2, P], BF16)
        rest = sb("rest", [P, 2, GROUP, FEAT])
        ht = sb("ht", [P, 2, T_BANKS, 4 * P], BF16)
        rows_sb = sb("rows_sb", [P, GROUP, TAB2_NODE])
        ps_t = [ps(f"ps_t{i}") for i in range(T_BANKS)]
        ps_w = [ps(f"ps_w{i}") for i in range(W_BANKS)]
        parts_in = [sem(f"parts_in{h}") for h in range(2)]
        totalled, x_ready = sem("totalled"), sem("x_ready")
        w_step, split_step, split_ready = sem("w_step"), sem("split_step"), sem("split_ready")
        ln_step, var_ready, std_ready, h_ready = sem("ln_step"), sem("var_ready"), sem("std_ready"), sem("h_ready")
        turned, ht_ready, product, evacuated = sem("turned"), sem("ht_ready"), sem("product"), sem("evacuated")
        stored = [sem(f"stored{k}") for k in range(GROUP)]

        with nc.Block() as block:

            @block.sync
            def _(sp):
                def load(i, h, first):
                    j = 2 * i + h
                    if not first:
                        sp.wait_ge(totalled, j - 1)
                    for n, acc in enumerate(accs):
                        sp.dma_start(parts[:, h, n, :].rearrange("p (t f) -> p t f", f=FEAT),
                                     bass.AP(acc, j * (GROUP * P * FEAT), [[FEAT, P], [P * FEAT, GROUP], [1, FEAT]])
                                     ).then_inc(parts_in[h], 16)

                def store(j):
                    for k in range(GROUP):
                        n = j * GROUP + k
                        sp.wait_ge(evacuated, n + 1)
                        sp.dma_start(bass.AP(table2, n * P * TAB2_NODE, [[TAB2_NODE, P], [1, TAB2_NODE]]),
                                     rows_sb[:, k, :]).then_inc(stored[k], 16)

                load(0, 0, True)
                load(0, 1, True)
                with sp.Fori(1, GROUPS // 2) as i:
                    for h in range(2):
                        load(i, h, False)
                        store(2 * i + h - 2)
                for h in range(2):
                    store(GROUPS - 2 + h)
                for k in range(GROUP):
                    sp.wait_ge(stored[k], 16 * GROUPS)

            @block.vector
            def _(dve):
                def update(i, h, first):
                    j = 2 * i + h
                    xg = x_sb[:, bass.ds(j * GCOLS, GCOLS)]
                    dve.wait_ge(parts_in[h], 16 * COPIES * (i + 1))
                    nc.vector.tensor_reduce(total[:], parts[:, h, :, :].rearrange("p n c -> p c n"), AX, ALU.add
                                            ).then_inc(totalled, 1)
                    dve.wait_ge(totalled, j + 1)
                    nc.vector.tensor_tensor(xg, xg, total[:], ALU.add).then_inc(x_ready, 1)
                    dve.wait_ge(x_ready, j + 1)
                    if not first:
                        dve.wait_ge(turned, j - 1)
                    ln_group(nc, dve, ln, xg, j, h, ln_step, var_ready, std_ready, h_ready)

                    b = 4 * j
                    whole = ln["h"][:, h, :].rearrange("p (t f) -> p t f", f=FEAT)
                    side = [pieces[:, h, :, a, :] for a in range(2)]
                    high, middle, low = side[0][:, :, 0:FEAT], side[0][:, :, FEAT:2 * FEAT], side[1][:, :, 0:FEAT]
                    nc.vector.tensor_copy(high, whole).then_inc(split_step, 1)
                    dve.wait_ge(split_step, b + 1)
                    nc.vector.tensor_tensor(rest[:, 0, :, :], whole, high, ALU.subtract).then_inc(split_step, 1)
                    dve.wait_ge(split_step, b + 2)
                    nc.vector.tensor_copy(middle, rest[:, 0, :, :]).then_inc(split_step, 1)
                    dve.wait_ge(split_step, b + 3)
                    nc.vector.tensor_tensor(rest[:, 1, :, :], rest[:, 0, :, :], middle, ALU.subtract).then_inc(split_step, 1)
                    dve.wait_ge(split_step, b + 4)
                    nc.vector.tensor_copy(low, rest[:, 1, :, :])
                    nc.vector.tensor_copy(side[1][:, :, 3 * FEAT:], rest[:, 1, :, :])
                    for copy in (side[0][:, :, 2 * FEAT:], side[1][:, :, FEAT:3 * FEAT]):
                        last = nc.vector.tensor_copy(copy, side[0][:, :, 0:2 * FEAT])
                    last.then_inc(split_ready, 1)

                high, middle, low = (w_split[:, n, :] for n in range(3))
                nc.vector.tensor_copy(high, w2_sb[:]).then_inc(w_step, 1)
                dve.wait_ge(w_step, 1)
                nc.vector.tensor_tensor(w_rest[:, 0, :], w2_sb[:], high, ALU.subtract).then_inc(w_step, 1)
                dve.wait_ge(w_step, 2)
                nc.vector.tensor_copy(middle, w_rest[:, 0, :]).then_inc(w_step, 1)
                dve.wait_ge(w_step, 3)
                nc.vector.tensor_tensor(w_rest[:, 1, :], w_rest[:, 0, :], middle, ALU.subtract).then_inc(w_step, 1)
                dve.wait_ge(w_step, 4)
                nc.vector.tensor_copy(low, w_rest[:, 1, :]).then_inc(w_step, 1)
                dve.wait_ge(w_step, 5)
                for a, order in enumerate(((0, 0, 1, 1), (0, 2, 2, 1))):
                    for n, piece in enumerate(order):
                        rows = slice(n * FEAT, (n + 1) * FEAT)
                        last = nc.vector.tensor_copy(w_pieces[rows, a, :], w_split[rows, piece, :])
                last.then_inc(w_step, 1)

                update(0, 0, True)
                update(0, 1, True)
                with dve.Fori(1, GROUPS // 2) as i:
                    for h in range(2):
                        update(i, h, False)

            @block.tensor
            def _(pe):
                def group(j, h, first):
                    turn_and_multiply(nc, pe, pieces, ps_t, ps_w, ht, w_pieces, ident_b, j, h, first,
                                      split_ready, turned, ht_ready, product, evacuated)

                pe.wait_ge(w_step, 6)
                group_first(group)
                with pe.Fori(1, GROUPS // 2) as i:
                    for h in range(2):
                        group(2 * i + h, h, False)

            @block.scalar
            def _(act):
                def group(j, h, first, more=True):
                    table_rows(nc, act, ln, ps_t, ps_w, ht, rows_sb, eps_sb, j, h, first, more,
                               var_ready, std_ready, turned, ht_ready, product, evacuated, stored)

                root(nc, act, ln, eps_sb, 0, 0, var_ready, std_ready)
                group_first(group)
                with act.Fori(1, GROUPS // 2 - 1) as i:
                    for h in range(2):
                        group(2 * i + h, h, False)
                group(GROUPS - 2, 0, False)
                group(GROUPS - 1, 1, False, more=False)


def ordered_finish(nc, in_order, records, sums, x_sb, last_edge, local_id, group_base, carry_id,
                   out):
    with ExitStack() as ctx:
        def sb(name, shape, dt=F32):
            return ctx.enter_context(nc.sbuf_tensor(f"{name}_n", shape, dt))

        def ps(name):
            return ctx.enter_context(nc.psum_tensor(f"{name}_n", [P, 512], F32))

        def sem(name):
            return ctx.enter_context(nc.semaphore(f"{name}_n"))

        K = QUARTERS - 1
        ends_dst = sb("ends_dst", [K, 2, REC], I32)
        ends_sum = sb("ends_sum", [K, FEAT])
        same = sb("same", [K, 1])
        cut_id = sb("cut_id", [K, 1])
        idx = sb("idx", [P, 2, GROUP], I32)
        picked = sb("picked", [P, 2, GROUP, FEAT])
        owner = sb("owner", [K, 2, GROUP * P])
        new_x = sb("new_x", [P, 2, GCOLS])
        ps_carry = [ps(f"ps_carry{h}") for h in range(2)]

        ends_in, ends_step = sem("ends_in"), sem("ends_step")
        idx_ready, owner_ready, carry_ready = sem("idx_ready"), sem("owner_ready"), sem("carry_ready")
        picked_in = [sem(f"picked_in{h}") for h in range(2)]
        carried, x_ready = sem("carried"), sem("x_ready")
        pool_waited = sem("pool_waited")
        out_stored = [sem(f"out_stored{h}") for h in range(2)]

        with nc.Block() as block:

            @block.sync
            def _(sp):
                with sp.If(sp.value_load(in_order[0:1, 0:1]) > 0):
                    sp.dma_start(ends_dst[:].rearrange("k a r -> k (a r)"),
                                 bass.AP(records, QEDGES * REC, [[QEDGES * REC, K], [1, 2 * REC]])).then_inc(ends_in, 16)
                    sp.dma_start(ends_sum[:], bass.AP(sums, QUARTERS * (QEDGES - 1) * FEAT, [[FEAT, K], [1, FEAT]])
                                 ).then_inc(ends_in, 16)
                    def store(i, h, tiles):
                        j = 2 * i + h
                        sp.wait_ge(x_ready, j + 1)
                        sp.dma_start(
                            bass.AP(out.tensor, j * (GROUP * P * FEAT), [[FEAT, P], [P * FEAT, tiles], [1, FEAT]]),
                            new_x[:, h, 0:tiles * FEAT].rearrange("p (t f) -> p t f", f=FEAT)
                        ).then_inc(out_stored[h], 16)

                    with sp.Fori(0, GROUPS // 2 - 1) as i:
                        for h in range(2):
                            store(i, h, GROUP)
                    store(GROUPS // 2 - 1, 0, GROUP)
                    store(GROUPS // 2 - 1, 1, GROUP - 1)
                    sp.dma_start(out[(TILES - 1) * P:NODES, :],
                                 new_x[0:LAST_ROWS, 1, (GROUP - 1) * FEAT:]).then_inc(out_stored[1], 16)
                    sp.wait_ge(out_stored[0], 16 * (GROUPS // 2))
                    sp.wait_ge(out_stored[1], 16 * (GROUPS // 2) + 16)

            @block.gpsimd
            def _(pool):
                with pool.If(pool.value_load(in_order[0:1, 0:1]) > 0):
                    def fetch(i, h, first):
                        j = 2 * i + h
                        pool.wait_ge(idx_ready, j + 1)
                        if not first:
                            pool.wait_ge(x_ready, j - 1)
                        pool.sem_inc(pool_waited, 1)
                        for k in range(GROUP):
                            pool.indirect_dma_start(
                                out=picked[:, h, k, :], out_offset=None, in_=sums.ap(),
                                in_offset=bass.IndirectOffsetOnAxis(ap=idx[:, h, k:k + 1], axis=0)
                            ).then_inc(picked_in[h], 16)

                    fetch(0, 0, True)
                    fetch(0, 1, True)
                    with pool.Fori(1, GROUPS // 2) as i:
                        for h in range(2):
                            fetch(i, h, False)

            @block.vector
            def _(dve):
                with dve.If(dve.value_load(in_order[0:1, 0:1]) > 0):
                    def indices(i, h):
                        nc.vector.tensor_copy(idx[:, h, :], last_edge[:, bass.ds((2 * i + h) * GROUP, GROUP)]
                                              ).then_inc(idx_ready, 1)

                    def owners(i, h, first):
                        j = 2 * i + h
                        if not first:
                            dve.wait_ge(carry_ready, j - 1)
                        nc.vector.tensor_scalar(owner[:, h, :], local_id[:], carry_id[:, bass.ds(j, 1)], None,
                                                ALU.is_equal).then_inc(owner_ready, 1)

                    def add(i, h, first):
                        j = 2 * i + h
                        xg = x_sb[:, bass.ds(j * GCOLS, GCOLS)]
                        dve.wait_ge(carry_ready, j + 1)
                        if not first:
                            dve.wait_ge(out_stored[h], 16 * i)
                        nc.vector.tensor_tensor(new_x[:, h, :], xg, ps_carry[h][:, 0:GCOLS], ALU.add).then_inc(carried, 1)
                        dve.wait_ge(carried, j + 1)
                        dve.wait_ge(picked_in[h], 16 * GROUP * (i + 1))
                        nc.vector.tensor_tensor(new_x[:, h, :], new_x[:, h, :],
                                                picked[:, h, :, :].rearrange("p t f -> p (t f)"),
                                                ALU.add).then_inc(x_ready, 1)

                    indices(0, 0)
                    indices(0, 1)
                    dve.wait_ge(ends_in, 32)
                    nc.vector.tensor_tensor(same[:], ends_dst[:, 0, R_DST:R_DST + 1], ends_dst[:, 1, R_DST:R_DST + 1],
                                            ALU.is_equal).then_inc(ends_step, 1)
                    dve.wait_ge(ends_step, 1)
                    nc.vector.scalar_tensor_tensor(out=cut_id[:], in0=ends_dst[:, 0, R_DST:R_DST + 1], scalar=1.0,
                                                   in1=same[:], op0=ALU.add, op1=ALU.mult).then_inc(ends_step, 1)
                    dve.wait_ge(ends_step, 2)
                    nc.vector.tensor_scalar(cut_id[:], cut_id[:], -1.0, None, ALU.add).then_inc(ends_step, 1)
                    dve.wait_ge(ends_step, 3)
                    nc.vector.tensor_scalar(carry_id[:], group_base[:], cut_id[:, 0:1], None, ALU.add
                                            ).then_inc(ends_step, 1)
                    dve.wait_ge(ends_step, 4)
                    owners(0, 0, True)
                    owners(0, 1, True)
                    for h in range(2):
                        add(0, h, True)
                        indices(1, h)
                        owners(1, h, False)
                    with dve.Fori(1, GROUPS // 2 - 1) as i:
                        for h in range(2):
                            add(i, h, False)
                            indices(i + 1, h)
                            owners(i + 1, h, False)
                    for h in range(2):
                        add(GROUPS // 2 - 1, h, False)

            @block.tensor
            def _(pe):
                with pe.If(pe.value_load(in_order[0:1, 0:1]) > 0):
                    pe.wait_ge(ends_in, 32)

                    def carry(j, h, first):
                        pe.wait_ge(owner_ready, j + 1)
                        if not first:
                            pe.wait_ge(carried, j - 1)
                        for k in range(GROUP):
                            mm = nc.tensor.matmul(ps_carry[h][:, k * FEAT:(k + 1) * FEAT],
                                                  owner[:, h, k * P:(k + 1) * P], ends_sum[:], start=True, stop=True)
                        mm.then_inc(carry_ready, 1)

                    carry(0, 0, True)
                    carry(1, 1, True)
                    with pe.Fori(1, GROUPS // 2) as i:
                        for h in range(2):
                            carry(2 * i + h, h, False)


def any_order_finish(nc, in_order, accs, x, x_sb, out):
    with ExitStack() as ctx:
        def sb(name, shape, dt=F32):
            return ctx.enter_context(nc.sbuf_tensor(f"{name}_f", shape, dt))

        def sem(name):
            return ctx.enter_context(nc.semaphore(f"{name}_f"))

        parts = sb("parts", [P, 2, COPIES, GCOLS])
        total = sb("total", [P, GCOLS])
        x_in, totalled, x_ready, stored = sem("x_in"), sem("totalled"), sem("x_ready"), sem("stored")
        x_seen = sem("x_seen")
        parts_in = [sem(f"parts_in{h}") for h in range(2)]
        whole = (TILES - 1) * P

        with nc.Block() as block:

            @block.sync
            def _(sp):
                with sp.If(sp.value_load(in_order[0:1, 0:1]) == 0):
                    sp.dma_start(x_sb[:, 0:(TILES - 1) * FEAT].rearrange("p (t f) -> p t f", f=FEAT),
                                 x[0:whole, :].rearrange("(t p) f -> p t f", p=P)).then_inc(x_in, 16)
                    sp.dma_start(x_sb[0:LAST_ROWS, (TILES - 1) * FEAT:], x[whole:NODES, :]).then_inc(x_in, 16)

                    def load(i, h, first):
                        j = 2 * i + h
                        if not first:
                            sp.wait_ge(totalled, j - 1)
                        for n, acc in enumerate(accs):
                            sp.dma_start(parts[:, h, n, :].rearrange("p (t f) -> p t f", f=FEAT),
                                         bass.AP(acc, j * (GROUP * P * FEAT), [[FEAT, P], [P * FEAT, GROUP], [1, FEAT]])
                                         ).then_inc(parts_in[h], 16)

                    load(0, 0, True)
                    load(0, 1, True)
                    with sp.Fori(1, GROUPS // 2) as i:
                        for h in range(2):
                            load(i, h, False)
                    sp.wait_ge(x_ready, GROUPS)
                    sp.dma_start(out[0:whole, :].rearrange("(t p) f -> p t f", p=P),
                                 x_sb[:, 0:(TILES - 1) * FEAT].rearrange("p (t f) -> p t f", f=FEAT)).then_inc(stored, 16)
                    sp.dma_start(out[whole:NODES, :], x_sb[0:LAST_ROWS, (TILES - 1) * FEAT:]).then_inc(stored, 16)
                    sp.wait_ge(stored, 32)

            @block.vector
            def _(dve):
                with dve.If(dve.value_load(in_order[0:1, 0:1]) == 0):
                    def update(i, h):
                        j = 2 * i + h
                        xg = x_sb[:, bass.ds(j * GCOLS, GCOLS)]
                        dve.wait_ge(parts_in[h], 16 * COPIES * (i + 1))
                        nc.vector.tensor_reduce(total[:], parts[:, h, :, :].rearrange("p n c -> p c n"), AX, ALU.add
                                                ).then_inc(totalled, 1)
                        dve.wait_ge(totalled, j + 1)
                        nc.vector.tensor_tensor(xg, xg, total[:], ALU.add).then_inc(x_ready, 1)
                        dve.wait_ge(x_ready, j + 1)
                        dve.sem_inc(x_seen, 1)

                    dve.wait_ge(x_in, 32)
                    with dve.Fori(0, GROUPS // 2) as i:
                        for h in range(2):
                            update(i, h)


_INS = ["x", "src", "dst", "edge_attr_2", "edge_type_16", "edge_weight1", "L0_gnn_weight", "L1_gnn_weight",
        "L1_gnn_w_comp"]


def kernel(**inputs):
    import concourse.bacc as _bacc
    from concourse.bass_utils import run_bass_kernel_spmd as _run

    nc = _bacc.Bacc("TRN2", target_bir_lowering=False, num_devices=1)
    arrays, args = {}, []
    for name in _INS:
        a = np.ascontiguousarray(inputs[name])
        arrays[f"in_{name}"] = a
        args.append(nc.dram_tensor(f"in_{name}", a.shape, mybir.dt.from_np(a.dtype), kind="ExternalInput").ap())
    out = nc.dram_tensor("out", (NODES, FEAT), F32, kind="ExternalOutput").ap()
    gnn_kernel(nc, *args, out)
    r = _run(nc, [arrays], core_ids=[0])
    return r.results[0]["out"]
```
